# Optimizing a Trainium2 kernel written in Bass

```python
import numpy as np
import jax
import jax.numpy as jnp

def _softmax(x, axis=-1):
    return jax.nn.softmax(x, axis=axis)

def _gelu(x):
    return jax.nn.gelu(x, approximate=True)

def _silu(x):
    return jax.nn.silu(x)

def _sigmoid(x):
    return jax.nn.sigmoid(x)

def _layernorm(x, axis=-1, eps=1e-05):
    m = jnp.mean(x, axis=axis, keepdims=True)
    v = jnp.var(x, axis=axis, keepdims=True)
    return (x - m) / jnp.sqrt(v + eps)

def _scatter_add(tgt, idx, src, axis=0):
    return tgt.at[idx].add(src)

def _segment_sum(src, seg, n):
    return jax.ops.segment_sum(src, seg, n)
kernel_name = 'mk_flamingo_gated_d2_seqx_r8_758f5d'

def setup_inputs(seed: int=0):
    np.random.seed(seed)
    _w = jnp.asarray

    def _rec_inputs():
        import jax
        import jax.numpy as jnp
        _rk = jax.random.key(seed)
        x = -0.0003929 + 0.9999 * jax.random.normal(jax.random.fold_in(_rk, 1), (8, 128, 256), jnp.float32)
        _lenS = 128 - jax.random.randint(jax.random.fold_in(_rk, 7), (8,), 0, max(1, 128 // 4) + 1, jnp.int32)
        _lenS2 = 128 - jax.random.randint(jax.random.fold_in(_rk, 8), (8,), 0, max(1, 128 // 4) + 1, jnp.int32)
        _ctx_2048P = jax.random.normal(jax.random.fold_in(_rk, 11), (8, 16, 256), jnp.float32)
        _ctx_2048c = jax.random.dirichlet(jax.random.fold_in(_rk, 511), 0.3 * jnp.ones((16,), jnp.float32), (8, 128))
        _ctx_2048t = jnp.einsum('bsk,bkd->bsd', _ctx_2048c, _ctx_2048P)
        _ctx_2048t = _ctx_2048t * jax.lax.rsqrt(jnp.mean(jnp.square(_ctx_2048t)) + 1e-12) * 0.953939
        ctx_2048 = -0.000514642 + 1.00011 * (_ctx_2048t + 0.3 * jax.random.normal(jax.random.fold_in(_rk, 611), (8, 128, 256), jnp.float32))
        _g = jax.random.normal(jax.random.fold_in(_rk, 9001), (2, 2), jnp.float32)
        _g = jnp.sign(_g) * jnp.maximum(jnp.abs(_g), 1.0) + (_g == 0) * 1.0
        g_xattn = _g[0]
        g_ffn = _g[1]
        return (x, ctx_2048, g_xattn, g_ffn)
    x, ctx_2048, g_xattn, g_ffn = _rec_inputs()

    def _L0_xattn_setup():
        import jax, jax.numpy as jnp
        import numpy as np
        DIM = 256
        NHEADS = 32
        HEAD_DIM = DIM // NHEADS
        EPS = 1e-06

        def _rmsnorm(t):
            return t * jax.lax.rsqrt(jnp.mean(t * t, axis=-1, keepdims=True) + EPS)
        key = jax.random.key(seed)
        kx, kc, kq, kk, kv = jax.random.split(key, 5)
        x = jax.random.normal(kx, (2, 512, DIM), dtype=jnp.float32)
        context = jax.random.normal(kc, (2, 64, DIM), dtype=jnp.float32)
        std = 0.02
        Wq = jax.random.normal(kq, (DIM, DIM), dtype=jnp.float32) * std
        Wk = jax.random.normal(kk, (DIM, DIM), dtype=jnp.float32) * std
        Wv = jax.random.normal(kv, (DIM, DIM), dtype=jnp.float32) * std
        return {'x': x, 'context': context, 'Wq': Wq, 'Wk': Wk, 'Wv': Wv}
    _L0_xattn_all = _L0_xattn_setup()
    _L0_xattn_in = {k: v for k, v in _L0_xattn_all.items() if k in ('Wq', 'Wk', 'Wv')}
    del _L0_xattn_all

    def _L0_ffn_setup():
        import jax, jax.numpy as jnp
        import numpy as np
        TOP_K = 2
        key = jax.random.key(seed)
        ks = jax.random.split(key, 7)
        B, S, H = (2, 256, 256)
        E, A, NS = (8, 64, 2048)
        x = jax.random.normal(ks[0], (B, S, H), jnp.float32)
        gate_w = jax.random.normal(ks[1], (E, H), jnp.float32) * 0.01
        W = jax.random.normal(ks[2], (H, H), jnp.float32) * 0.02
        atoms = jax.random.normal(ks[3], (A, NS), jnp.float32) * 0.02
        expert_atom_weights = jax.random.normal(ks[4], (E, A), jnp.float32) * 0.1
        importance = jax.random.normal(ks[5], (E, NS), jnp.float32) * 0.1
        mask_idx = jax.random.randint(ks[6], (NS,), 0, H * H, jnp.int32)
        return dict(x=x, gate_w=gate_w, W=W, atoms=atoms, expert_atom_weights=expert_atom_weights, importance=importance, mask_idx=mask_idx)
    _L0_ffn_all = _L0_ffn_setup()
    _L0_ffn_in = {k: v for k, v in _L0_ffn_all.items() if k in ('gate_w', 'W', 'atoms', 'expert_atom_weights', 'importance', 'mask_idx')}
    del _L0_ffn_all

    def _L1_xattn_setup():
        import jax, jax.numpy as jnp
        import numpy as np
        DIM = 256
        N_HEADS = 16
        HEAD_DIM = DIM // N_HEADS
        EPS = 1e-06
        IMG_LEN = 257

        def rms_norm(x, g, eps=EPS):
            var = jnp.mean(x * x, axis=-1, keepdims=True)
            return x * jax.lax.rsqrt(var + eps) * g

        def _attend(q, k, v, k_mask=None):
            scale = 1.0 / jnp.sqrt(jnp.asarray(HEAD_DIM, q.dtype))
            scores = jnp.einsum('bqnd,bknd->bnqk', q, k) * scale
            if k_mask is not None:
                neg = jnp.asarray(jnp.finfo(scores.dtype).min, scores.dtype)
                scores = jnp.where(k_mask[:, None, None, :], scores, neg)
            probs = jax.nn.softmax(scores, axis=-1)
            return jnp.einsum('bnqk,bknd->bqnd', probs, v)
        key = jax.random.key(seed)
        ks = jax.random.split(key, 16)
        B, L1, L2 = (1, 2048, 769)
        std = 0.02
        inp = {'x': jax.random.normal(ks[0], (B, L1, DIM), jnp.float32), 'context': jax.random.normal(ks[1], (B, L2, DIM), jnp.float32), 'context_lens': jax.random.randint(ks[2], (B,), 32, 513, jnp.int32), 'Wq': jax.random.normal(ks[3], (DIM, DIM), jnp.float32) * std, 'bq': jnp.zeros((DIM,), jnp.float32), 'gq': jnp.ones((DIM,), jnp.float32), 'Wk': jax.random.normal(ks[4], (DIM, DIM), jnp.float32) * std, 'bk': jnp.zeros((DIM,), jnp.float32), 'gk': jnp.ones((DIM,), jnp.float32), 'Wv': jax.random.normal(ks[5], (DIM, DIM), jnp.float32) * std, 'bv': jnp.zeros((DIM,), jnp.float32), 'Wk_img': jax.random.normal(ks[6], (DIM, DIM), jnp.float32) * std, 'bk_img': jnp.zeros((DIM,), jnp.float32), 'gk_img': jnp.ones((DIM,), jnp.float32), 'Wv_img': jax.random.normal(ks[7], (DIM, DIM), jnp.float32) * std, 'bv_img': jnp.zeros((DIM,), jnp.float32), 'Wo': jax.random.normal(ks[8], (DIM, DIM), jnp.float32) * std, 'bo': jnp.zeros((DIM,), jnp.float32)}
        return inp
    _L1_xattn_all = _L1_xattn_setup()
    _L1_xattn_in = {k: v for k, v in _L1_xattn_all.items() if k in ('context_lens', 'Wq', 'bq', 'gq', 'Wk', 'bk', 'gk', 'Wv', 'bv', 'Wk_img', 'bk_img', 'gk_img', 'Wv_img', 'bv_img', 'Wo', 'bo')}
    del _L1_xattn_all

    def _L1_ffn_setup():
        import jax, jax.numpy as jnp
        import numpy as np
        EPS = 1e-05

        def _quant_weight(w):
            scale = jnp.clip(jnp.mean(jnp.abs(w)), EPS, None)
            wq = jnp.clip(jnp.round(w / scale), -1.0, 1.0) * scale
            return w + jax.lax.stop_gradient(wq - w)

        def _quant_act(x):
            scale = 127.0 / jnp.clip(jnp.max(jnp.abs(x), axis=-1, keepdims=True), EPS, None)
            xq = jnp.clip(jnp.round(x * scale), -128.0, 127.0) / scale
            return x + jax.lax.stop_gradient(xq - x)

        def bitlinear(x, w):
            return jnp.einsum('btc,oc->bto', _quant_act(x), _quant_weight(w))
        key = jax.random.key(seed)
        k1, k2, k3 = jax.random.split(key, 3)
        B, T, C, F = (2, 512, 256, 1024)
        x = jax.random.normal(k1, (B, T, C), dtype=jnp.float32)
        w_gate_up = jax.random.normal(k2, (2 * F, C), dtype=jnp.float32) * 0.02
        w_down = jax.random.normal(k3, (C, F), dtype=jnp.float32) * 0.02
        return {'x': x, 'w_gate_up': w_gate_up, 'w_down': w_down}
    _L1_ffn_all = _L1_ffn_setup()
    _L1_ffn_in = {k: v for k, v in _L1_ffn_all.items() if k in ('w_gate_up', 'w_down')}
    del _L1_ffn_all
    return {'x': x, 'ctx_2048': ctx_2048, 'g_xattn': g_xattn, 'g_ffn': g_ffn, 'L0_xattn_Wq': _L0_xattn_in['Wq'], 'L0_xattn_Wk': _L0_xattn_in['Wk'], 'L0_xattn_Wv': _L0_xattn_in['Wv'], 'L0_ffn_gate_w': _L0_ffn_in['gate_w'], 'L0_ffn_W': _L0_ffn_in['W'], 'L0_ffn_atoms': _L0_ffn_in['atoms'], 'L0_ffn_expert_atom_weights': _L0_ffn_in['expert_atom_weights'], 'L0_ffn_importance': _L0_ffn_in['importance'], 'L0_ffn_mask_idx': _L0_ffn_in['mask_idx'], 'L1_xattn_context_lens': _L1_xattn_in['context_lens'], 'L1_xattn_Wq': _L1_xattn_in['Wq'], 'L1_xattn_bq': _L1_xattn_in['bq'], 'L1_xattn_gq': _L1_xattn_in['gq'], 'L1_xattn_Wk': _L1_xattn_in['Wk'], 'L1_xattn_bk': _L1_xattn_in['bk'], 'L1_xattn_gk': _L1_xattn_in['gk'], 'L1_xattn_Wv': _L1_xattn_in['Wv'], 'L1_xattn_bv': _L1_xattn_in['bv'], 'L1_xattn_Wk_img': _L1_xattn_in['Wk_img'], 'L1_xattn_bk_img': _L1_xattn_in['bk_img'], 'L1_xattn_gk_img': _L1_xattn_in['gk_img'], 'L1_xattn_Wv_img': _L1_xattn_in['Wv_img'], 'L1_xattn_bv_img': _L1_xattn_in['bv_img'], 'L1_xattn_Wo': _L1_xattn_in['Wo'], 'L1_xattn_bo': _L1_xattn_in['bo'], 'L1_ffn_w_gate_up': _L1_ffn_in['w_gate_up'], 'L1_ffn_w_down': _L1_ffn_in['w_down']}

def reference(x, ctx_2048, g_xattn, g_ffn, L0_xattn_Wq, L0_xattn_Wk, L0_xattn_Wv, L0_ffn_gate_w, L0_ffn_W, L0_ffn_atoms, L0_ffn_expert_atom_weights, L0_ffn_importance, L0_ffn_mask_idx, L1_xattn_context_lens, L1_xattn_Wq, L1_xattn_bq, L1_xattn_gq, L1_xattn_Wk, L1_xattn_bk, L1_xattn_gk, L1_xattn_Wv, L1_xattn_bv, L1_xattn_Wk_img, L1_xattn_bk_img, L1_xattn_gk_img, L1_xattn_Wv_img, L1_xattn_bv_img, L1_xattn_Wo, L1_xattn_bo, L1_ffn_w_gate_up, L1_ffn_w_down):
    import jax
    import jax.numpy as jnp

    def _L0_xattn_ref(x, context, Wq, Wk, Wv):
        import jax, jax.numpy as jnp
        import numpy as np
        DIM = 256
        NHEADS = 32
        HEAD_DIM = DIM // NHEADS
        EPS = 1e-06

        def _rmsnorm(t):
            return t * jax.lax.rsqrt(jnp.mean(t * t, axis=-1, keepdims=True) + EPS)
        b, n, _ = x.shape
        m = context.shape[1]
        q = x @ Wq.T
        k_raw = context @ Wk.T
        v_raw = context @ Wv.T
        q = q.reshape(b, n, NHEADS, HEAD_DIM).transpose(0, 2, 1, 3)
        kv = jnp.concatenate([k_raw, v_raw], axis=-1)
        kv = kv.reshape(b, m, NHEADS, HEAD_DIM, 2)
        k = kv[..., 0].transpose(0, 2, 1, 3)
        v = kv[..., 1].transpose(0, 2, 1, 3)
        q = _rmsnorm(q)
        k = _rmsnorm(k)
        scale = HEAD_DIM ** (-0.5)
        scores = jnp.einsum('bhnd,bhmd->bhnm', q, k) * scale
        attn = jax.nn.softmax(scores, axis=-1)
        out = jnp.einsum('bhnm,bhmd->bhnd', attn, v)
        return out.transpose(0, 2, 1, 3).reshape(b, n, NHEADS * HEAD_DIM)

    def _L0_ffn_ref(x, gate_w, W, atoms, expert_atom_weights, importance, mask_idx):
        import jax, jax.numpy as jnp
        import numpy as np
        TOP_K = 2
        B, S, H = x.shape
        xt = x.reshape(-1, H)
        logits = jnp.clip(xt @ gate_w.T, -50.0, 50.0)
        top_w, top_idx = jax.lax.top_k(logits, TOP_K)
        rw = jax.nn.softmax(top_w, axis=-1)
        deltas = jax.nn.softmax(expert_atom_weights, axis=-1) @ atoms
        weighted = deltas * jax.nn.sigmoid(importance)
        rows = mask_idx // H
        cols = mask_idx % H
        vals = jnp.einsum('tk,tks->ts', rw, weighted[top_idx])
        xg = xt[:, cols]
        contrib = jax.ops.segment_sum((xg * vals).T, rows, num_segments=H)
        out = xt @ W.T + contrib.T
        return out.reshape(B, S, H)

    def _L1_xattn_ref(x, context, context_lens, Wq, bq, gq, Wk, bk, gk, Wv, bv, Wk_img, bk_img, gk_img, Wv_img, bv_img, Wo, bo):
        import jax, jax.numpy as jnp
        import numpy as np
        DIM = 256
        N_HEADS = 16
        HEAD_DIM = DIM // N_HEADS
        EPS = 1e-06
        IMG_LEN = 257

        def rms_norm(x, g, eps=EPS):
            var = jnp.mean(x * x, axis=-1, keepdims=True)
            return x * jax.lax.rsqrt(var + eps) * g

        def _attend(q, k, v, k_mask=None):
            scale = 1.0 / jnp.sqrt(jnp.asarray(HEAD_DIM, q.dtype))
            scores = jnp.einsum('bqnd,bknd->bnqk', q, k) * scale
            if k_mask is not None:
                neg = jnp.asarray(jnp.finfo(scores.dtype).min, scores.dtype)
                scores = jnp.where(k_mask[:, None, None, :], scores, neg)
            probs = jax.nn.softmax(scores, axis=-1)
            return jnp.einsum('bnqk,bknd->bqnd', probs, v)
        b = x.shape[0]
        n, d = (N_HEADS, HEAD_DIM)
        ctx_img = context[:, :IMG_LEN]
        ctx_txt = context[:, IMG_LEN:]
        q = rms_norm(x @ Wq + bq, gq).reshape(b, -1, n, d)
        k = rms_norm(ctx_txt @ Wk + bk, gk).reshape(b, -1, n, d)
        v = (ctx_txt @ Wv + bv).reshape(b, -1, n, d)
        k_img = rms_norm(ctx_img @ Wk_img + bk_img, gk_img).reshape(b, -1, n, d)
        v_img = (ctx_img @ Wv_img + bv_img).reshape(b, -1, n, d)
        img_x = _attend(q, k_img, v_img)
        k_mask = jnp.arange(k.shape[1])[None, :] < context_lens[:, None]
        txt_x = _attend(q, k, v, k_mask)
        out = (txt_x + img_x).reshape(b, -1, n * d)
        return out @ Wo + bo

    def _L1_ffn_ref(x, w_gate_up, w_down):
        import jax, jax.numpy as jnp
        import numpy as np
        EPS = 1e-05

        def _quant_weight(w):
            scale = jnp.clip(jnp.mean(jnp.abs(w)), EPS, None)
            wq = jnp.clip(jnp.round(w / scale), -1.0, 1.0) * scale
            return w + jax.lax.stop_gradient(wq - w)

        def _quant_act(x):
            scale = 127.0 / jnp.clip(jnp.max(jnp.abs(x), axis=-1, keepdims=True), EPS, None)
            xq = jnp.clip(jnp.round(x * scale), -128.0, 127.0) / scale
            return x + jax.lax.stop_gradient(xq - x)

        def bitlinear(x, w):
            return jnp.einsum('btc,oc->bto', _quant_act(x), _quant_weight(w))
        h = bitlinear(x, w_gate_up)
        a, b = jnp.split(h, 2, axis=-1)
        h = jax.nn.silu(a) * b
        return bitlinear(h, w_down)
    x = x + jnp.tanh(g_xattn[0]) * _L0_xattn_ref(_layernorm(x, axis=-1), ctx_2048, L0_xattn_Wq, L0_xattn_Wk, L0_xattn_Wv)
    x = x + jnp.tanh(g_ffn[0]) * _L0_ffn_ref(_layernorm(x, axis=-1), L0_ffn_gate_w, L0_ffn_W, L0_ffn_atoms, L0_ffn_expert_atom_weights, L0_ffn_importance, L0_ffn_mask_idx)
    x = x + jnp.tanh(g_xattn[1]) * _L1_xattn_ref(_layernorm(x, axis=-1), ctx_2048, L1_xattn_context_lens, L1_xattn_Wq, L1_xattn_bq, L1_xattn_gq, L1_xattn_Wk, L1_xattn_bk, L1_xattn_gk, L1_xattn_Wv, L1_xattn_bv, L1_xattn_Wk_img, L1_xattn_bk_img, L1_xattn_gk_img, L1_xattn_Wv_img, L1_xattn_bv_img, L1_xattn_Wo, L1_xattn_bo)
    x = x + jnp.tanh(g_ffn[1]) * _L1_ffn_ref(_layernorm(x, axis=-1), L1_ffn_w_gate_up, L1_ffn_w_down)
    return x

_drawn_inputs = setup_inputs


def setup_inputs(seed=0):
    import zlib

    import numpy as np

    out = dict(_drawn_inputs(seed))
    spreads = {'g_ffn': (-1.0, 0.6),
     'L1_xattn_bq': (0.0, 0.8),
     'L1_xattn_gq': (1.0, 0.6),
     'L1_xattn_bk': (0.0, 0.1),
     'L1_xattn_gk': (1.0, 0.2),
     'L1_xattn_bv': (0.0, 0.1),
     'L1_xattn_bk_img': (0.0, 0.8),
     'L1_xattn_gk_img': (1.0, 0.6),
     'L1_xattn_bv_img': (0.0, 0.321),
     'L1_xattn_bo': (0.0, 0.1)}
    factors = {'L0_ffn_gate_w': 8.0,
     'L0_ffn_atoms': 8.0,
     'L0_ffn_expert_atom_weights': 8.0,
     'L0_ffn_importance': 8.0,
     'L1_xattn_Wq': 3.441,
     'L1_xattn_Wk_img': 3.263,
     'L1_ffn_w_gate_up': 6.451,
     'L1_ffn_w_down': 5.808}
    for name, (base, spread) in spreads.items():
        noise = np.random.default_rng([zlib.crc32(name.encode()), seed]).standard_normal(out[name].shape)
        drawn = base * np.exp(spread * noise) if base else spread * noise
        out[name] = jnp.asarray(drawn.astype(out[name].dtype))
    for name, factor in factors.items():
        out[name] = (out[name] * factor).astype(out[name].dtype)
    return out
```

```python
from contextlib import ExitStack

import concourse.bass as bass
from concourse import mybir

F32 = mybir.dt.float32
F16 = mybir.dt.float16
BF16 = mybir.dt.bfloat16
I32 = mybir.dt.int32
U32 = mybir.dt.uint32
ALU = mybir.AluOpType
ACT = mybir.ActivationFunctionType
AX = mybir.AxisListType

P = 128
B, N, D = 8, 128, 256
KD = D // P
H0, DH0 = 32, 8
H1, DH1 = 16, 16
E, A, NS = 8, 64, 2048
NCH = NS // P
FF = 1024
LN_EPS, RMS_EPS, Q_EPS = 1e-5, 1e-6, 1e-5
ROUND = 1.5 * 2.0 ** 23
SCATTERS_BEFORE = 4

SEMAPHORES = """
passed const_ready x_first x_rest ct_loaded0 ct_loaded1 wa_loaded wkv_loaded small_loaded idx_loaded
atoms_loaded wb_loaded wc_loaded cvec_loaded wgu_loaded wd_loaded tanh_done
ln_stats ln_mv ln_veps ln_rstd ln_xn ln_xt_pe ln_xt
a_qk_pe kv_pe a_sq a_ss a_sse a_rs a_qkn a_v a_hi a_lo a_stq_pe a_stk_pe a_qs a_ks
a_s_pe a_exp a_pv_pe a_ot a_otok_pe a_rd a_att a_x
t_f32 t_eq t_eqm t_cnt t_int t_new t_soft t_softact t_smt_pe t_smt t_dt_pe t_sig t_sigact t_wt
t_piece t_sum_pe t_vals t_zero t_zeroed t_stage t_scattered t_loaded b_table
w_abs w_sum w_sum_pe w_scale w_mask w_tern
b_log_pe b_gate b_exp b_y_pe b_y
c_vec c_qkb c_vb c_qk_pe c_sq c_sse c_rs c_norm c_hi c_lo c_stq_pe c_stk_pe c_qs c_ks
c_s_pe c_max c_nb c_exp c_pt_pe c_pt c_pv_pe c_ot c_otok_pe c_rd c_on c_ont_pe c_ont c_wo_pe c_wo
c_x
d_amax d_scale d_round d_xq d_xqt_pe d_xqt d_up_pe d_th d_u d_h d_hmax d_hscale d_hround d_hq
d_hqt_pe d_hqt d_down_pe d_beta d_out stored
""".split()


class Tile:

    def __init__(self, pair, parity):
        self.pair, self.p = pair, parity
        self.b = pair * 2 + parity
        self.first = isinstance(pair, int) and self.b == 0

    def later(self, n):
        q = self.p + n
        return Tile(self.pair + q // 2, q % 2)


def over_batches(eng, body):
    body(Tile(0, 0), 2)
    body(Tile(0, 1), 2)
    with eng.Fori(1, B // 2 - 1) as i:
        for p in range(2):
            body(Tile(i, p), 2)
    body(Tile(B // 2 - 1, 0), 1)
    body(Tile(B // 2 - 1, 1), 0)


def after(eng, sem, value):
    if not isinstance(value, int) or value > 0:
        eng.wait_ge(sem, value)


def wait_alone(eng, sem, value, s):
    eng.wait_ge(sem, value)
    eng.sem_inc(s["passed"], 1)


def strided(view, dims):
    return bass.AP(tensor=view.tensor, offset=view.offset, ap=[list(view.ap[0])] + [list(d) for d in dims])


def spread(dram, n):
    return bass.AP(tensor=dram.tensor, offset=dram.offset, ap=[[0, P], [1, n]])


def build(nc, x, ctx_t, g_xattn, g_ffn, a_wq, a_wkv, b_gate, b_w, b_atoms, b_eaw, b_imp, b_idx,
          c_wq, c_wkv, c_bqk, c_bv, c_gq, c_gk, c_wo, c_bo, d_wgu, d_wd, out):
    stack = ExitStack()
    with stack:
        def sb(name, shape, dt=F32):
            return stack.enter_context(nc.sbuf_tensor(name, shape, dt))

        s = {n: stack.enter_context(nc.semaphore(n)) for n in SEMAPHORES}
        pair = [stack.enter_context(nc.psum_tensor(f"banks{2 * i}_{2 * i + 1}", [P, 1024], F32)) for i in range(4)]
        bank = [pair[i // 2][:, (i % 2) * 512:(i % 2 + 1) * 512] for i in range(8)]

        def banks(first):
            return pair[first // 2][:, :]

        X = sb("X", [P, B, D])
        id32 = sb("id32", [P, P])
        id16 = sb("id16", [P, P], F16)
        idbf = sb("idbf", [P, P], BF16)
        ones = sb("ones", [P, P])
        below = sb("below", [P, P], BF16)
        neghalf = sb("neghalf", [P, 64])
        eps = sb("eps", [P, 3])
        iota8 = sb("iota8", [P, 8])
        dump = sb("dump", [P, NCH])
        gains = sb("gains", [P, 4])
        tg = sb("tg", [P, 4])
        stats = sb("stats", [P, 6])
        mv = sb("mv", [P, 2])
        veps = sb("veps", [P, 1])
        rstd = sb("rstd", [P, 1])
        xn = sb("xn", [P, D])
        xt = [sb(f"xt{p}", [P, KD, P]) for p in range(2)]
        ct = [sb(f"ct{p}", [P, KD, P]) for p in range(2)]
        wqa = sb("wqa", [P, KD, D])
        wkva = sb("wkva", [P, KD, 2 * D])
        sq = sb("sq", [P, 2 * D])
        ss = sb("ss", [P, 2 * H0])
        sse = sb("sse", [P, 2 * H0])
        rs = sb("rs", [P, 2 * H0])
        qkn = sb("qkn", [P, 2 * D])
        stq = sb("stq", [P, 4 * D], F16)
        stk = sb("stk", [P, 4 * D], F16)
        qs = [sb(f"qs{p}", [P, 8, P], F16) for p in range(2)]
        ks = [sb(f"ks{p}", [P, 8, P], F16) for p in range(2)]
        ve = [sb(f"ve{p}", [P, H0 * 32]) for p in range(2)]
        probs = [sb(f"probs{h}", [P, 16 * P]) for h in range(2)]
        ots = sb("ots", [P, 3 * P])
        rd = sb("rd", [P, H0])
        att = sb("att", [P, D])
        table = sb("table", [P, KD * D * E])
        idx_row = probs[0][:, :].bitcast(I32)
        idx_rowf = probs[1]
        idx_col = sb("idx_col", [P, NCH], I32)
        idx_colf = sb("idx_colf", [P, NCH])
        same = sb("same", [P, NS], BF16)
        same_below = sb("same_below", [P, NS], BF16)
        ci = sb("ci", [P, NCH], I32)
        ri = sb("ri", [P, NCH], I32)
        cf = sb("cf", [P, NCH])
        rf = sb("rf", [P, NCH])
        rowid = sb("rowid", [P, NCH])
        cnt = sb("cnt", [P, NCH])
        away = sb("away", [P, NCH])
        newid = sb("newid", [P, NCH], U32)
        atoms = sb("atoms", [A, NS])
        eaw = sb("eaw", [E, A])
        eaw_max = sb("eaw_max", [E, 1])
        eaw_exp = sb("eaw_exp", [E, A])
        eaw_sum = sb("eaw_sum", [E, 1])
        eaw_soft = sb("eaw_soft", [E, A])
        soft_t = sb("soft_t", [A, E])
        imp = sb("imp", [P, NCH * E])
        sig = sb("sig", [P, NCH * E])
        wt = sb("wt", [P, NCH * E])
        rest = sb("rest", [P, NCH * E])
        piece = [sb(f"piece{i}", [P, NCH * E], BF16) for i in range(3)]
        vals = sb("vals", [P, NCH * E])
        stage_idx = sb("stage_idx", [P, 1], U32)
        stage_val = sb("stage_val", [P, E])
        wb = sb("wb", [P, KD, D])
        gw = sb("gw", [P, KD, E])
        dw = sb("dw", [P, KD, E, D])
        l8 = sb("l8", [P, E])
        m8 = sb("m8", [P, 8])
        i8 = sb("i8", [P, 8], U32)
        i2 = sb("i2", [P, 2])
        gsm = sb("gsm", [P, 8])
        oh = sb("oh", [P, 2, E])
        gate = [sb(f"gate{p}", [P, E]) for p in range(2)]
        wqc = sb("wqc", [P, KD, D])
        wkvc = sb("wkvc", [P, KD, 2 * D])
        woc = sb("woc", [P, KD, D])
        bqk = sb("bqk", [P, 2 * D])
        bv = sb("bv", [P, D])
        bo = sb("bo", [P, D])
        gqk = sb("gqk", [P, 2, D])
        gscale = sb("gscale", [P, 4])
        ssc = sb("ssc", [P, 2])
        ssce = sb("ssce", [P, 2])
        rsc = sb("rsc", [P, 2])
        vce = [sb(f"vce{p}", [P, H1 * 32]) for p in range(2)]
        mx = sb("mx", [P, H1])
        nb = sb("nb", [P, H1])
        den = sb("den", [P, H1])
        pc, pts = probs
        otc = sb("otc", [P, D])
        rdc = sb("rdc", [P, H1])
        on = sb("on", [P, D])
        ont = sb("ont", [P, KD, P])
        wo_out = sb("wo_out", [P, D])
        wgu = sb("wgu", [P, KD * 2 * FF])
        wd = sb("wd", [P, 8 * D])
        wgu_q = sb("wgu_q", [P, KD * 2 * FF], BF16)
        wd_q = sb("wd_q", [P, 8 * D], BF16)
        neg = sb("neg", [P, 768], BF16)
        junk = sb("junk", [P, 768])
        wabs = sb("wabs", [P, 2, B])
        wsum = sb("wsum", [P, 2])
        wscale = sb("wscale", [P, 2])
        wlim = sb("wlim", [P, 2, 2])
        wsc127 = sb("wsc127", [P, 2])
        am = sb("am", [P, 1])
        ac = sb("ac", [P, 1])
        xsc = sb("xsc", [P, 2])
        alpha = [sb(f"alpha{p}", [P, 4]) for p in range(2)]
        xr = sb("xr", [P, D])
        xq = sb("xq", [P, D], BF16)
        xqt = [sb(f"xqt{p}", [P, KD, P], BF16) for p in range(2)]
        th, u, hid, hr = (table[:, i * FF:(i + 1) * FF] for i in range(4))
        hm = sb("hm", [P, 4])
        hq = sb("hq", [P, FF], BF16)
        hqt = sb("hqt", [P, 8, P], BF16)

        scratch = nc.dram_tensor("delta_table", (D * D + P, E), F32, kind="Internal").ap()

        SM = bank[4:6]
        OTA, OTOKA = bank[6], bank[7]

        block = stack.enter_context(nc.Block())

        @block.sync
        def _(sp):
            sp.dma_start(X[:, 0:2, :], x[0:2].rearrange("b n d -> n b d")).then_inc(s["x_first"], 16)
            sp.dma_start(wqa[:, :, :], a_wq.rearrange("(k p) o -> p k o", p=P)).then_inc(s["wa_loaded"], 16)

            def load_ct(t, stage):
                after(sp, s["kv_pe"], stage * B + t.b - 1)
                sp.dma_start(ct[t.p][:, :, :], ctx_t[t.b].rearrange("(k p) m -> p k m", p=P))\
                  .then_inc(s[f"ct_loaded{t.p}"], 16)

            load_ct(Tile(0, 0), 0)
            sp.dma_start(wkva[:, :, :], a_wkv.rearrange("(k p) o -> p k o", p=P)).then_inc(s["wkv_loaded"], 16)
            load_ct(Tile(0, 1), 0)
            sp.dma_start(X[:, 2:B, :], x[2:B].rearrange("b n d -> n b d")).then_inc(s["x_rest"], 16)
            sp.wait_ge(s["t_zero"], 1)
            sp.dma_start(scratch[0:D * D, :].rearrange("(p n) e -> p (n e)", p=P), table[:, :]).then_inc(s["t_zeroed"], 16)
            sp.dma_start(scratch[D * D:D * D + P, :], table[:, 0:E]).then_inc(s["t_zeroed"], 16)
            sp.dma_start(wgu[:, :].rearrange("p (k o) -> p k o", k=KD), d_wgu.rearrange("(k p) o -> p k o", p=P)).then_inc(s["wgu_loaded"], 16)
            sp.dma_start(wd[:, :].rearrange("p (k o) -> p k o", k=8), d_wd.rearrange("(k p) o -> p k o", p=P)).then_inc(s["wd_loaded"], 16)
            sp.dma_start(wb[:, :, :], b_w.rearrange("(k p) o -> p k o", p=P)).then_inc(s["wb_loaded"], 16)
            sp.dma_start(gw[:, :, :], b_gate.rearrange("(k p) o -> p k o", p=P)).then_inc(s["wb_loaded"], 16)
            sp.dma_start(wqc[:, :, :], c_wq.rearrange("(k p) o -> p k o", p=P)).then_inc(s["wc_loaded"], 16)
            sp.dma_start(wkvc[:, :, :], c_wkv.rearrange("(k p) o -> p k o", p=P)).then_inc(s["wc_loaded"], 16)
            sp.dma_start(woc[:, :, :], c_wo.rearrange("(k p) o -> p k o", p=P)).then_inc(s["wc_loaded"], 16)
            sp.dma_start(bqk[:, :], spread(c_bqk, 2 * D)).then_inc(s["cvec_loaded"], 16)
            sp.dma_start(bv[:, :], spread(c_bv, D)).then_inc(s["cvec_loaded"], 16)
            sp.dma_start(bo[:, :], spread(c_bo, D)).then_inc(s["cvec_loaded"], 16)
            sp.dma_start(gqk[:, 0, :], spread(c_gq, D)).then_inc(s["cvec_loaded"], 16)
            sp.dma_start(gqk[:, 1, :], spread(c_gk, D)).then_inc(s["cvec_loaded"], 16)
            with sp.Fori(1, B // 2) as i:
                for p in range(2):
                    load_ct(Tile(i, p), 0)
            sp.wait_ge(s["t_scattered"], 16 * NCH)
            sp.dma_start(table[:, :].rearrange("p (k n) -> p k n", k=KD),
                         scratch[0:D * D, :].rearrange("(k p n) e -> p k (n e)", p=P, k=KD)).then_inc(s["t_loaded"], 16)
            with sp.Fori(0, B // 2) as i:
                for p in range(2):
                    load_ct(Tile(i, p), 1)
            with sp.Fori(0, B) as b:
                sp.wait_ge(s["d_out"], b + 1)
                sp.dma_start(out[b], X[:, b, :]).then_inc(s["stored"], 16)
            sp.wait_ge(s["stored"], 16 * B)

        @block.gpsimd
        def _(gp):
            gp.memset(id32[:, :], 0.0).then_inc(s["const_ready"], 1)
            gp.memset(ones[:, :], 1.0).then_inc(s["const_ready"], 1)
            gp.wait_ge(s["const_ready"], 2)
            gp.affine_select(out=id32[:, :], in_=id32[:, :], compare_op=ALU.not_equal, fill=1.0, base=0,
                             pattern=[[-1, P]], channel_multiplier=1).then_inc(s["const_ready"], 1)
            gp.memset(neghalf[:, :], -0.5)
            gp.memset(eps[:, 0:1], LN_EPS)
            gp.memset(eps[:, 1:2], DH0 * RMS_EPS)
            gp.memset(eps[:, 2:3], D * RMS_EPS).then_inc(s["const_ready"], 1)
            gp.wait_ge(s["const_ready"], 4)
            gp.tensor_copy(id16[:, :], id32[:, :]).then_inc(s["const_ready"], 1)
            gp.tensor_copy(idbf[:, :], id32[:, :]).then_inc(s["const_ready"], 1)

            def ln_rstd(stage, t):
                T = stage * B + t.b
                gp.wait_ge(s["ln_mv"], T + 1)
                gp.tensor_tensor(veps[:, :], mv[:, 1:2], eps[:, 0:1], ALU.add).then_inc(s["ln_veps"], 1)
                gp.wait_ge(s["ln_veps"], T + 1)
                gp.tensor_tensor(rstd[:, :], veps[:, :], neghalf[:, 0:1], ALU.pow).then_inc(s["ln_rstd"], 1)

            def rms_a(t):
                gp.wait_ge(s["a_ss"], t.b + 1)
                gp.tensor_tensor(sse[:, :], ss[:, :], eps[:, 1:2].broadcast_to([P, 2 * H0]), ALU.add).then_inc(s["a_sse"], 1)
                gp.wait_ge(s["a_sse"], t.b + 1)
                gp.tensor_tensor(rs[:, :], sse[:, :], neghalf[:, :], ALU.pow).then_inc(s["a_rs"], 1)

            def low_parts(t, hi, norm, done, width):
                reps = D // width
                q3 = qkn[:, 0:D].rearrange("p (h d) -> p h d", d=width).unsqueeze(2).broadcast_to([P, reps, 2, width])
                k3 = qkn[:, D:2 * D].rearrange("p (h d) -> p h d", d=width).unsqueeze(2).broadcast_to([P, reps, 2, width])
                q4 = stq[:, :].rearrange("p (h r d) -> p h r d", r=4, d=width)
                k4 = stk[:, :].rearrange("p (h r d) -> p h r d", r=4, d=width)
                gp.wait_ge(s[hi], 2 * t.b + 1)
                gp.tensor_tensor(q4[:, :, 2:4, :], q3, q4[:, :, 0:2, :], ALU.subtract).then_inc(s[done], 1)
                gp.wait_ge(s[hi], 2 * t.b + 2)
                gp.tensor_tensor(k4[:, :, 1:4:2, :], k3, k4[:, :, 0:3:2, :], ALU.subtract).then_inc(s[done], 1)

            def scatter(j):
                after(gp, s["t_scattered"], 16 * j)
                gp.tensor_copy(stage_idx[:, :], newid[:, bass.ds(j, 1)])
                gp.tensor_copy(stage_val[:, :], vals[:, bass.ds(j * E, E)]).then_inc(s["t_stage"], 1)
                wait_alone(gp, s["t_stage"], j + 1, s)
                gp.indirect_dma_start(out=scratch, out_offset=bass.IndirectOffsetOnAxis(ap=stage_idx[:, 0:1], axis=0),
                                      in_=stage_val[:, :], in_offset=None, compute_op=ALU.add)\
                  .then_inc(s["t_scattered"], 16)

            ln_rstd(0, Tile(0, 0))
            ln_rstd(0, Tile(0, 1))
            gp.memset(table[:, :], 0.0).then_inc(s["t_zero"], 1)
            gp.memset(ve[0][:, :], 0.0).then_inc(s["const_ready"], 1)
            gp.memset(ve[1][:, :], 0.0).then_inc(s["const_ready"], 1)
            gp.wait_ge(s["const_ready"], 8)
            for p in range(2):
                for R, nr in ((0, 3), (1, 3), (2, 2)):
                    last = gp.memset(strided(ve[p][:, 384 * R + 8:], [[137, nr], [32, 4]]), 1.0)
            last.then_inc(s["const_ready"], 1)
            rms_a(Tile(0, 0))
            low_parts(Tile(0, 0), "a_hi", "a_qkn", "a_lo", DH0)
            gp.iota(iota8[:, :], pattern=[[1, 8]], base=0, channel_multiplier=0, allow_small_or_imprecise_dtypes=True)
            gp.iota(dump[:, :], pattern=[[0, NCH]], base=D * D, channel_multiplier=1, allow_small_or_imprecise_dtypes=True)
            gp.memset(below[:, :], 0.0).then_inc(s["const_ready"], 1)
            gp.wait_ge(s["const_ready"], 10)
            gp.affine_select(out=below[:, :], in_=below[:, :], compare_op=ALU.is_gt, fill=1.0, base=1,
                             pattern=[[1, P]], channel_multiplier=-1).then_inc(s["const_ready"], 1)
            gp.memset(vce[0][:, :], 0.0)
            gp.memset(vce[1][:, :], 0.0).then_inc(s["const_ready"], 1)
            gp.wait_ge(s["t_new"], 9)
            gp.wait_ge(s["t_vals"], 1)
            gp.wait_ge(s["t_zeroed"], 32)
            for j in range(SCATTERS_BEFORE):
                scatter(j)

            def batch_a(t, ahead):
                if ahead >= 1:
                    rms_a(t.later(1))
                if ahead >= 2:
                    scatter(t.b * 2 + SCATTERS_BEFORE)
                if ahead >= 1:
                    low_parts(t.later(1), "a_hi", "a_qkn", "a_lo", DH0)
                if ahead >= 2:
                    ln_rstd(0, t.later(2))
                    scatter(t.b * 2 + SCATTERS_BEFORE + 1)
                if ahead == 1:
                    gp.wait_ge(s["t_loaded"], 16)
                    gp.wait_ge(s["wb_loaded"], 32)
                    for k in range(KD):
                        by_e = table[:, k * D * E:(k + 1) * D * E].rearrange("p (r e) -> p e r", e=E)
                        gp.tensor_tensor(dw[:, k, :, :], by_e, wb[:, k, :].unsqueeze(1).broadcast_to([P, E, D]),
                                         ALU.add).then_inc(s["b_table"], 1)

            over_batches(gp, batch_a)

            ln_rstd(1, Tile(0, 0))

            def batch_b(t, ahead):
                if ahead >= 1:
                    ln_rstd(1, t.later(1))

            over_batches(gp, batch_b)

            def rms_c(t):
                gp.wait_ge(s["c_sq"], 2 * t.b + 2)
                gp.tensor_tensor(ssce[:, :], ssc[:, :], eps[:, 2:3].broadcast_to([P, 2]), ALU.add).then_inc(s["c_sse"], 1)
                gp.wait_ge(s["c_sse"], t.b + 1)
                gp.tensor_tensor(rsc[:, :], ssce[:, :], neghalf[:, 0:2], ALU.pow).then_inc(s["c_rs"], 1)

            ln_rstd(2, Tile(0, 0))
            rms_c(Tile(0, 0))
            low_parts(Tile(0, 0), "c_hi", "c_norm", "c_lo", DH1)
            ln_rstd(2, Tile(0, 1))

            def batch_c(t, ahead):
                if ahead >= 1:
                    rms_c(t.later(1))
                    low_parts(t.later(1), "c_hi", "c_norm", "c_lo", DH1)
                if ahead >= 2:
                    ln_rstd(2, t.later(2))

            over_batches(gp, batch_c)

            ln_rstd(3, Tile(0, 0))

            def batch_d(t, ahead):
                if ahead >= 1:
                    ln_rstd(3, t.later(1))
                wait_alone(gp, s["d_hscale"], 3 * t.b + 3, s)
                gp.tensor_scalar(hr, hid, hm[:, 2:3], ROUND, ALU.mult, ALU.add).then_inc(s["d_hround"], 1)

            over_batches(gp, batch_d)

        @block.scalar
        def _(act):
            act.dma_start(gains[:, 0:2], spread(g_xattn, 2)).then_inc(s["small_loaded"], 16)
            act.dma_start(gains[:, 2:4], spread(g_ffn, 2)).then_inc(s["small_loaded"], 16)
            act.dma_start(idx_col[:, :], b_idx.rearrange("(c p) -> p c", p=P), allow_slow_non_contiguous=True).then_inc(s["idx_loaded"], 16)
            act.dma_start(idx_row, spread(b_idx, NS)).then_inc(s["idx_loaded"], 16)
            act.dma_start(eaw[:, :], b_eaw).then_inc(s["atoms_loaded"], 16)
            act.dma_start(atoms[:, :], b_atoms).then_inc(s["atoms_loaded"], 16)
            act.dma_start(imp[:, :], b_imp).then_inc(s["atoms_loaded"], 16)
            act.wait_ge(s["small_loaded"], 32)
            act.activation(tg[:, :], gains[:, :], ACT.Tanh).then_inc(s["tanh_done"], 1)

            def copy_xt(stage, t, src):
                act.wait_ge(s["ln_xt_pe"], stage * B + t.b + 1)
                act.activation(xt[t.p][:, :, :].rearrange("p k n -> p (k n)"), src, ACT.Copy)\
                   .then_inc(s["ln_xt"], 1)

            def square_a(t):
                act.wait_ge(s["a_qk_pe"], t.b + 1)
                after(act, s["a_ss"], t.b)
                act.activation(sq[:, :], SM[1][:, :], ACT.Square).then_inc(s["a_sq"], 1)

            def copy_v_a(t):
                act.wait_ge(s["kv_pe"], t.b + 1)
                for R, nr in ((0, 3), (1, 3), (2, 2)):
                    src = strided(SM[0][:, 96 * R:], [[32, nr], [8, 4], [1, 8]])
                    dst = strided(ve[t.p][:, 384 * R:], [[137, nr], [32, 4], [1, 8]])
                    last = act.activation(dst, src, ACT.Copy)
                last.then_inc(s["a_v"], 1)

            def high_parts(t, ready, width, used, done):
                reps = D // width
                act.wait_ge(s[ready[0]], ready[1])
                after(act, s[used], t.b)
                for half, dst in ((0, stq[:, :].rearrange("p (h r d) -> p h r d", r=4, d=width)[:, :, 0:2, :]),
                                  (1, stk[:, :].rearrange("p (h r d) -> p h r d", r=4, d=width)[:, :, 0:3:2, :])):
                    src = qkn[:, half * D:(half + 1) * D].rearrange("p (h d) -> p h d", d=width)
                    act.activation(dst, src.unsqueeze(2).broadcast_to([P, reps, 2, width]), ACT.Copy)\
                       .then_inc(s[done], 1)

            def copy_qs(t, ready, src, done):
                act.wait_ge(s[ready], t.b + 1)
                act.activation(qs[t.p][:, :, :].rearrange("p w n -> p (w n)"), src, ACT.Copy).then_inc(s[done], 1)

            def exp_a(t, step):
                half, pair = step // 2, step % 2
                act.wait_ge(s["a_s_pe"], 4 * t.b + step + 1)
                act.activation(probs[half][:, pair * 1024:(pair + 1) * 1024], banks(2 * pair), ACT.Exp,
                               scale=float(DH0) ** 0.5).then_inc(s["a_exp"], 1)

            def copy_ot(t):
                act.wait_ge(s["a_pv_pe"], 2 * t.b + 2)
                after(act, s["a_otok_pe"], t.b)
                act.activation(ots[:, :], OTA[:, 0:384], ACT.Copy).then_inc(s["a_ot"], 1)

            t0, t1 = Tile(0, 0), Tile(0, 1)
            act.wait_ge(s["const_ready"], 9)
            copy_xt(0, t0, SM[0][:, 0:256])
            square_a(t0)
            copy_v_a(t0)
            high_parts(t0, ("a_qkn", 1), DH0, "a_stk_pe", "a_hi")
            copy_qs(t0, "a_stq_pe", SM[0][:, :].bitcast(F16), "a_qs")
            copy_xt(0, t1, SM[0][:, 0:256])
            act.wait_ge(s["t_soft"], 1)
            act.activation(eaw_exp[:, :], eaw[:, :], ACT.Exp, bias=eaw_max[:, 0:1], accum_out=eaw_sum[:, 0:1])\
               .then_inc(s["t_softact"], 1)
            act.activation(sig[:, :], imp[:, :], ACT.Exp, scale=-1.0).then_inc(s["t_sigact"], 1)
            act.wait_ge(s["wgu_loaded"], 16)
            act.wait_ge(s["wd_loaded"], 16)

            def batch_a(t, ahead):
                exp_a(t, 0)
                exp_a(t, 1)
                if ahead >= 1:
                    square_a(t.later(1))
                exp_a(t, 2)
                if ahead >= 1:
                    copy_v_a(t.later(1))
                    high_parts(t.later(1), ("a_qkn", t.later(1).b + 1), DH0, "a_stk_pe", "a_hi")
                exp_a(t, 3)
                after(act, s["w_abs"], 2 * t.b)
                act.activation(junk[:, 0:512], wgu[:, bass.ds(t.b * 512, 512)], ACT.Abs, accum_out=wabs[:, 0, bass.ds(t.b, 1)])\
                   .then_inc(s["w_abs"], 1)
                act.activation(junk[:, 512:768], wd[:, bass.ds(t.b * 256, 256)], ACT.Abs, accum_out=wabs[:, 1, bass.ds(t.b, 1)])\
                   .then_inc(s["w_abs"], 1)
                if ahead >= 1:
                    copy_qs(t.later(1), "a_stq_pe", SM[0][:, :].bitcast(F16), "a_qs")
                copy_ot(t)
                if ahead >= 2:
                    copy_xt(0, t.later(2), SM[0][:, 0:256])

            over_batches(act, batch_a)

            def gate_exp(t):
                act.wait_ge(s["b_gate"], 10 * t.b + 4)
                act.activation(gsm[:, 1:2], gsm[:, 0:1], ACT.Exp).then_inc(s["b_exp"], 1)

            copy_xt(1, t0, bank[6][:, 0:256])
            gate_exp(t0)

            def batch_b(t, ahead):
                if ahead >= 1:
                    copy_xt(1, t.later(1), bank[6][:, 0:256])
                    gate_exp(t.later(1))

            over_batches(act, batch_b)

            def square_c(t):
                act.wait_ge(s["c_qkb"], t.b + 1)
                after(act, s["c_sq"], 2 * t.b)
                for i in range(2):
                    act.activation(junk[:, i * D:(i + 1) * D], qkn_raw[:, i * D:(i + 1) * D], ACT.Square,
                                   accum_out=ssc[:, i:i + 1]).then_inc(s["c_sq"], 1)

            qkn_raw = sq

            def exp_c(t, step):
                for i in range(8):
                    at = step * 8 + i
                    if i == 0:
                        act.wait_ge(s["c_nb"], 2 * t.b + step + 1)
                    if i % 4 == 0:
                        after(act, s["c_pt_pe"], 4 * t.b)
                    act.activation(pc[:, at * P:(at + 1) * P], bank[2 * step + i // 4][:, (i % 4) * P:(i % 4 + 1) * P],
                                   ACT.Exp, bias=nb[:, at:at + 1], scale=gscale[:, 2:3],
                                   accum_out=den[:, at:at + 1]).then_inc(s["c_exp"], 1)

            def copy_ont(t):
                act.wait_ge(s["c_ont_pe"], t.b + 1)
                act.activation(ont[:, :, :].rearrange("p k n -> p (k n)"), bank[7][:, 0:256], ACT.Copy)\
                   .then_inc(s["c_ont"], 1)

            def copy_otc(t):
                act.wait_ge(s["c_pv_pe"], 4 * t.b + 4)
                after(act, s["c_otok_pe"], t.b)
                act.activation(otc[:, :], bank[6][:, 0:256], ACT.Copy).then_inc(s["c_ot"], 1)

            copy_xt(2, t0, bank[7][:, 0:256])
            square_c(t0)
            high_parts(t0, ("c_norm", 2), DH1, "c_stk_pe", "c_hi")
            copy_qs(t0, "c_stq_pe", bank[4][:, :].bitcast(F16), "c_qs")
            copy_xt(2, t1, bank[7][:, 0:256])

            def batch_c(t, ahead):
                if not t.first:
                    copy_ont(t.later(-1))
                exp_c(t, 0)
                if ahead >= 1:
                    square_c(t.later(1))
                exp_c(t, 1)
                if ahead >= 1:
                    high_parts(t.later(1), ("c_norm", 2 * t.later(1).b + 2), DH1, "c_stk_pe", "c_hi")
                copy_otc(t)
                if ahead >= 1:
                    copy_qs(t.later(1), "c_stq_pe", bank[4][:, :].bitcast(F16), "c_qs")
                if ahead >= 2:
                    copy_xt(2, t.later(2), bank[7][:, 0:256])

            over_batches(act, batch_c)
            copy_ont(Tile(3, 1))

            def copy_xqt(t):
                act.wait_ge(s["d_xqt_pe"], t.b + 1)
                act.activation(xqt[t.p][:, :, :].rearrange("p k n -> p (k n)"), bank[4][:, :].bitcast(BF16)[:, 0:256],
                               ACT.Copy).then_inc(s["d_xqt"], 1)

            def tanh_d(t, h):
                act.wait_ge(s["d_up_pe"], 2 * t.b + h + 1)
                if h == 0:
                    after(act, s["d_u"], 2 * t.b)
                act.activation(th[:, h * 512:(h + 1) * 512], bank[2 * h][:, :], ACT.Tanh, scale=alpha[t.p][:, 1:2])\
                   .then_inc(s["d_th"], 1)

            def ints_d(t):
                act.wait_ge(s["d_hround"], t.b + 1)
                after(act, s["d_hqt_pe"], t.b)
                act.activation(hq[:, :], hr, ACT.Copy, bias=-ROUND).then_inc(s["d_hq"], 1)

            def copy_hqt(t):
                act.wait_ge(s["d_hqt_pe"], t.b + 1)
                after(act, s["d_down_pe"], t.b)
                act.activation(hqt[:, :, :].rearrange("p k n -> p (k n)"), bank[5][:, :].bitcast(BF16), ACT.Copy)\
                   .then_inc(s["d_hqt"], 1)

            copy_xqt(t0)
            tanh_d(t0, 0)
            tanh_d(t0, 1)

            def batch_d(t, ahead):
                if ahead >= 1:
                    copy_xqt(t.later(1))
                ints_d(t)
                if ahead >= 1:
                    tanh_d(t.later(1), 0)
                    tanh_d(t.later(1), 1)
                copy_hqt(t)

            over_batches(act, batch_d)

        @block.tensor
        def _(pe):
            mm, tr = nc.tensor.matmul, nc.tensor.transpose
            t0, t1 = Tile(0, 0), Tile(0, 1)

            def turn_xn(stage, t, dst):
                pe.wait_ge(s["ln_xn"], stage * B + t.b + 1)
                for k in range(KD):
                    last = tr(dst[:, k * P:(k + 1) * P], xn[:, k * P:(k + 1) * P], id32[:, :])
                last.then_inc(s["ln_xt_pe"], 1)

            def project(dst, lhs, rhs):
                for k in range(KD):
                    last = mm(dst, lhs[:, k, :], rhs(k), start=(k == 0), stop=(k == KD - 1))
                return last

            def xn_a(t):
                after(pe, s["a_qs"], t.b)
                turn_xn(0, t, SM[0])

            def qkv_a(t):
                pe.wait_ge(s["ln_xt"], t.b + 1)
                after(pe, s["a_ks"], t.b)
                project(SM[1][:, 0:D], xt[t.p], lambda k: wqa[:, k, :])
                pe.wait_ge(s[f"ct_loaded{t.p}"], t.pair * 16 + 16)
                project(SM[1][:, D:2 * D], ct[t.p], lambda k: wkva[:, k, 0:D]).then_inc(s["a_qk_pe"], 1)
                project(SM[0][:, 0:D], ct[t.p], lambda k: wkva[:, k, D:2 * D]).then_inc(s["kv_pe"], 1)

            def stacks(t, low, vdone, dsts, names):
                pe.wait_ge(s[low], 2 * t.b + 2)
                pe.wait_ge(s[vdone], t.b + 1)
                for src, dst, name in zip((stq, stk), dsts, names):
                    d16 = dst[:, :].bitcast(F16)
                    for w in range(8):
                        last = tr(d16[:, w * P:(w + 1) * P], src[:, w * P:(w + 1) * P], id16[:, :])
                    last.then_inc(s[name], 1)

            def scores_a(t, step):
                half, pair = step // 2, step % 2
                if step == 0:
                    pe.wait_ge(s["a_qs"], t.b + 1)
                    pe.wait_ge(s["a_ks"], t.b + 1)
                if step >= 2:
                    pe.wait_ge(s["a_exp"], 4 * t.b + step - 1)
                for g in range(4):
                    for j in range(2):
                        h4 = 2 * pair + j
                        rows = slice(32 * h4, 32 * h4 + 32)
                        last = mm(bank[h4][:, g * P:(g + 1) * P], ks[t.p][rows, 4 * half + g, :],
                                  qs[t.p][rows, 4 * half + g, :], start=True, stop=True)
                last.then_inc(s["a_s_pe"], 1)

            def pv_a(t, half):
                pe.wait_ge(s["a_exp"], 4 * t.b + 2 * half + 2)
                if half == 0:
                    after(pe, s["a_ot"], t.b)
                for g in range(4):
                    v = 4 * half + g
                    for h4 in range(4):
                        h = 4 * v + h4
                        last = mm(OTA[32 * h4:32 * h4 + 32, (v // 3) * P:(v // 3 + 1) * P], ve[t.p][:, 32 * h:32 * h + 32],
                                  probs[half][:, (4 * h4 + g) * P:(4 * h4 + g + 1) * P],
                                  start=(v % 3 == 0), stop=(v % 3 == 2 or v == 7))
                last.then_inc(s["a_pv_pe"], 1)

            def turn_out_a(t):
                pe.wait_ge(s["a_ot"], t.b + 1)
                after(pe, s["a_att"], t.b)
                for R in range(3):
                    last = tr(OTOKA[:, R * P:(R + 1) * P], ots[:, R * P:(R + 1) * P], id32[:, :])
                last.then_inc(s["a_otok_pe"], 1)

            pe.wait_ge(s["const_ready"], 9)
            xn_a(t0)
            pe.wait_ge(s["wa_loaded"], 16)
            pe.wait_ge(s["wkv_loaded"], 16)
            qkv_a(t0)
            stacks(t0, "a_lo", "a_v", SM, ("a_stq_pe", "a_stk_pe"))
            xn_a(t1)
            pe.wait_ge(s["t_soft"], 3)
            tr(bank[7][0:A, 0:E], eaw_soft[:, :], id32[0:E, 0:E]).then_inc(s["t_smt_pe"], 1)
            pe.wait_ge(s["t_smt"], 1)
            pe.wait_ge(s["atoms_loaded"], 48)
            for c in range(NCH):
                last = mm(bank[6][:, c * E:(c + 1) * E], atoms[:, c * P:(c + 1) * P], soft_t[:, :], start=True, stop=True)
            last.then_inc(s["t_dt_pe"], 1)
            pe.wait_ge(s["t_piece"], 5)
            for c in range(NCH):
                for i in range(3):
                    last = mm(bank[7][:, c * E:(c + 1) * E], same[:, c * P:(c + 1) * P], piece[i][:, c * E:(c + 1) * E],
                              start=(i == 0), stop=(i == 2))
            last.then_inc(s["t_sum_pe"], 1)
            pe.wait_ge(s["t_vals"], 1)

            def batch_a(t, ahead):
                scores_a(t, 0)
                scores_a(t, 1)
                if ahead >= 1:
                    qkv_a(t.later(1))
                scores_a(t, 2)
                pv_a(t, 0)
                scores_a(t, 3)
                if ahead >= 1:
                    stacks(t.later(1), "a_lo", "a_v", SM, ("a_stq_pe", "a_stk_pe"))
                pv_a(t, 1)
                if ahead >= 2:
                    xn_a(t.later(2))
                turn_out_a(t)

            over_batches(pe, batch_a)

            def logits(t):
                pe.wait_ge(s["ln_xt"], B + t.b + 1)
                after(pe, s["b_gate"], 10 * t.b)
                project(bank[7][:, 0:E], xt[t.p], lambda k: gw[:, k, :]).then_inc(s["b_log_pe"], 1)

            def xn_b(t):
                pe.wait_ge(s["ln_xt"], B + t.b)
                turn_xn(1, t, bank[6])

            def experts(t, unit):
                pe.wait_ge(s["b_y"], 8 * t.b + 2 * unit + 2)
                for k in range(KD):
                    last = mm(bank[unit][:, :], xt[t.p][:, k, :],
                              dw[:, k, 2 * unit:2 * unit + 2, :].rearrange("p e r -> p (e r)"), start=(k == 0), stop=(k == KD - 1))
                last.then_inc(s["b_y_pe"], 1)

            pe.wait_ge(s["a_ot"], B)
            xn_b(t0)
            pe.wait_ge(s["w_sum"], 2)
            mm(bank[5][:, 0:2], ones[:, :], wsum[:, :], start=True, stop=True).then_inc(s["w_sum_pe"], 1)
            pe.wait_ge(s["a_att"], B)
            pe.wait_ge(s["wb_loaded"], 32)
            logits(t0)
            pe.wait_ge(s["b_table"], KD)

            def batch_b(t, ahead):
                experts(t, 0)
                experts(t, 1)
                if ahead >= 1:
                    xn_b(t.later(1))
                experts(t, 2)
                if ahead >= 1:
                    logits(t.later(1))
                experts(t, 3)

            over_batches(pe, batch_b)

            def xn_c(t):
                after(pe, s["c_norm"], 2 * t.b)
                turn_xn(2, t, bank[7])

            def v_c(t):
                pe.wait_ge(s[f"ct_loaded{t.p}"], 16 * (B // 2) + t.pair * 16 + 16)
                after(pe, s["c_ot"], t.b - 1)
                project(bank[6][:, 0:D], ct[t.p], lambda k: wkvc[:, k, D:2 * D])

            def qk_c(t):
                pe.wait_ge(s["ln_xt"], 2 * B + t.b + 1)
                project(bank[7][:, 0:D], xt[t.p], lambda k: wqc[:, k, :])
                project(bank[7][:, D:2 * D], ct[t.p], lambda k: wkvc[:, k, 0:D]).then_inc(s["kv_pe"], 1)

            def scores_c(t, step):
                if step == 0:
                    pe.wait_ge(s["c_qs"], t.b + 1)
                    pe.wait_ge(s["c_ks"], t.b + 1)
                for w4 in range(4):
                    for j in range(2):
                        rows = slice(64 * j, 64 * j + 64)
                        w = 4 * step + w4
                        last = mm(bank[2 * step + j][:, w4 * P:(w4 + 1) * P], qs[t.p][rows, w, :], ks[t.p][rows, w, :],
                                  start=True, stop=True)
                last.then_inc(s["c_s_pe"], 1)

            def turn_probs(t, k):
                pe.wait_ge(s["c_exp"], 16 * t.b + 4 * k + 4)
                if k == 0:
                    pe.wait_ge(s["c_qs"], t.b + 1)
                    pe.wait_ge(s["c_ks"], t.b + 1)
                if k >= 2:
                    pe.wait_ge(s["c_pt"], 4 * t.b + k - 1)
                for i in range(4):
                    at = 4 * k + i
                    last = tr(bank[4 + k % 2][:, i * P:(i + 1) * P], pc[:, at * P:(at + 1) * P], id32[:, :])
                last.then_inc(s["c_pt_pe"], 1)

            def pv_c(t, k):
                step, j = k // 2, k % 2
                pe.wait_ge(s["c_pt"], 4 * t.b + k + 1)
                for w4 in range(4):
                    h = 2 * (4 * step + w4) + j
                    last = mm(bank[6][32 * w4:32 * w4 + 32, step * P:(step + 1) * P], vce[t.p][:, 32 * h:32 * h + 32],
                              pts[:, (4 * k + w4) * P:(4 * k + w4 + 1) * P], start=(j == 0), stop=(j == 1))
                last.then_inc(s["c_pv_pe"], 1)

            def turn_out_c(t):
                pe.wait_ge(s["c_ot"], t.b + 1)
                pe.wait_ge(s["ln_xt"], 2 * B + (min(t.b + 3, B) if isinstance(t.b, int) else t.b + 3))
                for k in range(KD):
                    last = tr(bank[7][:, k * P:(k + 1) * P], otc[:, k * P:(k + 1) * P], id32[:, :])
                last.then_inc(s["c_otok_pe"], 1)

            def turn_on(t):
                pe.wait_ge(s["c_on"], t.b + 1)
                for k in range(KD):
                    last = tr(bank[7][:, k * P:(k + 1) * P], on[:, k * P:(k + 1) * P], id32[:, :])
                last.then_inc(s["c_ont_pe"], 1)

            def out_c(t):
                pe.wait_ge(s["c_ont"], t.b + 1)
                project(bank[7][:, 0:D], ont, lambda k: woc[:, k, :]).then_inc(s["c_wo_pe"], 1)

            pe.wait_ge(s["b_gate"], 10 * B)
            pe.wait_ge(s["b_y"], 8 * B + 8)
            pe.wait_ge(s["ln_xt"], 2 * B)
            xn_c(t0)
            pe.wait_ge(s["wc_loaded"], 48)
            v_c(t0)
            qk_c(t0)
            pe.wait_ge(s["w_scale"], 3)
            stacks(t0, "c_lo", "c_vb", bank[4:6], ("c_stq_pe", "c_stk_pe"))
            xn_c(t1)

            def batch_c(t, ahead):
                before = not t.first
                prev = t.later(-1)
                if before:
                    turn_out_c(prev)
                scores_c(t, 0)
                if before:
                    turn_on(prev)
                scores_c(t, 1)
                if before:
                    out_c(prev)
                if ahead >= 1:
                    v_c(t.later(1))
                    if before:
                        after(pe, s["c_wo"], t.b)
                    qk_c(t.later(1))
                    pe.wait_ge(s["c_vb"], t.b + 2)
                for k in range(2):
                    turn_probs(t, k)
                for k in range(2):
                    pv_c(t, k)
                for k in range(2, 4):
                    turn_probs(t, k)
                for k in range(2, 4):
                    pv_c(t, k)
                if ahead >= 1:
                    stacks(t.later(1), "c_lo", "c_vb", bank[4:6], ("c_stq_pe", "c_stk_pe"))
                if ahead >= 2:
                    xn_c(t.later(2))

            over_batches(pe, batch_c)
            t7 = Tile(3, 1)
            turn_out_c(t7)
            turn_on(t7)
            out_c(t7)

            def turn_xq(t):
                pe.wait_ge(s["d_xq"], t.b + 1)
                after(pe, s["d_xqt"], t.b)
                for k in range(KD):
                    last = tr(bank[4][:, :].bitcast(BF16)[:, k * P:(k + 1) * P], xq[:, k * P:(k + 1) * P], idbf[:, :])
                last.then_inc(s["d_xqt_pe"], 1)

            def up(t):
                pe.wait_ge(s["d_xqt"], t.b + 1)
                for h in range(2):
                    after(pe, s["d_h"], 2 * t.b + h - 1)
                    for part in range(2):
                        for k in range(KD):
                            at = k * 2 * FF + part * FF + h * 512
                            last = mm(bank[2 * h + part][:, :], xqt[t.p][:, k, :], wgu_q[:, at:at + 512],
                                      start=(k == 0), stop=(k == KD - 1))
                    last.then_inc(s["d_up_pe"], 1)

            def turn_hq(t):
                pe.wait_ge(s["d_hq"], t.b + 1)
                after(pe, s["d_hqt"], t.b)
                for k in range(8):
                    last = tr(bank[5][:, :].bitcast(BF16)[:, k * P:(k + 1) * P], hq[:, k * P:(k + 1) * P], idbf[:, :])
                last.then_inc(s["d_hqt_pe"], 1)

            def down(t):
                pe.wait_ge(s["d_hqt"], t.b + 1)
                after(pe, s["d_out"], t.b)
                for k in range(8):
                    last = mm(bank[6][:, 0:D], hqt[:, k, :], wd_q[:, k * D:(k + 1) * D], start=(k == 0), stop=(k == 7))
                last.then_inc(s["d_down_pe"], 1)

            pe.wait_ge(s["c_wo"], B)
            pe.wait_ge(s["w_tern"], 2 * B)
            turn_xq(t0)
            up(t0)

            def batch_d(t, ahead):
                if ahead >= 1:
                    turn_xq(t.later(1))
                    up(t.later(1))
                turn_hq(t)
                down(t)

            over_batches(pe, batch_d)

        @block.vector
        def _(v):
            t0, t1 = Tile(0, 0), Tile(0, 1)

            def row(t):
                return X[:, bass.ds(t.b, 1), :].rearrange("p a d -> p (a d)")

            def layer_norm(stage, t):
                T = stage * B + t.b
                v.bn_stats(stats[:, :], row(t)).then_inc(s["ln_stats"], 1)
                wait_alone(v, s["ln_stats"], T + 1, s)
                v.bn_aggr(mv[:, :], stats[:, :]).then_inc(s["ln_mv"], 1)
                v.wait_ge(s["ln_rstd"], T + 1)
                after(v, s["ln_xt_pe"], T)
                v.tensor_scalar(xn[:, :], row(t), mv[:, 0:1], rstd[:, 0:1], ALU.subtract, ALU.mult)\
                 .then_inc(s["ln_xn"], 1)

            def by_head(view, h, d):
                return view.rearrange("p (h d) -> p h d", d=d)

            def sums_a(t):
                v.wait_ge(s["a_sq"], t.b + 1)
                v.tensor_reduce(ss[:, :], by_head(sq[:, :], 2 * H0, DH0), AX.X, ALU.add).then_inc(s["a_ss"], 1)

            def norm_a(t):
                v.wait_ge(s["a_rs"], t.b + 1)
                after(v, s["a_lo"], 2 * t.b)
                v.tensor_tensor(by_head(qkn[:, :], 2 * H0, DH0), by_head(SM[1][:, :], 2 * H0, DH0),
                                rs[:, :].unsqueeze(2).broadcast_to([P, 2 * H0, DH0]), ALU.mult).then_inc(s["a_qkn"], 1)

            def copy_ks(t, ready, src, done):
                v.wait_ge(s[ready], t.b + 1)
                v.tensor_copy(ks[t.p][:, :, :].rearrange("p w n -> p (w n)"), src).then_inc(s[done], 1)

            def output_a(t):
                v.wait_ge(s["a_otok_pe"], t.b + 1)
                v.reciprocal(strided(rd[:, 0:], [[12, 2], [1, 4], [4, 3]]),
                             strided(OTOKA[:, 8:], [[128, 2], [32, 4], [9, 3]]))
                v.reciprocal(strided(rd[:, 24:], [[1, 4], [4, 2]]),
                             strided(OTOKA[:, 264:], [[32, 4], [9, 2]])).then_inc(s["a_rd"], 1)
                v.wait_ge(s["a_rd"], t.b + 1)
                for R, nr in ((0, 3), (1, 3), (2, 2)):
                    last = v.tensor_tensor(strided(att[:, 96 * R:], [[32, nr], [8, 4], [1, 8]]),
                                           strided(OTOKA[:, 128 * R:], [[9, nr], [32, 4], [1, 8]]),
                                           strided(rd[:, 12 * R:], [[4, nr], [1, 4], [0, 8]]), ALU.mult)
                last.then_inc(s["a_att"], 1)
                v.wait_ge(s["a_att"], t.b + 1)
                v.scalar_tensor_tensor(row(t), att[:, :], tg[:, 0:1], row(t), ALU.mult, ALU.add).then_inc(s["a_x"], 1)

            v.wait_ge(s["x_first"], 16)
            layer_norm(0, t0)
            layer_norm(0, t1)
            sums_a(t0)
            norm_a(t0)
            copy_ks(t0, "a_stk_pe", SM[1][:, :].bitcast(F16), "a_ks")

            v.wait_ge(s["idx_loaded"], 32)
            v.tensor_copy(idx_rowf[:, :], idx_row)
            v.tensor_copy(idx_colf[:, :], idx_col[:, :]).then_inc(s["t_f32"], 1)
            v.wait_ge(s["t_f32"], 1)
            v.tensor_tensor(same[:, :].rearrange("p (c n) -> p c n", c=NCH), idx_rowf[:, :].rearrange("p (c n) -> p c n", c=NCH),
                            idx_colf[:, :].unsqueeze(2).broadcast_to([P, NCH, P]), ALU.is_equal).then_inc(s["t_eq"], 1)
            v.tensor_scalar(ci[:, :], idx_col[:, :], D - 1, None, ALU.bitwise_and).then_inc(s["t_int"], 1)
            v.tensor_scalar(ri[:, :], idx_col[:, :], 8, None, ALU.logical_shift_right).then_inc(s["t_int"], 1)
            v.wait_ge(s["const_ready"], 12)
            v.wait_ge(s["t_eq"], 1)
            v.tensor_tensor(same_below[:, :].rearrange("p (c n) -> p c n", c=NCH), same[:, :].rearrange("p (c n) -> p c n", c=NCH),
                            below[:, :].unsqueeze(1).broadcast_to([P, NCH, P]), ALU.mult).then_inc(s["t_eqm"], 1)
            v.wait_ge(s["t_eqm"], 1)
            v.tensor_reduce(cnt[:, :], same_below[:, :].rearrange("p (c n) -> p c n", c=NCH), AX.X, ALU.add).then_inc(s["t_cnt"], 1)
            v.wait_ge(s["t_int"], 2)
            v.tensor_copy(cf[:, :], ci[:, :]).then_inc(s["t_new"], 1)
            v.tensor_copy(rf[:, :], ri[:, :]).then_inc(s["t_new"], 1)
            v.wait_ge(s["t_new"], 2)
            v.scalar_tensor_tensor(rowid[:, :], cf[:, :], float(D), rf[:, :], ALU.mult, ALU.add).then_inc(s["t_new"], 1)
            v.wait_ge(s["t_new"], 3)
            v.wait_ge(s["t_cnt"], 1)
            v.tensor_tensor(away[:, :], dump[:, :], rowid[:, :], ALU.subtract).then_inc(s["t_new"], 1)
            v.tensor_scalar(cf[:, :], cnt[:, :], 0.5, None, ALU.is_gt).then_inc(s["t_new"], 1)
            v.wait_ge(s["t_new"], 5)
            v.tensor_tensor(rf[:, :], away[:, :], cf[:, :], ALU.mult).then_inc(s["t_new"], 1)
            v.wait_ge(s["t_new"], 6)
            v.tensor_tensor(cf[:, :], rf[:, :], rowid[:, :], ALU.add).then_inc(s["t_new"], 1)
            v.wait_ge(s["t_new"], 7)
            v.tensor_copy(newid[:, :], cf[:, :]).then_inc(s["t_new"], 2)
            v.wait_ge(s["atoms_loaded"], 48)
            v.tensor_reduce(eaw_max[:, :], eaw[:, :], AX.X, ALU.max, negate=True).then_inc(s["t_soft"], 1)
            v.wait_ge(s["t_softact"], 1)
            v.reciprocal(eaw_max[:, :], eaw_sum[:, :]).then_inc(s["t_soft"], 1)
            v.wait_ge(s["t_soft"], 2)
            v.tensor_scalar(eaw_soft[:, :], eaw_exp[:, :], eaw_max[:, 0:1], None, ALU.mult).then_inc(s["t_soft"], 1)
            v.wait_ge(s["t_smt_pe"], 1)
            v.tensor_copy(soft_t[:, :], bank[7][0:A, 0:E]).then_inc(s["t_smt"], 1)
            v.wait_ge(s["t_sigact"], 1)
            v.tensor_scalar(rest[:, :], sig[:, :], 1.0, None, ALU.add).then_inc(s["t_sig"], 1)
            v.wait_ge(s["t_sig"], 1)
            v.reciprocal(imp[:, :], rest[:, :]).then_inc(s["t_sig"], 1)
            v.wait_ge(s["t_sig"], 2)
            v.wait_ge(s["t_dt_pe"], 1)
            v.tensor_tensor(wt[:, :], bank[6][:, 0:NCH * E], imp[:, :], ALU.mult).then_inc(s["t_wt"], 1)
            v.wait_ge(s["t_wt"], 1)
            v.tensor_copy(piece[0][:, :], wt[:, :]).then_inc(s["t_piece"], 1)
            v.wait_ge(s["t_piece"], 1)
            v.tensor_tensor(rest[:, :], wt[:, :], piece[0][:, :], ALU.subtract).then_inc(s["t_piece"], 1)
            v.wait_ge(s["t_piece"], 2)
            v.tensor_copy(piece[1][:, :], rest[:, :]).then_inc(s["t_piece"], 1)
            v.wait_ge(s["t_piece"], 3)
            v.tensor_tensor(wt[:, :], rest[:, :], piece[1][:, :], ALU.subtract).then_inc(s["t_piece"], 1)
            v.wait_ge(s["t_piece"], 4)
            v.tensor_copy(piece[2][:, :], wt[:, :]).then_inc(s["t_piece"], 1)
            v.wait_ge(s["t_sum_pe"], 1)
            v.tensor_copy(vals[:, :], bank[7][:, 0:NCH * E]).then_inc(s["t_vals"], 1)
            v.wait_ge(s["x_rest"], 16)
            v.wait_ge(s["tanh_done"], 1)

            def batch_a(t, ahead):
                if ahead >= 1:
                    sums_a(t.later(1))
                    norm_a(t.later(1))
                    copy_ks(t.later(1), "a_stk_pe", SM[1][:, :].bitcast(F16), "a_ks")
                if ahead >= 2:
                    layer_norm(0, t.later(2))
                output_a(t)

            over_batches(v, batch_a)

            def gates(t):
                G = 10 * t.b
                v.wait_ge(s["b_log_pe"], t.b + 1)
                v.tensor_scalar(l8[:, :], bank[7][:, 0:E], 50.0, -50.0, ALU.min, ALU.max).then_inc(s["b_gate"], 1)
                wait_alone(v, s["b_gate"], G + 1, s)
                v.max(m8[:, :], l8[:, :]).then_inc(s["b_gate"], 1)
                wait_alone(v, s["b_gate"], G + 2, s)
                v.max_index(i8[:, :], m8[:, :], l8[:, :]).then_inc(s["b_gate"], 1)
                v.tensor_tensor(gsm[:, 0:1], m8[:, 1:2], m8[:, 0:1], ALU.subtract).then_inc(s["b_gate"], 1)
                v.wait_ge(s["b_gate"], G + 3)
                v.tensor_copy(i2[:, :], i8[:, 0:2])
                v.wait_ge(s["b_exp"], t.b + 1)
                v.tensor_scalar(gsm[:, 2:3], gsm[:, 1:2], 1.0, None, ALU.add).then_inc(s["b_gate"], 1)
                v.wait_ge(s["b_gate"], G + 5)
                v.reciprocal(gsm[:, 3:4], gsm[:, 2:3]).then_inc(s["b_gate"], 1)
                v.wait_ge(s["b_gate"], G + 6)
                v.tensor_scalar(gsm[:, 4:5], gsm[:, 3:4], tg[:, 2:3], None, ALU.mult).then_inc(s["b_gate"], 1)
                v.wait_ge(s["b_gate"], G + 7)
                v.tensor_scalar(gsm[:, 5:6], gsm[:, 4:5], gsm[:, 1:2], None, ALU.mult).then_inc(s["b_gate"], 1)
                v.tensor_scalar(oh[:, 0, :], iota8[:, :], i2[:, 0:1], gsm[:, 4:5], ALU.is_equal, ALU.mult)
                v.wait_ge(s["b_gate"], G + 8)
                v.tensor_scalar(oh[:, 1, :], iota8[:, :], i2[:, 1:2], gsm[:, 5:6], ALU.is_equal, ALU.mult).then_inc(s["b_gate"], 1)
                v.wait_ge(s["b_gate"], G + 9)
                v.tensor_tensor(gate[t.p][:, :], oh[:, 0, :], oh[:, 1, :], ALU.add).then_inc(s["b_gate"], 1)

            def ternary(t):
                for i, (w, wq, n) in enumerate(((wgu, wgu_q, 512), (wd, wd_q, 256))):
                    src = w[:, bass.ds(t.b * n, n)]
                    tmp = neg[:, 512 * i:512 * i + n]
                    after(v, s["w_tern"], 2 * t.b)
                    v.tensor_scalar(tmp, src, wlim[:, i, 1:2], None, ALU.is_lt).then_inc(s["w_mask"], 1)
                    v.wait_ge(s["w_mask"], 2 * t.b + i + 1)
                    v.scalar_tensor_tensor(wq[:, bass.ds(t.b * n, n)], src, wlim[:, i, 0:1], tmp, ALU.is_gt, ALU.subtract)\
                     .then_inc(s["w_tern"], 1)

            def combine(t, unit):
                v.wait_ge(s["b_y_pe"], 4 * t.b + unit + 1)
                if unit == 0:
                    v.wait_ge(s["b_gate"], 10 * t.b + 10)
                for j in range(2):
                    e = 2 * unit + j
                    v.wait_ge(s["b_y"], 8 * t.b + e + 8)
                    v.scalar_tensor_tensor(row(t), bank[unit][:, j * D:(j + 1) * D], gate[t.p][:, e:e + 1], row(t),
                                           ALU.mult, ALU.add).then_inc(s["b_y"], 1)

            v.sem_inc(s["b_y"], 8)
            v.wait_ge(s["a_x"], B)
            layer_norm(1, t0)
            v.wait_ge(s["w_abs"], 2 * B)
            v.tensor_reduce(wsum[:, :], wabs[:, :, :], AX.X, ALU.add).then_inc(s["w_sum"], 2)
            v.wait_ge(s["w_sum_pe"], 1)
            for i, n in enumerate((2 * FF * D, FF * D)):
                v.tensor_scalar(wscale[:, i:i + 1], bank[5][:, i:i + 1], 1.0 / n, Q_EPS, ALU.mult, ALU.max)\
                 .then_inc(s["w_scale"], 1)
            v.wait_ge(s["w_scale"], 2)
            v.tensor_scalar(wlim[:, :, 0], wscale[:, :], 0.5, None, ALU.mult)
            v.tensor_scalar(wlim[:, :, 1], wscale[:, :], -0.5, None, ALU.mult)
            v.tensor_scalar(wsc127[:, :], wscale[:, :], 1.0 / 127.0, None, ALU.mult).then_inc(s["w_scale"], 1)
            v.wait_ge(s["w_scale"], 3)
            gates(t0)
            v.wait_ge(s["cvec_loaded"], 80)
            v.tensor_tensor(gqk[:, 0, :], gqk[:, 0, :], gqk[:, 1, :], ALU.mult).then_inc(s["c_vec"], 1)
            v.wait_ge(s["c_vec"], 1)
            v.tensor_reduce(gscale[:, 0:1], gqk[:, 0, :], AX.X, ALU.max, apply_absolute_value=True).then_inc(s["c_vec"], 1)
            v.wait_ge(s["c_vec"], 2)
            v.tensor_scalar(gscale[:, 0:1], gscale[:, 0:1], 1e-30, None, ALU.max).then_inc(s["c_vec"], 1)
            v.wait_ge(s["c_vec"], 3)
            v.reciprocal(gscale[:, 1:2], gscale[:, 0:1]).then_inc(s["c_vec"], 1)
            v.tensor_scalar(gscale[:, 2:3], gscale[:, 0:1], float(DH1) ** -0.5, None, ALU.mult)
            v.tensor_scalar(gscale[:, 3:4], gscale[:, 0:1], -float(DH1) ** -0.5, None, ALU.mult)
            v.wait_ge(s["c_vec"], 4)
            v.tensor_scalar(gqk[:, 1, :], gqk[:, 0, :], gscale[:, 1:2], float(D) ** 0.5, ALU.mult, ALU.mult).then_inc(s["c_vec"], 1)
            v.wait_ge(s["c_vec"], 5)

            def batch_b(t, ahead):
                combine(t, 0)
                if ahead >= 1:
                    layer_norm(1, t.later(1))
                combine(t, 1)
                combine(t, 2)
                ternary(t)
                if ahead >= 1:
                    gates(t.later(1))
                combine(t, 3)

            over_batches(v, batch_b)

            def bias_v(t):
                v.wait_ge(s["kv_pe"], B + t.b + 1)
                v.tensor_tensor(strided(vce[t.p][:, 0:], [[64, 8], [48, 2], [1, 16]]),
                                strided(bank[6][:, 0:], [[32, 8], [16, 2], [1, 16]]),
                                strided(bv[:, 0:], [[32, 8], [16, 2], [1, 16]]), ALU.add).then_inc(s["c_vb"], 1)

            def bias_qk(t):
                v.wait_ge(s["kv_pe"], B + t.b + 1)
                v.tensor_tensor(sq[:, :], bank[7][:, :], bqk[:, :], ALU.add).then_inc(s["c_qkb"], 1)

            def norm_c(t):
                v.wait_ge(s["c_rs"], t.b + 1)
                after(v, s["c_lo"], 2 * t.b)
                v.scalar_tensor_tensor(qkn[:, 0:D], sq[:, 0:D], rsc[:, 0:1], gqk[:, 1, :], ALU.mult, ALU.mult)\
                 .then_inc(s["c_norm"], 1)
                v.tensor_scalar(qkn[:, D:2 * D], sq[:, D:2 * D], rsc[:, 1:2], float(D) ** 0.5, ALU.mult, ALU.mult).then_inc(s["c_norm"], 1)

            def maxima(t, step):
                cols = slice(8 * step, 8 * step + 8)
                v.wait_ge(s["c_s_pe"], 2 * t.b + step + 1)
                v.tensor_reduce(mx[:, cols], banks(2 * step).rearrange("p (h m) -> p h m", m=P), AX.X, ALU.max)\
                 .then_inc(s["c_max"], 1)
                v.wait_ge(s["c_max"], 2 * t.b + step + 1)
                after(v, s["c_exp"], 16 * t.b)
                v.tensor_scalar(nb[:, cols], mx[:, cols], gscale[:, 3:4], None, ALU.mult).then_inc(s["c_nb"], 1)

            def copy_pt(t, k):
                v.wait_ge(s["c_pt_pe"], 4 * t.b + k + 1)
                if k == 0:
                    after(v, s["c_pv_pe"], 4 * t.b)
                v.tensor_copy(pts[:, k * 512:(k + 1) * 512], bank[4 + k % 2][:, :]).then_inc(s["c_pt"], 1)

            def output_c(t):
                v.wait_ge(s["c_otok_pe"], t.b + 1)
                v.wait_ge(s["c_rd"], t.b + 1)
                v.tensor_tensor(by_head(on[:, :], H1, DH1), by_head(bank[7][:, 0:D], H1, DH1),
                                rdc[:, :].unsqueeze(2).broadcast_to([P, H1, DH1]), ALU.mult).then_inc(s["c_on"], 1)

            def inverse_den(t):
                v.wait_ge(s["c_exp"], 16 * t.b + 16)
                v.reciprocal(strided(rdc[:, 0:], [[8, 2], [1, 2], [2, 4]]), den[:, :].rearrange("p (s j w) -> p s j w", s=2, j=2))\
                 .then_inc(s["c_rd"], 1)

            def residual_c(t):
                v.wait_ge(s["c_wo_pe"], t.b + 1)
                v.tensor_tensor(wo_out[:, :], bank[7][:, 0:D], bo[:, :], ALU.add).then_inc(s["c_wo"], 1)
                v.wait_ge(s["c_wo"], t.b + 1)
                v.scalar_tensor_tensor(row(t), wo_out[:, :], tg[:, 1:2], row(t), ALU.mult, ALU.add).then_inc(s["c_x"], 1)

            v.wait_ge(s["b_y"], 8 + 8 * B)
            layer_norm(2, t0)
            bias_v(t0)
            bias_qk(t0)
            norm_c(t0)
            layer_norm(2, t1)
            copy_ks(t0, "c_stk_pe", bank[5][:, :].bitcast(F16), "c_ks")

            def batch_c(t, ahead):
                prev = t.later(-1)
                before = not t.first
                if before:
                    output_c(prev)
                maxima(t, 0)
                maxima(t, 1)
                if before:
                    residual_c(prev)
                if ahead >= 1:
                    bias_v(t.later(1))
                    bias_qk(t.later(1))
                copy_pt(t, 0)
                copy_pt(t, 1)
                if ahead >= 1:
                    norm_c(t.later(1))
                copy_pt(t, 2)
                copy_pt(t, 3)
                inverse_den(t)
                if ahead >= 2:
                    layer_norm(2, t.later(2))
                if ahead >= 1:
                    copy_ks(t.later(1), "c_stk_pe", bank[5][:, :].bitcast(F16), "c_ks")

            over_batches(v, batch_c)
            t7 = Tile(3, 1)
            output_c(t7)
            residual_c(t7)

            def quantise(t):
                v.wait_ge(s["ln_xn"], 3 * B + t.b + 1)
                v.tensor_reduce(am[:, :], xn[:, :], AX.X, ALU.max, apply_absolute_value=True).then_inc(s["d_amax"], 1)
                v.wait_ge(s["d_amax"], t.b + 1)
                v.tensor_scalar(ac[:, :], am[:, :], Q_EPS, None, ALU.max).then_inc(s["d_scale"], 1)
                v.wait_ge(s["d_scale"], 4 * t.b + 1)
                v.reciprocal(xsc[:, 0:1], ac[:, :]).then_inc(s["d_scale"], 1)
                v.tensor_scalar(alpha[t.p][:, 0:1], ac[:, :], wsc127[:, 0:1], None, ALU.mult).then_inc(s["d_scale"], 1)
                v.wait_ge(s["d_scale"], 4 * t.b + 3)
                v.tensor_scalar(xsc[:, 1:2], xsc[:, 0:1], 127.0, None, ALU.mult)
                v.tensor_scalar(alpha[t.p][:, 1:2], alpha[t.p][:, 0:1], 0.5, None, ALU.mult)
                v.tensor_scalar(alpha[t.p][:, 2:3], alpha[t.p][:, 0:1], alpha[t.p][:, 0:1], 0.5, ALU.mult, ALU.mult)\
                 .then_inc(s["d_scale"], 1)
                v.wait_ge(s["d_scale"], 4 * t.b + 4)
                v.tensor_scalar(xr[:, :], xn[:, :], xsc[:, 1:2], ROUND, ALU.mult, ALU.add).then_inc(s["d_round"], 1)
                v.wait_ge(s["d_round"], t.b + 1)
                after(v, s["d_xqt_pe"], t.b)
                v.tensor_scalar(xq[:, :], xr[:, :], -ROUND, None, ALU.add).then_inc(s["d_xq"], 1)

            def norm_d(t):
                T = 3 * B + t.b
                v.bn_stats(stats[:, :], row(t)).then_inc(s["ln_stats"], 1)
                wait_alone(v, s["ln_stats"], T + 1, s)
                v.bn_aggr(mv[:, :], stats[:, :]).then_inc(s["ln_mv"], 1)
                v.wait_ge(s["ln_rstd"], T + 1)
                v.tensor_scalar(xn[:, :], row(t), mv[:, 0:1], rstd[:, 0:1], ALU.subtract, ALU.mult)\
                 .then_inc(s["ln_xn"], 1)

            def swiglu(t, h):
                cols = slice(512 * h, 512 * h + 512)
                v.wait_ge(s["d_th"], 2 * t.b + h + 1)
                v.scalar_tensor_tensor(u[:, cols], th[:, cols], 1.0, bank[2 * h + 1][:, :], ALU.add, ALU.mult).then_inc(s["d_u"], 1)
                v.wait_ge(s["d_u"], 2 * t.b + h + 1)
                if h == 0:
                    after(v, s["d_hround"], t.b)
                v.scalar_tensor_tensor(hid[:, cols], bank[2 * h][:, :], alpha[t.p][:, 2:3], u[:, cols], ALU.mult, ALU.mult)\
                 .then_inc(s["d_h"], 1)

            def hidden_scale(t):
                v.wait_ge(s["d_h"], 2 * t.b + 2)
                v.tensor_reduce(hm[:, 0:1], hid, AX.X, ALU.max, apply_absolute_value=True).then_inc(s["d_hmax"], 1)
                v.wait_ge(s["d_hmax"], t.b + 1)
                v.tensor_scalar(hm[:, 1:2], hm[:, 0:1], Q_EPS, None, ALU.max).then_inc(s["d_hscale"], 1)
                v.wait_ge(s["d_hscale"], 3 * t.b + 1)
                v.reciprocal(hm[:, 0:1], hm[:, 1:2]).then_inc(s["d_hscale"], 1)
                v.wait_ge(s["d_hscale"], 3 * t.b + 2)
                v.tensor_scalar(hm[:, 2:3], hm[:, 0:1], 127.0, None, ALU.mult).then_inc(s["d_hscale"], 1)
                v.tensor_scalar(hm[:, 3:4], hm[:, 1:2], wsc127[:, 1:2], tg[:, 3:4], ALU.mult, ALU.mult)\
                 .then_inc(s["d_beta"], 1)

            def output_d(t):
                v.wait_ge(s["d_beta"], t.b + 1)
                v.wait_ge(s["d_down_pe"], t.b + 1)
                v.scalar_tensor_tensor(row(t), bank[6][:, 0:D], hm[:, 3:4], row(t), ALU.mult, ALU.add).then_inc(s["d_out"], 1)

            v.wait_ge(s["c_x"], B)
            norm_d(t0)
            quantise(t0)
            swiglu(t0, 0)
            swiglu(t0, 1)

            def batch_d(t, ahead):
                hidden_scale(t)
                if ahead >= 1:
                    norm_d(t.later(1))
                    quantise(t.later(1))
                    swiglu(t.later(1), 0)
                    swiglu(t.later(1), 1)
                output_d(t)

            over_batches(v, batch_d)


def kernel(**inputs):
    import numpy as np
    from concourse import bacc
    from concourse.bass_utils import run_bass_kernel_spmd

    a = {n: np.asarray(v) for n, v in inputs.items()}
    kv = np.concatenate([a["L0_xattn_Wk"], a["L0_xattn_Wv"]], axis=0)
    arrays = {
        "x": a["x"],
        "ctx_t": a["ctx_2048"].transpose(0, 2, 1),
        "g_xattn": a["g_xattn"],
        "g_ffn": a["g_ffn"],
        "a_wq": a["L0_xattn_Wq"].T,
        "a_wkv": np.concatenate([kv[0::2], kv[1::2]], axis=0).T,
        "b_gate": a["L0_ffn_gate_w"].T,
        "b_w": a["L0_ffn_W"].T,
        "b_atoms": a["L0_ffn_atoms"],
        "b_eaw": a["L0_ffn_expert_atom_weights"],
        "b_imp": a["L0_ffn_importance"].reshape(E, NCH, P).transpose(2, 1, 0).reshape(P, NCH * E),
        "b_idx": a["L0_ffn_mask_idx"],
        "c_wq": a["L1_xattn_Wq"],
        "c_wkv": np.concatenate([a["L1_xattn_Wk_img"], a["L1_xattn_Wv_img"]], axis=1),
        "c_bqk": np.concatenate([a["L1_xattn_bq"], a["L1_xattn_bk_img"]]),
        "c_bv": a["L1_xattn_bv_img"],
        "c_gq": a["L1_xattn_gq"],
        "c_gk": a["L1_xattn_gk_img"],
        "c_wo": a["L1_xattn_Wo"],
        "c_bo": a["L1_xattn_bo"],
        "d_wgu": a["L1_ffn_w_gate_up"].T,
        "d_wd": a["L1_ffn_w_down"].T,
    }
    arrays = {n: np.ascontiguousarray(v) for n, v in arrays.items()}
    nc = bacc.Bacc("TRN2", target_bir_lowering=False, num_devices=1)
    args = [nc.dram_tensor(n, v.shape, mybir.dt.from_np(v.dtype), kind="ExternalInput").ap() for n, v in arrays.items()]
    args.append(nc.dram_tensor("out", (B, N, D), F32, kind="ExternalOutput").ap())
    build(nc, *args)
    r = run_bass_kernel_spmd(nc, [arrays], core_ids=[0])
    return r.results[0]["out"]
```

```python
from contextlib import ExitStack

import concourse.bass as bass
from concourse import mybir

F32 = mybir.dt.float32
F16 = mybir.dt.float16
BF16 = mybir.dt.bfloat16
I32 = mybir.dt.int32
U32 = mybir.dt.uint32
ALU = mybir.AluOpType
ACT = mybir.ActivationFunctionType
AX = mybir.AxisListType

P = 128
B, N, D = 8, 128, 256
KD = D // P
H0, DH0 = 32, 8
H1, DH1 = 16, 16
E, A, NS = 8, 64, 2048
NCH = NS // P
FF = 1024
LN_EPS, RMS_EPS, Q_EPS = 1e-5, 1e-6, 1e-5
ROUND = 1.5 * 2.0 ** 23
ROOT_UNIT = 9 / 64
ROOT, GATE = 10, 10

SEMAPHORES = """
passed const_ready ve_ready x_first x_rest ct_loaded0 ct_loaded1 wa_loaded wkv_loaded small_loaded idx_loaded
atoms_loaded wb_loaded wc_loaded cvec_loaded wgu_loaded wd_loaded tanh_done
ln_stats ln_mv ln_veps ln_rstd ln_xn ln_xt_pe ln_xt
a_qk_pe kv_pe a_sq a_ss a_rs a_qkn a_v a_hi a_lo a_stq_pe a_stk_pe a_qs a_ks
a_s_pe a_exp a_pv_pe a_ot a_otok_pe a_rd a_att a_x
t_eq t_eqm t_cnt t_int t_new t_soft t_softact t_smt_pe t_smt t_dt_pe t_sig t_sigact t_wt
t_piece t_sum_pe t_vals t_zero t_zeroed t_stage t_scattered t_loaded b_table
w_abs w_sum w_sum_pe w_scale w_sign w_mask w_tern
b_log_pe b_gate b_exp b_y_pe b_y
c_vec c_qkb c_vb c_qk_pe c_sq c_sse c_rs c_norm c_hi c_lo c_stq_pe c_stk_pe c_qs c_ks
c_s_pe c_max c_nb c_exp c_pt_pe c_pt c_pv_pe c_ot c_otok_pe c_rd c_on c_ont_pe c_ont c_wo_pe c_wo
c_x
d_amax d_scale d_round d_xq d_xqt_pe d_xqt d_up_pe d_th d_u d_h d_hmax d_hscale d_hround d_hq
d_hqt_pe d_hqt d_down_pe d_beta d_out stored
""".split()


class Tile:

    def __init__(self, pair, parity):
        self.pair, self.p = pair, parity
        self.b = pair * 2 + parity
        self.first = isinstance(pair, int) and self.b == 0

    def later(self, n):
        q = self.p + n
        return Tile(self.pair + q // 2, q % 2)


def over_batches(eng, body):
    body(Tile(0, 0), 2)
    body(Tile(0, 1), 2)
    with eng.Fori(1, B // 2 - 1) as i:
        for p in range(2):
            body(Tile(i, p), 2)
    body(Tile(B // 2 - 1, 0), 1)
    body(Tile(B // 2 - 1, 1), 0)


def after(eng, sem, value):
    if not isinstance(value, int) or value > 0:
        eng.wait_ge(sem, value)


def wait_alone(eng, sem, value, s):
    eng.wait_ge(sem, value)
    eng.sem_inc(s["passed"], 1)


def strided(view, dims):
    return bass.AP(tensor=view.tensor, offset=view.offset, ap=[list(view.ap[0])] + [list(d) for d in dims])


def spread(dram, n):
    return bass.AP(tensor=dram.tensor, offset=dram.offset, ap=[[0, P], [1, n]])


def build(nc, x, ctx_t, g_xattn, g_ffn, a_wq, a_wkv, b_gate, b_w, b_atoms, b_eaw, b_imp, b_idx,
          c_wq, c_wkv, c_bqk, c_bv, c_gq, c_gk, c_wo, c_bo, d_wgu, d_wd, out):
    stack = ExitStack()
    with stack:
        def sb(name, shape, dt=F32):
            return stack.enter_context(nc.sbuf_tensor(name, shape, dt))

        s = {n: stack.enter_context(nc.semaphore(n)) for n in SEMAPHORES}
        pair = [stack.enter_context(nc.psum_tensor(f"banks{2 * i}_{2 * i + 1}", [P, 1024], F32)) for i in range(4)]
        bank = [pair[i // 2][:, (i % 2) * 512:(i % 2 + 1) * 512] for i in range(8)]

        def banks(first):
            return pair[first // 2][:, :]

        X = sb("X", [P, B, D])
        id32 = sb("id32", [P, P])
        id16 = sb("id16", [P, P], F16)
        idbf = sb("idbf", [P, P], BF16)
        ones = sb("ones", [P, P])
        below = sb("below", [P, P], BF16)
        neghalf = sb("neghalf", [P, 2])
        eps = sb("eps", [P, 2])
        iota8 = sb("iota8", [P, 8])
        dump = sb("dump", [P, NCH])
        gains = sb("gains", [P, 4])
        tg = sb("tg", [P, 4])
        stats = sb("stats", [P, 6])
        mv = sb("mv", [P, 2])
        veps = sb("veps", [P, 1])
        rstd = sb("rstd", [P, 1])
        xn = sb("xn", [P, D])
        xt = [sb(f"xt{p}", [P, KD, P]) for p in range(2)]
        ct = [sb(f"ct{p}", [P, KD, P]) for p in range(2)]
        wqa = sb("wqa", [P, KD, D])
        wkva = sb("wkva", [P, KD, 2 * D])
        sq = sb("sq", [P, 2 * D])
        ss = sb("ss", [P, 2 * H0])
        rs = sb("rs", [P, 2 * H0])
        root = [sb(f"root{i}", [P, 2 * H0]) for i in range(2)]
        qkn = sb("qkn", [P, 2 * D])
        stq = sb("stq", [P, 4 * D], F16)
        stk = sb("stk", [P, 4 * D], F16)
        qs = [sb(f"qs{p}", [P, 8, P], F16) for p in range(2)]
        ks = [sb(f"ks{p}", [P, 8, P], F16) for p in range(2)]
        ve = [sb(f"ve{p}", [P, H0 * 32]) for p in range(2)]
        probs = [sb(f"probs{h}", [P, 16 * P]) for h in range(2)]
        ots = sb("ots", [P, 3 * P])
        rd = sb("rd", [P, H0])
        att = sb("att", [P, D])
        table = sb("table", [P, KD * D * E])
        idx_col = sb("idx_col", [P, NCH], I32)
        same = sb("same", [P, NS], BF16)
        same_below = sb("same_below", [P, NS], BF16)
        ci = sb("ci", [P, NCH], I32)
        ri = sb("ri", [P, NCH], I32)
        cf = sb("cf", [P, NCH])
        rf = sb("rf", [P, NCH])
        rowid = sb("rowid", [P, NCH])
        cnt = sb("cnt", [P, NCH])
        away = sb("away", [P, NCH])
        newid = sb("newid", [P, NCH], U32)
        atoms = sb("atoms", [A, NS])
        eaw = sb("eaw", [E, A])
        eaw_max = sb("eaw_max", [E, 1])
        eaw_exp = sb("eaw_exp", [E, A])
        eaw_sum = sb("eaw_sum", [E, 1])
        eaw_soft = sb("eaw_soft", [E, A])
        soft_t = sb("soft_t", [A, E])
        imp = sb("imp", [P, NCH * E])
        sig = sb("sig", [P, NCH * E])
        wt = sb("wt", [P, NCH * E])
        rest = sb("rest", [P, NCH * E])
        piece = [sb(f"piece{i}", [P, NCH * E], BF16) for i in range(3)]
        vals = sb("vals", [P, NCH * E])
        stage_idx = sb("stage_idx", [P, 1], U32)
        stage_val = sb("stage_val", [P, E])
        wb = sb("wb", [P, KD, D])
        gw = sb("gw", [P, KD, E])
        dw = sb("dw", [P, KD, E, D])
        idx_row = dw[:, 0, :, :].rearrange("p e r -> p (e r)").bitcast(I32)
        l8 = sb("l8", [P, E])
        m8 = sb("m8", [P, 8])
        i8 = sb("i8", [P, 8], U32)
        i2 = sb("i2", [P, 2])
        gsm = sb("gsm", [P, 8])
        oh = sb("oh", [P, 2, E])
        gate = [sb(f"gate{p}", [P, E]) for p in range(2)]
        wqc = sb("wqc", [P, KD, D])
        wkvc = sb("wkvc", [P, KD, 2 * D])
        woc = sb("woc", [P, KD, D])
        bqk = sb("bqk", [P, 2 * D])
        bv = sb("bv", [P, D])
        bo = sb("bo", [P, D])
        gqk = sb("gqk", [P, 2, D])
        gscale = sb("gscale", [P, 4])
        ssc = sb("ssc", [P, 2])
        ssce = sb("ssce", [P, 2])
        rsc = sb("rsc", [P, 2])
        vce = [sb(f"vce{p}", [P, H1 * 32]) for p in range(2)]
        mx = sb("mx", [P, H1])
        nb = sb("nb", [P, H1])
        den = [sb(f"den{p}", [P, H1]) for p in range(2)]
        pc, pts = probs
        otc = sb("otc", [P, D])
        rdc = sb("rdc", [P, H1])
        on = sb("on", [P, D])
        ont = sb("ont", [P, KD, P])
        wo_out = sb("wo_out", [P, D])
        wgu = sb("wgu", [P, KD * 2 * FF])
        wd = sb("wd", [P, 8 * D])
        wgu_q = sb("wgu_q", [P, KD * 2 * FF], BF16)
        wd_q = sb("wd_q", [P, 8 * D], BF16)
        neg = sb("neg", [P, 768], BF16)
        sgn = sb("sgn", [P, 768], BF16)
        junk = sb("junk", [P, 768])
        wabs = sb("wabs", [P, 2, B])
        wsum = sb("wsum", [P, 2])
        wscale = sb("wscale", [P, 2])
        wlim = sb("wlim", [P, 2, 2])
        wsc127 = sb("wsc127", [P, 2])
        am = sb("am", [P, 1])
        ac = sb("ac", [P, 1])
        xsc = sb("xsc", [P, 2])
        alpha = [sb(f"alpha{p}", [P, 4]) for p in range(2)]
        xr = sb("xr", [P, D])
        xq = sb("xq", [P, D], BF16)
        xqt = [sb(f"xqt{p}", [P, KD, P], BF16) for p in range(2)]
        th, u, hid, hr = (table[:, i * FF:(i + 1) * FF] for i in range(4))
        hm = sb("hm", [P, 4])
        hq = sb("hq", [P, FF], BF16)
        hqt = sb("hqt", [P, 8, P], BF16)

        scratch = nc.dram_tensor("delta_table", (D * D + P, E), F32, kind="Internal").ap()

        STA, XVA, OTA, QKA = bank[4:8]

        block = stack.enter_context(nc.Block())

        @block.sync
        def _(sp):
            sp.dma_start(X[:, 0:2, :], x[0:2].rearrange("b n d -> n b d")).then_inc(s["x_first"], 16)
            sp.dma_start(wqa[:, :, :], a_wq.rearrange("(k p) o -> p k o", p=P)).then_inc(s["wa_loaded"], 16)

            def load_ct(t, stage):
                after(sp, s["kv_pe"], stage * B + t.b - 1)
                sp.dma_start(ct[t.p][:, :, :], ctx_t[t.b].rearrange("(k p) m -> p k m", p=P))\
                  .then_inc(s[f"ct_loaded{t.p}"], 16)

            load_ct(Tile(0, 0), 0)
            sp.dma_start(wkva[:, :, :], a_wkv.rearrange("(k p) o -> p k o", p=P)).then_inc(s["wkv_loaded"], 16)
            load_ct(Tile(0, 1), 0)
            sp.dma_start(X[:, 2:B, :], x[2:B].rearrange("b n d -> n b d")).then_inc(s["x_rest"], 16)
            load_ct(Tile(1, 0), 0)
            sp.wait_ge(s["t_zero"], 1)
            sp.dma_start(scratch[0:D * D, :].rearrange("(p n) e -> p (n e)", p=P), table[:, :]).then_inc(s["t_zeroed"], 16)
            sp.dma_start(scratch[D * D:D * D + P, :], table[:, 0:E]).then_inc(s["t_zeroed"], 16)
            sp.dma_start(wgu[:, :].rearrange("p (k o) -> p k o", k=KD), d_wgu.rearrange("(k p) o -> p k o", p=P)).then_inc(s["wgu_loaded"], 16)
            load_ct(Tile(1, 1), 0)
            sp.dma_start(wd[:, :].rearrange("p (k o) -> p k o", k=8), d_wd.rearrange("(k p) o -> p k o", p=P)).then_inc(s["wd_loaded"], 16)
            sp.dma_start(wb[:, :, :], b_w.rearrange("(k p) o -> p k o", p=P)).then_inc(s["wb_loaded"], 16)
            sp.dma_start(gw[:, :, :], b_gate.rearrange("(k p) o -> p k o", p=P)).then_inc(s["wb_loaded"], 16)
            sp.dma_start(wqc[:, :, :], c_wq.rearrange("(k p) o -> p k o", p=P)).then_inc(s["wc_loaded"], 16)
            sp.dma_start(wkvc[:, :, :], c_wkv.rearrange("(k p) o -> p k o", p=P)).then_inc(s["wc_loaded"], 16)
            sp.dma_start(woc[:, :, :], c_wo.rearrange("(k p) o -> p k o", p=P)).then_inc(s["wc_loaded"], 16)
            sp.dma_start(bqk[:, :], spread(c_bqk, 2 * D)).then_inc(s["cvec_loaded"], 16)
            sp.dma_start(bv[:, :], spread(c_bv, D)).then_inc(s["cvec_loaded"], 16)
            sp.dma_start(bo[:, :], spread(c_bo, D)).then_inc(s["cvec_loaded"], 16)
            sp.dma_start(gqk[:, 0, :], spread(c_gq, D)).then_inc(s["cvec_loaded"], 16)
            sp.dma_start(gqk[:, 1, :], spread(c_gk, D)).then_inc(s["cvec_loaded"], 16)
            with sp.Fori(2, B // 2) as i:
                for p in range(2):
                    load_ct(Tile(i, p), 0)
            sp.wait_ge(s["t_scattered"], 16 * NCH)
            sp.dma_start(table[:, :].rearrange("p (k n) -> p k n", k=KD),
                         scratch[0:D * D, :].rearrange("(k p n) e -> p k (n e)", p=P, k=KD)).then_inc(s["t_loaded"], 16)
            with sp.Fori(0, B // 2) as i:
                for p in range(2):
                    load_ct(Tile(i, p), 1)
            with sp.Fori(0, B) as b:
                sp.wait_ge(s["d_out"], b + 1)
                sp.dma_start(out[b], X[:, b, :]).then_inc(s["stored"], 16)
            sp.wait_ge(s["stored"], 16 * B)

        @block.gpsimd
        def _(gp):
            gp.memset(id32[:, :], 0.0).then_inc(s["const_ready"], 1)
            gp.memset(ones[:, :], 1.0).then_inc(s["const_ready"], 1)
            gp.wait_ge(s["const_ready"], 2)
            gp.affine_select(out=id32[:, :], in_=id32[:, :], compare_op=ALU.not_equal, fill=1.0, base=0,
                             pattern=[[-1, P]], channel_multiplier=1).then_inc(s["const_ready"], 1)
            gp.memset(neghalf[:, :], -0.5)
            gp.memset(eps[:, 0:1], LN_EPS)
            gp.memset(eps[:, 1:2], D * RMS_EPS).then_inc(s["const_ready"], 1)
            gp.wait_ge(s["const_ready"], 4)
            gp.tensor_copy(id16[:, :], id32[:, :]).then_inc(s["const_ready"], 1)
            gp.tensor_copy(idbf[:, :], id32[:, :]).then_inc(s["const_ready"], 1)

            def ln_rstd(stage, t):
                T = stage * B + t.b
                gp.wait_ge(s["ln_mv"], T + 1)
                gp.tensor_tensor(veps[:, :], mv[:, 1:2], eps[:, 0:1], ALU.add).then_inc(s["ln_veps"], 1)
                gp.wait_ge(s["ln_veps"], T + 1)
                gp.tensor_tensor(rstd[:, :], veps[:, :], neghalf[:, 0:1], ALU.pow).then_inc(s["ln_rstd"], 1)

            def low_parts(t, hi, norm, done, width):
                reps = D // width
                q3 = qkn[:, 0:D].rearrange("p (h d) -> p h d", d=width).unsqueeze(2).broadcast_to([P, reps, 2, width])
                k3 = qkn[:, D:2 * D].rearrange("p (h d) -> p h d", d=width).unsqueeze(2).broadcast_to([P, reps, 2, width])
                q4 = stq[:, :].rearrange("p (h r d) -> p h r d", r=4, d=width)
                k4 = stk[:, :].rearrange("p (h r d) -> p h r d", r=4, d=width)
                gp.wait_ge(s[hi], 2 * t.b + 1)
                gp.tensor_tensor(q4[:, :, 2:4, :], q3, q4[:, :, 0:2, :], ALU.subtract).then_inc(s[done], 1)
                gp.wait_ge(s[hi], 2 * t.b + 2)
                gp.tensor_tensor(k4[:, :, 1:4:2, :], k3, k4[:, :, 0:3:2, :], ALU.subtract).then_inc(s[done], 1)

            def scatter(j):
                after(gp, s["t_scattered"], 16 * j)
                gp.tensor_copy(stage_idx[:, :], newid[:, bass.ds(j, 1)])
                gp.tensor_copy(stage_val[:, :], vals[:, bass.ds(j * E, E)]).then_inc(s["t_stage"], 1)
                wait_alone(gp, s["t_stage"], j + 1, s)
                gp.indirect_dma_start(out=scratch, out_offset=bass.IndirectOffsetOnAxis(ap=stage_idx[:, 0:1], axis=0),
                                      in_=stage_val[:, :], in_offset=None, compute_op=ALU.add)\
                  .then_inc(s["t_scattered"], 16)

            ln_rstd(0, Tile(0, 0))
            ln_rstd(0, Tile(0, 1))
            gp.iota(iota8[:, :], pattern=[[1, 8]], base=0, channel_multiplier=0, allow_small_or_imprecise_dtypes=True)
            gp.iota(dump[:, :], pattern=[[0, NCH]], base=D * D, channel_multiplier=1, allow_small_or_imprecise_dtypes=True)
            gp.memset(below[:, :], 0.0).then_inc(s["const_ready"], 1)
            gp.wait_ge(s["const_ready"], 7)
            gp.affine_select(out=below[:, :], in_=below[:, :], compare_op=ALU.is_gt, fill=1.0, base=1,
                             pattern=[[1, P]], channel_multiplier=-1).then_inc(s["const_ready"], 1)
            gp.memset(table[:, :], 0.0).then_inc(s["t_zero"], 1)
            low_parts(Tile(0, 0), "a_hi", "a_qkn", "a_lo", DH0)
            gp.memset(vce[0][:, :], 0.0)
            gp.memset(vce[1][:, :], 0.0).then_inc(s["const_ready"], 1)

            def batch_a(t, ahead):
                chunk = 3 * t.b - 2
                if ahead >= 2:
                    ln_rstd(0, t.later(2))
                    if not t.first:
                        scatter(chunk)
                if ahead >= 1:
                    low_parts(t.later(1), "a_hi", "a_qkn", "a_lo", DH0)
                if t.first:
                    gp.wait_ge(s["t_new"], 9)
                    gp.wait_ge(s["t_vals"], 1)
                    gp.wait_ge(s["t_zeroed"], 32)
                    scatter(0)
                elif ahead >= 2:
                    scatter(chunk + 1)
                    scatter(chunk + 2)

            over_batches(gp, batch_a)

            ln_rstd(1, Tile(0, 0))

            def batch_b(t, ahead):
                if ahead >= 1:
                    ln_rstd(1, t.later(1))

            over_batches(gp, batch_b)

            def rms_c(t):
                gp.wait_ge(s["c_sq"], 2 * t.b + 2)
                gp.tensor_tensor(ssce[:, :], ssc[:, :], eps[:, 1:2].broadcast_to([P, 2]), ALU.add).then_inc(s["c_sse"], 1)
                gp.wait_ge(s["c_sse"], t.b + 1)
                gp.tensor_tensor(rsc[:, :], ssce[:, :], neghalf[:, 0:2], ALU.pow).then_inc(s["c_rs"], 1)

            ln_rstd(2, Tile(0, 0))
            rms_c(Tile(0, 0))
            ln_rstd(2, Tile(0, 1))
            low_parts(Tile(0, 0), "c_hi", "c_norm", "c_lo", DH1)
            rms_c(Tile(0, 1))
            low_parts(Tile(0, 1), "c_hi", "c_norm", "c_lo", DH1)

            def batch_c(t, ahead):
                if ahead >= 2:
                    ln_rstd(2, t.later(2))
                    rms_c(t.later(2))
                    low_parts(t.later(2), "c_hi", "c_norm", "c_lo", DH1)

            over_batches(gp, batch_c)

            ln_rstd(3, Tile(0, 0))
            ln_rstd(3, Tile(0, 1))

            def batch_d(t, ahead):
                wait_alone(gp, s["d_hscale"], 3 * t.b + 3, s)
                gp.tensor_scalar(hr, hid, hm[:, 2:3], ROUND, ALU.mult, ALU.add).then_inc(s["d_hround"], 1)
                if ahead >= 2:
                    ln_rstd(3, t.later(2))

            over_batches(gp, batch_d)

        @block.scalar
        def _(act):
            act.dma_start(eaw[:, :], b_eaw).then_inc(s["atoms_loaded"], 16)
            act.dma_start(atoms[:, :], b_atoms).then_inc(s["atoms_loaded"], 16)
            act.dma_start(imp[:, :], b_imp).then_inc(s["atoms_loaded"], 16)
            act.dma_start(idx_col[:, :], b_idx.rearrange("(c p) -> p c", p=P), allow_slow_non_contiguous=True).then_inc(s["idx_loaded"], 16)
            act.dma_start(idx_row, spread(b_idx, NS)).then_inc(s["idx_loaded"], 16)
            act.dma_start(gains[:, 0:2], spread(g_xattn, 2)).then_inc(s["small_loaded"], 16)
            act.dma_start(gains[:, 2:4], spread(g_ffn, 2)).then_inc(s["small_loaded"], 16)
            def copy_xt(stage, t, src):
                act.wait_ge(s["ln_xt_pe"], stage * B + t.b + 1)
                act.activation(xt[t.p][:, :, :].rearrange("p k n -> p (k n)"), src, ACT.Copy)\
                   .then_inc(s["ln_xt"], 1)

            def square_a(t):
                act.wait_ge(s["a_qk_pe"], t.b + 1)
                after(act, s["a_ss"], t.b)
                act.activation(sq[:, :], QKA[:, :], ACT.Square).then_inc(s["a_sq"], 1)

            def copy_v_a(t):
                act.wait_ge(s["kv_pe"], t.b + 1)
                after(act, s["a_pv_pe"], 2 * t.b - 2)
                for R, nr in ((0, 3), (1, 3), (2, 2)):
                    src = strided(XVA[:, 96 * R:], [[32, nr], [8, 4], [1, 8]])
                    dst = strided(ve[t.p][:, 384 * R:], [[137, nr], [32, 4], [1, 8]])
                    last = act.activation(dst, src, ACT.Copy)
                last.then_inc(s["a_v"], 1)

            def high_parts(t, ready, width, used, done):
                reps = D // width
                act.wait_ge(s[ready[0]], ready[1])
                after(act, s[used], t.b)
                for half, dst in ((0, stq[:, :].rearrange("p (h r d) -> p h r d", r=4, d=width)[:, :, 0:2, :]),
                                  (1, stk[:, :].rearrange("p (h r d) -> p h r d", r=4, d=width)[:, :, 0:3:2, :])):
                    src = qkn[:, half * D:(half + 1) * D].rearrange("p (h d) -> p h d", d=width)
                    act.activation(dst, src.unsqueeze(2).broadcast_to([P, reps, 2, width]), ACT.Copy)\
                       .then_inc(s[done], 1)

            def copy_qs(t, ready, src, done):
                act.wait_ge(s[ready], t.b + 1)
                act.activation(qs[t.p][:, :, :].rearrange("p w n -> p (w n)"), src, ACT.Copy).then_inc(s[done], 1)

            def exp_a(t, step):
                half, pair = step // 2, step % 2
                act.wait_ge(s["a_s_pe"], 4 * t.b + step + 1)
                act.activation(probs[half][:, pair * 1024:(pair + 1) * 1024], banks(2 * pair), ACT.Exp,
                               scale=float(DH0) ** 0.5 * ROOT_UNIT ** 2).then_inc(s["a_exp"], 1)

            def copy_ot(t):
                act.wait_ge(s["a_pv_pe"], 2 * t.b + 2)
                after(act, s["a_otok_pe"], t.b)
                act.activation(ots[:, :], OTA[:, 0:384], ACT.Copy).then_inc(s["a_ot"], 1)

            t0, t1 = Tile(0, 0), Tile(0, 1)
            copy_xt(0, t0, XVA[:, 0:256])
            act.wait_ge(s["t_soft"], 1)
            act.activation(eaw_exp[:, :], eaw[:, :], ACT.Exp, bias=eaw_max[:, 0:1], accum_out=eaw_sum[:, 0:1])\
               .then_inc(s["t_softact"], 1)
            act.activation(sig[:, :], imp[:, :], ACT.Exp, scale=-1.0).then_inc(s["t_sigact"], 1)
            square_a(t0)
            act.wait_ge(s["ve_ready"], 3)
            copy_v_a(t0)
            high_parts(t0, ("a_qkn", 1), DH0, "a_stk_pe", "a_hi")
            copy_xt(0, t1, XVA[:, 0:256])
            act.wait_ge(s["small_loaded"], 32)
            act.activation(tg[:, :], gains[:, :], ACT.Tanh).then_inc(s["tanh_done"], 1)
            copy_qs(t0, "a_stq_pe", STA[:, :].bitcast(F16), "a_qs")
            square_a(t1)

            def batch_a(t, ahead):
                exp_a(t, 0)
                if ahead >= 1:
                    high_parts(t.later(1), ("a_qkn", t.later(1).b + 1), DH0, "a_stk_pe", "a_hi")
                if not t.first:
                    copy_ot(t.later(-1))
                if ahead >= 1:
                    copy_v_a(t.later(1))
                exp_a(t, 1)
                exp_a(t, 2)
                if ahead >= 2:
                    copy_xt(0, t.later(2), XVA[:, 0:256])
                exp_a(t, 3)
                if ahead >= 1:
                    copy_qs(t.later(1), "a_stq_pe", STA[:, :].bitcast(F16), "a_qs")
                if t.first:
                    act.wait_ge(s["wgu_loaded"], 16)
                    act.wait_ge(s["wd_loaded"], 16)
                after(act, s["w_abs"], 2 * t.b)
                act.activation(junk[:, 0:512], wgu[:, bass.ds(t.b * 512, 512)], ACT.Abs, accum_out=wabs[:, 0, bass.ds(t.b, 1)])\
                   .then_inc(s["w_abs"], 1)
                act.activation(junk[:, 512:768], wd[:, bass.ds(t.b * 256, 256)], ACT.Abs, accum_out=wabs[:, 1, bass.ds(t.b, 1)])\
                   .then_inc(s["w_abs"], 1)
                if ahead >= 2:
                    square_a(t.later(2))

            over_batches(act, batch_a)
            copy_ot(Tile(3, 1))

            def gate_exp(t):
                act.wait_ge(s["b_gate"], GATE * t.b + 3)
                act.activation(gsm[:, 1:2], gsm[:, 0:1], ACT.Exp).then_inc(s["b_exp"], 1)

            copy_xt(1, t0, bank[6][:, 0:256])
            gate_exp(t0)

            def below_mask(t):
                act.wait_ge(s["w_tern"], 2 * t.b + 1)
                for i, (w, n) in enumerate(((wgu, 512), (wd, 256))):
                    at = slice(512 * i, 512 * i + n)
                    act.activation(sgn[:, at], w[:, bass.ds(t.b * n, n)], ACT.Sign, bias=wlim[:, i, 0:1]).then_inc(s["w_sign"], 1)
                    act.wait_ge(s["w_sign"], 2 * t.b + i + 1)
                    act.activation(neg[:, at], sgn[:, at], ACT.Relu, scale=-1.0).then_inc(s["w_mask"], 1)

            act.wait_ge(s["w_scale"], 5)

            def batch_b(t, ahead):
                if ahead >= 1:
                    copy_xt(1, t.later(1), bank[6][:, 0:256])
                below_mask(t)
                if ahead >= 1:
                    gate_exp(t.later(1))

            over_batches(act, batch_b)

            def square_c(t):
                act.wait_ge(s["c_qkb"], t.b + 1)
                after(act, s["c_sq"], 2 * t.b)
                for i in range(2):
                    act.activation(junk[:, i * D:(i + 1) * D], qkn_raw[:, i * D:(i + 1) * D], ACT.Square,
                                   accum_out=ssc[:, i:i + 1]).then_inc(s["c_sq"], 1)

            qkn_raw = sq

            def exp_c(t, k):
                act.wait_ge(s["c_nb"], 2 * t.b + k // 2 + 1)
                after(act, s["c_pt_pe"], 4 * t.b - 3 + k)
                for i in range(4):
                    at = 4 * k + i
                    act.activation(pc[:, at * P:(at + 1) * P], bank[k][:, i * P:(i + 1) * P],
                                   ACT.Exp, bias=nb[:, at:at + 1], scale=gscale[:, 2:3],
                                   accum_out=den[t.p][:, at:at + 1]).then_inc(s["c_exp"], 1)

            def copy_ont(t):
                act.wait_ge(s["c_ont_pe"], t.b + 1)
                act.activation(ont[:, :, :].rearrange("p k n -> p (k n)"), bank[7][:, 0:256], ACT.Copy)\
                   .then_inc(s["c_ont"], 1)

            def copy_otc(t):
                act.wait_ge(s["c_pv_pe"], 4 * t.b + 4)
                after(act, s["c_otok_pe"], t.b)
                act.activation(otc[:, :], bank[6][:, 0:256], ACT.Copy).then_inc(s["c_ot"], 1)

            copy_xt(2, t0, bank[7][:, 0:256])
            square_c(t0)
            copy_xt(2, t1, bank[7][:, 0:256])
            high_parts(t0, ("c_norm", 2), DH1, "c_stk_pe", "c_hi")
            copy_qs(t0, "c_stq_pe", bank[4][:, :].bitcast(F16), "c_qs")
            square_c(t1)
            high_parts(t1, ("c_norm", 4), DH1, "c_stk_pe", "c_hi")

            def batch_c(t, ahead):
                exp_c(t, 0)
                if not t.first:
                    copy_otc(t.later(-1))
                exp_c(t, 1)
                if ahead >= 1:
                    copy_qs(t.later(1), "c_stq_pe", bank[4][:, :].bitcast(F16), "c_qs")
                if ahead >= 2:
                    copy_xt(2, t.later(2), bank[7][:, 0:256])
                exp_c(t, 2)
                if ahead >= 2:
                    square_c(t.later(2))
                exp_c(t, 3)
                if not t.first:
                    copy_ont(t.later(-1))
                if ahead >= 2:
                    high_parts(t.later(2), ("c_norm", 2 * t.later(2).b + 2), DH1, "c_stk_pe", "c_hi")

            over_batches(act, batch_c)
            copy_otc(Tile(3, 1))
            copy_ont(Tile(3, 1))

            def copy_xqt(t):
                act.wait_ge(s["d_xqt_pe"], t.b + 1)
                act.activation(xqt[t.p][:, :, :].rearrange("p k n -> p (k n)"), bank[4][:, :].bitcast(BF16)[:, 0:256],
                               ACT.Copy).then_inc(s["d_xqt"], 1)

            def tanh_d(t, h):
                act.wait_ge(s["d_up_pe"], 2 * t.b + h + 1)
                if h == 0:
                    after(act, s["d_u"], 2 * t.b)
                act.activation(th[:, h * 512:(h + 1) * 512], bank[2 * h][:, :], ACT.Tanh, scale=alpha[t.p][:, 1:2])\
                   .then_inc(s["d_th"], 1)

            def ints_d(t):
                act.wait_ge(s["d_hround"], t.b + 1)
                after(act, s["d_hqt_pe"], t.b)
                act.activation(hq[:, :], hr, ACT.Copy, bias=-ROUND).then_inc(s["d_hq"], 1)

            def copy_hqt(t):
                act.wait_ge(s["d_hqt_pe"], t.b + 1)
                after(act, s["d_down_pe"], t.b)
                act.activation(hqt[:, :, :].rearrange("p k n -> p (k n)"), bank[5][:, :].bitcast(BF16), ACT.Copy)\
                   .then_inc(s["d_hqt"], 1)

            copy_xqt(t0)
            tanh_d(t0, 0)
            tanh_d(t0, 1)
            copy_xqt(t1)

            def batch_d(t, ahead):
                if ahead >= 1:
                    tanh_d(t.later(1), 0)
                ints_d(t)
                if ahead >= 1:
                    tanh_d(t.later(1), 1)
                copy_hqt(t)
                if ahead >= 2:
                    copy_xqt(t.later(2))

            over_batches(act, batch_d)

        @block.tensor
        def _(pe):
            mm, tr = nc.tensor.matmul, nc.tensor.transpose
            t0, t1 = Tile(0, 0), Tile(0, 1)

            def turn_xn(stage, t, dst):
                pe.wait_ge(s["ln_xn"], stage * B + t.b + 1)
                for k in range(KD):
                    last = tr(dst[:, k * P:(k + 1) * P], xn[:, k * P:(k + 1) * P], id32[:, :])
                last.then_inc(s["ln_xt_pe"], 1)

            def project(dst, lhs, rhs):
                for k in range(KD):
                    last = mm(dst, lhs[:, k, :], rhs(k), start=(k == 0), stop=(k == KD - 1))
                return last

            def xn_a(t):
                after(pe, s["a_v"], t.b)
                turn_xn(0, t, XVA)

            def qkv_a(t):
                pe.wait_ge(s["ln_xt"], t.b + 1)
                after(pe, s["a_qkn"], t.b)
                project(QKA[:, 0:D], xt[t.p], lambda k: wqa[:, k, :])
                pe.wait_ge(s[f"ct_loaded{t.p}"], t.pair * 16 + 16)
                project(QKA[:, D:2 * D], ct[t.p], lambda k: wkva[:, k, 0:D]).then_inc(s["a_qk_pe"], 1)
                project(XVA[:, 0:D], ct[t.p], lambda k: wkva[:, k, D:2 * D]).then_inc(s["kv_pe"], 1)

            def turn_stack(src, dst, name):
                for w in range(8):
                    last = tr(dst[:, :].bitcast(F16)[:, w * P:(w + 1) * P], src[:, w * P:(w + 1) * P], id16[:, :])
                last.then_inc(s[name], 1)

            def stacks_a(t):
                pe.wait_ge(s["a_lo"], 2 * t.b + 1)
                after(pe, s["a_ks"], t.b)
                turn_stack(stq, STA, "a_stq_pe")
                pe.wait_ge(s["a_lo"], 2 * t.b + 2)
                pe.wait_ge(s["a_qs"], t.b + 1)
                turn_stack(stk, STA, "a_stk_pe")

            def scores_a(t, step):
                half, pair = step // 2, step % 2
                if step == 0:
                    pe.wait_ge(s["a_qs"], t.b + 1)
                    pe.wait_ge(s["a_ks"], t.b + 1)
                after(pe, s["a_exp"], 4 * t.b + step - 1)
                for g in range(4):
                    for j in range(2):
                        h4 = 2 * pair + j
                        rows = slice(32 * h4, 32 * h4 + 32)
                        last = mm(bank[h4][:, g * P:(g + 1) * P], ks[t.p][rows, 4 * half + g, :],
                                  qs[t.p][rows, 4 * half + g, :], start=True, stop=True)
                last.then_inc(s["a_s_pe"], 1)

            def pv_a(t, half):
                pe.wait_ge(s["a_exp"], 4 * t.b + 2 * half + 2)
                if half == 0:
                    if t.first:
                        pe.wait_ge(s["t_wt"], 1)
                    after(pe, s["a_att"], t.b)
                for g in range(4):
                    v = 4 * half + g
                    for h4 in range(4):
                        h = 4 * v + h4
                        last = mm(OTA[32 * h4:32 * h4 + 32, (v // 3) * P:(v // 3 + 1) * P], ve[t.p][:, 32 * h:32 * h + 32],
                                  probs[half][:, (4 * h4 + g) * P:(4 * h4 + g + 1) * P],
                                  start=(v % 3 == 0), stop=(v % 3 == 2 or v == 7))
                last.then_inc(s["a_pv_pe"], 1)

            def turn_out_a(t):
                pe.wait_ge(s["a_ot"], t.b + 1)
                for R in range(3):
                    last = tr(OTA[:, R * P:(R + 1) * P], ots[:, R * P:(R + 1) * P], id32[:, :])
                last.then_inc(s["a_otok_pe"], 1)

            pe.wait_ge(s["const_ready"], 3)
            xn_a(t0)
            pe.wait_ge(s["wa_loaded"], 16)
            pe.wait_ge(s["wkv_loaded"], 16)
            qkv_a(t0)
            pe.wait_ge(s["t_soft"], 3)
            tr(OTA[0:A, 256:256 + E], eaw_soft[:, :], id32[0:E, 0:E]).then_inc(s["t_smt_pe"], 1)
            pe.wait_ge(s["t_smt"], 1)
            pe.wait_ge(s["atoms_loaded"], 48)
            for c in range(NCH):
                last = mm(OTA[:, c * E:(c + 1) * E], atoms[:, c * P:(c + 1) * P], soft_t[:, :], start=True, stop=True)
            last.then_inc(s["t_dt_pe"], 1)
            xn_a(t1)
            pe.wait_ge(s["const_ready"], 6)
            stacks_a(t0)
            qkv_a(t1)
            scores_a(t0, 0)
            scores_a(t0, 1)

            def total_positions():
                pe.wait_ge(s["t_piece"], 5)
                pe.wait_ge(s["a_ks"], 2)
                for c in range(NCH):
                    for i in range(3):
                        last = mm(STA[:, c * E:(c + 1) * E], same[:, c * P:(c + 1) * P], piece[i][:, c * E:(c + 1) * E],
                                  start=(i == 0), stop=(i == 2))
                last.then_inc(s["t_sum_pe"], 1)

            def batch_a(t, ahead):
                scores_a(t, 2)
                if not t.first:
                    turn_out_a(t.later(-1))
                if ahead >= 2:
                    xn_a(t.later(2))
                scores_a(t, 3)
                pv_a(t, 0)
                if isinstance(t.b, int) and t.b == 1:
                    pe.wait_ge(s["t_vals"], 1)
                if ahead >= 1:
                    stacks_a(t.later(1))
                if ahead >= 2:
                    qkv_a(t.later(2))
                if ahead >= 1:
                    scores_a(t.later(1), 0)
                    scores_a(t.later(1), 1)
                pv_a(t, 1)
                if t.first:
                    total_positions()

            over_batches(pe, batch_a)
            turn_out_a(Tile(3, 1))

            def logits(t):
                pe.wait_ge(s["ln_xt"], B + t.b + 1)
                after(pe, s["b_gate"], GATE * t.b)
                project(bank[7][:, 0:E], xt[t.p], lambda k: gw[:, k, :]).then_inc(s["b_log_pe"], 1)

            def xn_b(t):
                pe.wait_ge(s["ln_xt"], B + t.b)
                turn_xn(1, t, bank[6])

            def experts(t, unit):
                pe.wait_ge(s["b_y"], 8 * t.b + 2 * unit + 2)
                for k in range(KD):
                    last = mm(bank[unit][:, :], xt[t.p][:, k, :],
                              dw[:, k, 2 * unit:2 * unit + 2, :].rearrange("p e r -> p (e r)"), start=(k == 0), stop=(k == KD - 1))
                last.then_inc(s["b_y_pe"], 1)

            pe.wait_ge(s["a_att"], B)
            xn_b(t0)
            pe.wait_ge(s["w_sum"], 2)
            mm(bank[5][:, 0:2], ones[:, :], wsum[:, :], start=True, stop=True).then_inc(s["w_sum_pe"], 1)
            pe.wait_ge(s["wb_loaded"], 32)
            logits(t0)
            pe.wait_ge(s["b_table"], 2 * KD)

            def batch_b(t, ahead):
                experts(t, 0)
                experts(t, 1)
                if ahead >= 1:
                    xn_b(t.later(1))
                experts(t, 2)
                if ahead >= 1:
                    logits(t.later(1))
                experts(t, 3)

            over_batches(pe, batch_b)

            def xn_c(t):
                after(pe, s["c_wo"], t.b - 3)
                after(pe, s["c_qkb"], t.b)
                turn_xn(2, t, bank[7])

            def v_c(t):
                pe.wait_ge(s[f"ct_loaded{t.p}"], 16 * (B // 2) + t.pair * 16 + 16)
                after(pe, s["c_ot"], t.b - 1)
                project(bank[6][:, 0:D], ct[t.p], lambda k: wkvc[:, k, D:2 * D]).then_inc(s["kv_pe"], 1)

            def qk_c(t):
                pe.wait_ge(s["ln_xt"], 2 * B + t.b + 1)
                project(bank[7][:, 0:D], xt[t.p], lambda k: wqc[:, k, :])
                pe.wait_ge(s[f"ct_loaded{t.p}"], 16 * (B // 2) + t.pair * 16 + 16)
                project(bank[7][:, D:2 * D], ct[t.p], lambda k: wkvc[:, k, 0:D]).then_inc(s["c_qk_pe"], 1)

            def stacks_c(t):
                pe.wait_ge(s["c_lo"], 2 * t.b + 2)
                after(pe, s["c_pt"], 4 * t.b - 4)
                turn_stack(stq, bank[4], "c_stq_pe")
                turn_stack(stk, bank[5], "c_stk_pe")

            def scores_c(t, step):
                if step == 0:
                    pe.wait_ge(s["c_qs"], t.b + 1)
                    pe.wait_ge(s["c_ks"], t.b + 1)
                after(pe, s["c_exp"], 16 * t.b - 8 + 8 * step)
                for w4 in range(4):
                    for j in range(2):
                        rows = slice(64 * j, 64 * j + 64)
                        w = 4 * step + w4
                        last = mm(bank[2 * step + j][:, w4 * P:(w4 + 1) * P], qs[t.p][rows, w, :], ks[t.p][rows, w, :],
                                  start=True, stop=True)
                last.then_inc(s["c_s_pe"], 1)

            def turn_probs(t, k):
                pe.wait_ge(s["c_exp"], 16 * t.b + 4 * k + 4)
                if k < 2:
                    nxt = min(t.b + 2, B) if isinstance(t.b, int) else t.b + 2
                    pe.wait_ge(s["c_qs" if k == 0 else "c_ks"], nxt)
                    after(pe, s["c_pt"], 4 * t.b)
                if k >= 2:
                    pe.wait_ge(s["c_pt"], 4 * t.b + k - 1)
                for i in range(4):
                    at = 4 * k + i
                    last = tr(bank[4 + k % 2][:, i * P:(i + 1) * P], pc[:, at * P:(at + 1) * P], id32[:, :])
                last.then_inc(s["c_pt_pe"], 1)

            def pv_c(t, k):
                step, j = k // 2, k % 2
                pe.wait_ge(s["c_pt"], 4 * t.b + k + 1)
                if k == 0:
                    pe.wait_ge(s["c_vb"], min(t.b + 2, B) if isinstance(t.b, int) else t.b + 2)
                    after(pe, s["c_ot"], t.b)
                for w4 in range(4):
                    h = 2 * (4 * step + w4) + j
                    last = mm(bank[6][32 * w4:32 * w4 + 32, step * P:(step + 1) * P], vce[t.p][:, 32 * h:32 * h + 32],
                              pts[:, (4 * k + w4) * P:(4 * k + w4 + 1) * P], start=(j == 0), stop=(j == 1))
                last.then_inc(s["c_pv_pe"], 1)

            def turn_out_c(t):
                pe.wait_ge(s["c_ot"], t.b + 1)
                after(pe, s["c_wo"], t.b)
                pe.wait_ge(s["c_qkb"], min(t.b + 4, B) if isinstance(t.b, int) else t.b + 4)
                for k in range(KD):
                    last = tr(bank[7][:, k * P:(k + 1) * P], otc[:, k * P:(k + 1) * P], id32[:, :])
                last.then_inc(s["c_otok_pe"], 1)

            def turn_on(t):
                pe.wait_ge(s["c_on"], t.b + 1)
                for k in range(KD):
                    last = tr(bank[7][:, k * P:(k + 1) * P], on[:, k * P:(k + 1) * P], id32[:, :])
                last.then_inc(s["c_ont_pe"], 1)

            def out_c(t):
                pe.wait_ge(s["c_ont"], t.b + 1)
                project(bank[7][:, 0:D], ont, lambda k: woc[:, k, :]).then_inc(s["c_wo_pe"], 1)

            pe.wait_ge(s["b_gate"], GATE * B)
            pe.wait_ge(s["b_y"], 8 * B + 8)
            pe.wait_ge(s["ln_xt"], 2 * B)
            pe.wait_ge(s["wc_loaded"], 48)
            xn_c(t0)
            qk_c(t0)
            v_c(t0)
            xn_c(t1)
            pe.wait_ge(s["w_scale"], 3)
            stacks_c(t0)
            qk_c(t1)
            scores_c(t0, 0)
            scores_c(t0, 1)

            def batch_c(t, ahead):
                prev, nxt = t.later(-1), t.later(1)
                if ahead >= 1:
                    stacks_c(nxt)
                    v_c(nxt)
                if ahead >= 2:
                    xn_c(t.later(2))
                turn_probs(t, 0)
                if ahead >= 2:
                    qk_c(t.later(2))
                turn_probs(t, 1)
                pv_c(t, 0)
                pv_c(t, 1)
                if ahead >= 1:
                    scores_c(nxt, 0)
                if not t.first:
                    turn_out_c(prev)
                turn_probs(t, 2)
                if not t.first:
                    turn_on(prev)
                pv_c(t, 2)
                turn_probs(t, 3)
                pv_c(t, 3)
                if ahead >= 1:
                    scores_c(nxt, 1)
                if not t.first:
                    out_c(prev)

            over_batches(pe, batch_c)
            t7 = Tile(3, 1)
            turn_out_c(t7)
            turn_on(t7)
            out_c(t7)

            def turn_xq(t):
                pe.wait_ge(s["d_xq"], t.b + 1)
                after(pe, s["d_xqt"], t.b)
                for k in range(KD):
                    last = tr(bank[4][:, :].bitcast(BF16)[:, k * P:(k + 1) * P], xq[:, k * P:(k + 1) * P], idbf[:, :])
                last.then_inc(s["d_xqt_pe"], 1)

            def up(t):
                pe.wait_ge(s["d_xqt"], t.b + 1)
                for h in range(2):
                    after(pe, s["d_h"], 2 * t.b + h - 1)
                    for part in range(2):
                        for k in range(KD):
                            at = k * 2 * FF + part * FF + h * 512
                            last = mm(bank[2 * h + part][:, :], xqt[t.p][:, k, :], wgu_q[:, at:at + 512],
                                      start=(k == 0), stop=(k == KD - 1))
                    last.then_inc(s["d_up_pe"], 1)

            def turn_hq(t):
                pe.wait_ge(s["d_hq"], t.b + 1)
                after(pe, s["d_hqt"], t.b)
                for k in range(8):
                    last = tr(bank[5][:, :].bitcast(BF16)[:, k * P:(k + 1) * P], hq[:, k * P:(k + 1) * P], idbf[:, :])
                last.then_inc(s["d_hqt_pe"], 1)

            def down(t):
                pe.wait_ge(s["d_hqt"], t.b + 1)
                after(pe, s["d_out"], t.b)
                for k in range(8):
                    last = mm(bank[6][:, 0:D], hqt[:, k, :], wd_q[:, k * D:(k + 1) * D], start=(k == 0), stop=(k == 7))
                last.then_inc(s["d_down_pe"], 1)

            pe.wait_ge(s["c_wo"], B)
            pe.wait_ge(s["w_tern"], 2 * B + 1)
            turn_xq(t0)
            up(t0)
            turn_xq(t1)

            def batch_d(t, ahead):
                if ahead >= 1:
                    up(t.later(1))
                turn_hq(t)
                if ahead >= 2:
                    turn_xq(t.later(2))
                down(t)

            over_batches(pe, batch_d)

        @block.vector
        def _(v):
            t0, t1 = Tile(0, 0), Tile(0, 1)

            def row(t):
                return X[:, bass.ds(t.b, 1), :].rearrange("p a d -> p (a d)")

            def layer_norm(stage, t):
                T = stage * B + t.b
                v.bn_stats(stats[:, :], row(t)).then_inc(s["ln_stats"], 1)
                wait_alone(v, s["ln_stats"], T + 1, s)
                v.bn_aggr(mv[:, :], stats[:, :]).then_inc(s["ln_mv"], 1)
                v.wait_ge(s["ln_rstd"], T + 1)
                after(v, s["ln_xt_pe"], T)
                v.tensor_scalar(xn[:, :], row(t), mv[:, 0:1], rstd[:, 0:1], ALU.subtract, ALU.mult)\
                 .then_inc(s["ln_xn"], 1)

            def by_head(view, h, d):
                return view.rearrange("p (h d) -> p h d", d=d)

            def sums_a(t):
                v.wait_ge(s["a_sq"], t.b + 1)
                v.tensor_reduce(ss[:, :], by_head(sq[:, :], 2 * H0, DH0), AX.X, ALU.add).then_inc(s["a_ss"], 1)

            def root_a(t):
                R = ROOT * t.b
                a, h, other = root[0][:, :], rs[:, :], root[1][:, :]
                y = ss[:, :]
                v.wait_ge(s["a_ss"], t.b + 1)
                v.tensor_scalar(a, ss[:, :], float(DH0) * RMS_EPS, None, ALU.add).then_inc(s["a_rs"], 1)
                v.wait_ge(s["a_rs"], R + 1)
                v.tensor_scalar(y.bitcast(I32), a.bitcast(I32), -0.5, float(0x5F3759DF), ALU.mult, ALU.add).then_inc(s["a_rs"], 1)
                for i in range(2):
                    v.wait_ge(s["a_rs"], R + 4 * i + 2)
                    v.scalar_tensor_tensor(h, y, ROOT_UNIT if i else 1.0, y, ALU.mult, ALU.mult).then_inc(s["a_rs"], 1)
                    v.wait_ge(s["a_rs"], R + 4 * i + 3)
                    v.tensor_tensor(other, h, a, ALU.mult).then_inc(s["a_rs"], 1)
                    v.wait_ge(s["a_rs"], R + 4 * i + 4)
                    v.scalar_tensor_tensor(h, other, -10.0 / 3.0, other, ALU.add, ALU.mult).then_inc(s["a_rs"], 1)
                    v.wait_ge(s["a_rs"], R + 4 * i + 5)
                    v.scalar_tensor_tensor(h if i else other, h, 5.0, y, ALU.add, ALU.mult).then_inc(s["a_rs"], 1)
                    y, other = other, y

            def norm_a(t):
                root_a(t)
                v.wait_ge(s["a_rs"], ROOT * t.b + ROOT)
                after(v, s["a_lo"], 2 * t.b)
                v.tensor_tensor(by_head(qkn[:, :], 2 * H0, DH0), by_head(QKA[:, :], 2 * H0, DH0),
                                rs[:, :].unsqueeze(2).broadcast_to([P, 2 * H0, DH0]), ALU.mult).then_inc(s["a_qkn"], 1)

            def copy_ks(t, ready, src, done):
                v.wait_ge(s[ready], t.b + 1)
                v.tensor_copy(ks[t.p][:, :, :].rearrange("p w n -> p (w n)"), src).then_inc(s[done], 1)

            def output_a(t):
                v.wait_ge(s["a_otok_pe"], t.b + 1)
                v.reciprocal(strided(rd[:, 0:], [[12, 2], [1, 4], [4, 3]]),
                             strided(OTA[:, 8:], [[128, 2], [32, 4], [9, 3]]))
                v.reciprocal(strided(rd[:, 24:], [[1, 4], [4, 2]]),
                             strided(OTA[:, 264:], [[32, 4], [9, 2]])).then_inc(s["a_rd"], 1)
                v.wait_ge(s["a_rd"], t.b + 1)
                for R, nr in ((0, 3), (1, 3), (2, 2)):
                    last = v.tensor_tensor(strided(att[:, 96 * R:], [[32, nr], [8, 4], [1, 8]]),
                                           strided(OTA[:, 128 * R:], [[9, nr], [32, 4], [1, 8]]),
                                           strided(rd[:, 12 * R:], [[4, nr], [1, 4], [0, 8]]), ALU.mult)
                last.then_inc(s["a_att"], 1)
                v.wait_ge(s["a_att"], t.b + 1)
                v.scalar_tensor_tensor(row(t), att[:, :], tg[:, 0:1], row(t), ALU.mult, ALU.add).then_inc(s["a_x"], 1)

            v.memset(ve[0][:, :], 0.0).then_inc(s["ve_ready"], 1)
            v.memset(ve[1][:, :], 0.0).then_inc(s["ve_ready"], 1)
            v.wait_ge(s["ve_ready"], 2)
            for p in range(2):
                for R, nr in ((0, 3), (1, 3), (2, 2)):
                    last = v.memset(strided(ve[p][:, 384 * R + 8:], [[137, nr], [32, 4]]), 1.0)
            last.then_inc(s["ve_ready"], 1)

            def softmax_of_atoms():
                v.wait_ge(s["atoms_loaded"], 48)
                v.tensor_reduce(eaw_max[:, :], eaw[:, :], AX.X, ALU.max, negate=True).then_inc(s["t_soft"], 1)
                v.wait_ge(s["t_softact"], 1)
                v.reciprocal(eaw_max[:, :], eaw_sum[:, :]).then_inc(s["t_soft"], 1)
                v.wait_ge(s["t_soft"], 2)
                v.tensor_scalar(eaw_soft[:, :], eaw_exp[:, :], eaw_max[:, 0:1], None, ALU.mult).then_inc(s["t_soft"], 1)
                v.wait_ge(s["t_smt_pe"], 1)
                v.tensor_copy(soft_t[:, :], OTA[0:A, 256:256 + E]).then_inc(s["t_smt"], 1)

            def sigmoid():
                v.wait_ge(s["t_sigact"], 1)
                v.tensor_scalar(rest[:, :], sig[:, :], 1.0, None, ALU.add).then_inc(s["t_sig"], 1)
                v.wait_ge(s["t_sig"], 1)
                v.reciprocal(imp[:, :], rest[:, :]).then_inc(s["t_sig"], 1)

            def compare_positions():
                v.wait_ge(s["idx_loaded"], 32)
                v.tensor_tensor(same[:, :].rearrange("p (c n) -> p c n", c=NCH), idx_row.rearrange("p (c n) -> p c n", c=NCH),
                                idx_col[:, :].unsqueeze(2).broadcast_to([P, NCH, P]), ALU.is_equal).then_inc(s["t_eq"], 1)
                v.tensor_scalar(ci[:, :], idx_col[:, :], D - 1, None, ALU.bitwise_and).then_inc(s["t_int"], 1)
                v.tensor_scalar(ri[:, :], idx_col[:, :], 8, None, ALU.logical_shift_right).then_inc(s["t_int"], 1)
                v.wait_ge(s["t_int"], 2)
                v.tensor_copy(cf[:, :], ci[:, :]).then_inc(s["t_new"], 1)
                v.tensor_copy(rf[:, :], ri[:, :]).then_inc(s["t_new"], 1)
                v.wait_ge(s["t_new"], 2)
                v.scalar_tensor_tensor(rowid[:, :], cf[:, :], float(D), rf[:, :], ALU.mult, ALU.add).then_inc(s["t_new"], 1)

            def weighted_values():
                v.wait_ge(s["t_sig"], 2)
                v.wait_ge(s["t_dt_pe"], 1)
                v.tensor_tensor(wt[:, :], OTA[:, 0:NCH * E], imp[:, :], ALU.mult).then_inc(s["t_wt"], 1)
                v.wait_ge(s["t_wt"], 1)
                v.tensor_copy(piece[0][:, :], wt[:, :]).then_inc(s["t_piece"], 1)
                v.wait_ge(s["t_piece"], 1)
                v.tensor_tensor(rest[:, :], wt[:, :], piece[0][:, :], ALU.subtract).then_inc(s["t_piece"], 1)
                v.wait_ge(s["t_piece"], 2)
                v.tensor_copy(piece[1][:, :], rest[:, :]).then_inc(s["t_piece"], 1)
                v.wait_ge(s["t_piece"], 3)
                v.tensor_tensor(wt[:, :], rest[:, :], piece[1][:, :], ALU.subtract).then_inc(s["t_piece"], 1)
                v.wait_ge(s["t_piece"], 4)
                v.tensor_copy(piece[2][:, :], wt[:, :]).then_inc(s["t_piece"], 1)

            def number_rows():
                v.wait_ge(s["const_ready"], 8)
                v.wait_ge(s["t_eq"], 1)
                v.tensor_tensor(same_below[:, :].rearrange("p (c n) -> p c n", c=NCH), same[:, :].rearrange("p (c n) -> p c n", c=NCH),
                                below[:, :].unsqueeze(1).broadcast_to([P, NCH, P]), ALU.mult).then_inc(s["t_eqm"], 1)
                v.wait_ge(s["t_eqm"], 1)
                v.tensor_reduce(cnt[:, :], same_below[:, :].rearrange("p (c n) -> p c n", c=NCH), AX.X, ALU.add).then_inc(s["t_cnt"], 1)
                v.wait_ge(s["t_new"], 3)
                v.wait_ge(s["t_cnt"], 1)
                v.tensor_tensor(away[:, :], dump[:, :], rowid[:, :], ALU.subtract).then_inc(s["t_new"], 1)
                v.tensor_scalar(cf[:, :], cnt[:, :], 0.5, None, ALU.is_gt).then_inc(s["t_new"], 1)
                v.wait_ge(s["t_new"], 5)
                v.tensor_tensor(rf[:, :], away[:, :], cf[:, :], ALU.mult).then_inc(s["t_new"], 1)
                v.wait_ge(s["t_new"], 6)
                v.tensor_tensor(cf[:, :], rf[:, :], rowid[:, :], ALU.add).then_inc(s["t_new"], 1)
                v.wait_ge(s["t_new"], 7)
                v.tensor_copy(newid[:, :], cf[:, :]).then_inc(s["t_new"], 2)

            def merge_table(k, half):
                if (k, half) == (0, 0):
                    v.wait_ge(s["t_loaded"], 16)
                    v.wait_ge(s["wb_loaded"], 32)
                by_e = table[:, k * D * E:(k + 1) * D * E].rearrange("p (r e) -> p e r", e=E)
                of = slice(half * E // 2, (half + 1) * E // 2)
                v.tensor_tensor(dw[:, k, of, :], by_e[:, of, :], wb[:, k, :].unsqueeze(1).broadcast_to([P, E // 2, D]),
                                ALU.add).then_inc(s["b_table"], 1)

            v.wait_ge(s["x_first"], 16)
            layer_norm(0, t0)
            layer_norm(0, t1)
            softmax_of_atoms()
            sums_a(t0)
            norm_a(t0)
            sigmoid()
            compare_positions()
            copy_ks(t0, "a_stk_pe", STA[:, :].bitcast(F16), "a_ks")
            weighted_values()
            sums_a(t1)
            norm_a(t1)
            v.wait_ge(s["x_rest"], 16)
            v.wait_ge(s["tanh_done"], 1)

            def batch_a(t, ahead):
                if ahead >= 2:
                    layer_norm(0, t.later(2))
                if t.first:
                    number_rows()
                else:
                    output_a(t.later(-1))
                if ahead >= 1:
                    copy_ks(t.later(1), "a_stk_pe", STA[:, :].bitcast(F16), "a_ks")
                if ahead >= 2:
                    sums_a(t.later(2))
                    norm_a(t.later(2))
                if t.first:
                    v.wait_ge(s["t_sum_pe"], 1)
                    v.tensor_copy(vals[:, :], STA[:, 0:NCH * E]).then_inc(s["t_vals"], 1)
                if ahead < 2:
                    merge_table(1 - ahead, 0)
                    merge_table(1 - ahead, 1)

            over_batches(v, batch_a)
            output_a(Tile(3, 1))

            def choose(t):
                G = GATE * t.b
                v.wait_ge(s["b_log_pe"], t.b + 1)
                v.tensor_scalar(l8[:, :], bank[7][:, 0:E], 50.0, -50.0, ALU.min, ALU.max).then_inc(s["b_gate"], 1)
                wait_alone(v, s["b_gate"], G + 1, s)
                v.max(m8[:, :], l8[:, :]).then_inc(s["b_gate"], 1)
                wait_alone(v, s["b_gate"], G + 2, s)
                v.tensor_tensor(gsm[:, 0:1], m8[:, 1:2], m8[:, 0:1], ALU.subtract).then_inc(s["b_gate"], 1)
                v.max_index(i8[:, :], m8[:, :], l8[:, :]).then_inc(s["b_gate"], 1)

            def gates(t):
                G = GATE * t.b
                v.wait_ge(s["b_exp"], t.b + 1)
                v.tensor_scalar(gsm[:, 2:3], gsm[:, 1:2], 1.0, None, ALU.add).then_inc(s["b_gate"], 1)
                v.wait_ge(s["b_gate"], G + 4)
                v.tensor_copy(i2[:, :], i8[:, 0:2]).then_inc(s["b_gate"], 1)
                v.wait_ge(s["b_gate"], G + 5)
                v.reciprocal(gsm[:, 3:4], gsm[:, 2:3]).then_inc(s["b_gate"], 1)
                v.wait_ge(s["b_gate"], G + 6)
                v.tensor_scalar(oh[:, 1, :], iota8[:, :], i2[:, 1:2], gsm[:, 1:2], ALU.is_equal, ALU.mult).then_inc(s["b_gate"], 1)
                v.wait_ge(s["b_gate"], G + 8)
                v.scalar_tensor_tensor(oh[:, 0, :], iota8[:, :], i2[:, 0:1], oh[:, 1, :], ALU.is_equal, ALU.add).then_inc(s["b_gate"], 1)
                v.wait_ge(s["b_gate"], G + 9)
                v.tensor_scalar(gate[t.p][:, :], oh[:, 0, :], gsm[:, 3:4], tg[:, 2:3], ALU.mult, ALU.mult).then_inc(s["b_gate"], 1)

            def ternary(t):
                for i, (w, wq, n) in enumerate(((wgu, wgu_q, 512), (wd, wd_q, 256))):
                    v.wait_ge(s["w_mask"], 2 * t.b + i + 1)
                    v.scalar_tensor_tensor(wq[:, bass.ds(t.b * n, n)], w[:, bass.ds(t.b * n, n)], wlim[:, i, 0:1],
                                           neg[:, 512 * i:512 * i + n], ALU.is_gt, ALU.subtract).then_inc(s["w_tern"], 1)

            def combine(t, unit):
                v.wait_ge(s["b_y_pe"], 4 * t.b + unit + 1)
                if unit == 0:
                    v.wait_ge(s["b_gate"], GATE * t.b + GATE)
                for j in range(2):
                    e = 2 * unit + j
                    v.wait_ge(s["b_y"], 8 * t.b + e + 8)
                    v.scalar_tensor_tensor(row(t), bank[unit][:, j * D:(j + 1) * D], gate[t.p][:, e:e + 1], row(t),
                                           ALU.mult, ALU.add).then_inc(s["b_y"], 1)

            v.sem_inc(s["b_y"], 8)
            v.wait_ge(s["a_x"], B)
            layer_norm(1, t0)
            v.wait_ge(s["w_abs"], 2 * B)
            v.tensor_reduce(wsum[:, :], wabs[:, :, :], AX.X, ALU.add).then_inc(s["w_sum"], 2)
            v.wait_ge(s["w_sum_pe"], 1)
            for i, n in enumerate((2 * FF * D, FF * D)):
                v.tensor_scalar(wscale[:, i:i + 1], bank[5][:, i:i + 1], 1.0 / n, Q_EPS, ALU.mult, ALU.max)\
                 .then_inc(s["w_scale"], 1)
            v.wait_ge(s["w_scale"], 2)
            v.tensor_scalar(wlim[:, :, 0], wscale[:, :], 0.5, None, ALU.mult)
            v.tensor_scalar(wlim[:, :, 1], wscale[:, :], -0.5, None, ALU.mult)
            v.tensor_scalar(wsc127[:, :], wscale[:, :], 1.0 / 127.0, None, ALU.mult).then_inc(s["w_scale"], 3)
            v.wait_ge(s["w_scale"], 5)
            v.sem_inc(s["w_tern"], 1)
            choose(t0)
            gates(t0)
            v.wait_ge(s["cvec_loaded"], 80)
            v.tensor_tensor(gqk[:, 0, :], gqk[:, 0, :], gqk[:, 1, :], ALU.mult).then_inc(s["c_vec"], 1)
            v.wait_ge(s["c_vec"], 1)
            v.tensor_reduce(gscale[:, 0:1], gqk[:, 0, :], AX.X, ALU.max, apply_absolute_value=True).then_inc(s["c_vec"], 1)
            v.wait_ge(s["c_vec"], 2)
            v.tensor_scalar(gscale[:, 0:1], gscale[:, 0:1], 1e-30, None, ALU.max).then_inc(s["c_vec"], 1)
            v.wait_ge(s["c_vec"], 3)
            v.reciprocal(gscale[:, 1:2], gscale[:, 0:1]).then_inc(s["c_vec"], 1)
            v.tensor_scalar(gscale[:, 2:3], gscale[:, 0:1], float(DH1) ** -0.5, None, ALU.mult)
            v.tensor_scalar(gscale[:, 3:4], gscale[:, 0:1], -float(DH1) ** -0.5, None, ALU.mult)
            v.wait_ge(s["c_vec"], 4)
            v.tensor_scalar(gqk[:, 1, :], gqk[:, 0, :], gscale[:, 1:2], float(D) ** 0.5, ALU.mult, ALU.mult).then_inc(s["c_vec"], 1)
            v.wait_ge(s["c_vec"], 5)

            def batch_b(t, ahead):
                if ahead >= 1:
                    layer_norm(1, t.later(1))
                combine(t, 0)
                combine(t, 1)
                ternary(t)
                combine(t, 2)
                if ahead >= 1:
                    choose(t.later(1))
                combine(t, 3)
                if ahead >= 1:
                    gates(t.later(1))

            over_batches(v, batch_b)

            def bias_v(t):
                v.wait_ge(s["kv_pe"], B + t.b + 1)
                v.tensor_tensor(strided(vce[t.p][:, 0:], [[64, 8], [48, 2], [1, 16]]),
                                strided(bank[6][:, 0:], [[32, 8], [16, 2], [1, 16]]),
                                strided(bv[:, 0:], [[32, 8], [16, 2], [1, 16]]), ALU.add).then_inc(s["c_vb"], 1)

            def bias_qk(t):
                v.wait_ge(s["c_qk_pe"], t.b + 1)
                v.tensor_tensor(sq[:, :], bank[7][:, :], bqk[:, :], ALU.add).then_inc(s["c_qkb"], 1)

            def norm_c(t):
                v.wait_ge(s["c_rs"], t.b + 1)
                after(v, s["c_lo"], 2 * t.b)
                v.scalar_tensor_tensor(qkn[:, 0:D], sq[:, 0:D], rsc[:, 0:1], gqk[:, 1, :], ALU.mult, ALU.mult)\
                 .then_inc(s["c_norm"], 1)
                v.tensor_scalar(qkn[:, D:2 * D], sq[:, D:2 * D], rsc[:, 1:2], float(D) ** 0.5, ALU.mult, ALU.mult).then_inc(s["c_norm"], 1)

            def maxima(t, step):
                cols = slice(8 * step, 8 * step + 8)
                v.wait_ge(s["c_s_pe"], 2 * t.b + step + 1)
                v.tensor_reduce(mx[:, cols], banks(2 * step).rearrange("p (h m) -> p h m", m=P), AX.X, ALU.max)\
                 .then_inc(s["c_max"], 1)
                v.wait_ge(s["c_max"], 2 * t.b + step + 1)
                after(v, s["c_exp"], 16 * t.b - 8 + 8 * step)
                v.tensor_scalar(nb[:, cols], mx[:, cols], gscale[:, 3:4], None, ALU.mult).then_inc(s["c_nb"], 1)

            def copy_pt(t, k):
                v.wait_ge(s["c_pt_pe"], 4 * t.b + k + 1)
                if k == 0:
                    after(v, s["c_pv_pe"], 4 * t.b)
                v.tensor_copy(pts[:, k * 512:(k + 1) * 512], bank[4 + k % 2][:, :]).then_inc(s["c_pt"], 1)

            def output_c(t):
                v.wait_ge(s["c_otok_pe"], t.b + 1)
                v.wait_ge(s["c_rd"], t.b + 1)
                v.tensor_tensor(by_head(on[:, :], H1, DH1), by_head(bank[7][:, 0:D], H1, DH1),
                                rdc[:, :].unsqueeze(2).broadcast_to([P, H1, DH1]), ALU.mult).then_inc(s["c_on"], 1)

            def inverse_den(t):
                v.wait_ge(s["c_exp"], 16 * t.b + 16)
                v.reciprocal(strided(rdc[:, 0:], [[8, 2], [1, 2], [2, 4]]), den[t.p][:, :].rearrange("p (s j w) -> p s j w", s=2, j=2))\
                 .then_inc(s["c_rd"], 1)

            def residual_c(t):
                v.wait_ge(s["c_wo_pe"], t.b + 1)
                v.tensor_tensor(wo_out[:, :], bank[7][:, 0:D], bo[:, :], ALU.add).then_inc(s["c_wo"], 1)
                v.wait_ge(s["c_wo"], t.b + 1)
                v.scalar_tensor_tensor(row(t), wo_out[:, :], tg[:, 1:2], row(t), ALU.mult, ALU.add).then_inc(s["c_x"], 1)

            def copy_ks_c(t):
                copy_ks(t, "c_stk_pe", bank[5][:, :].bitcast(F16), "c_ks")

            v.wait_ge(s["b_y"], 8 + 8 * B)
            layer_norm(2, t0)
            v.wait_ge(s["const_ready"], 9)
            bias_v(t0)
            bias_qk(t0)
            layer_norm(2, t1)
            norm_c(t0)
            copy_ks_c(t0)
            bias_qk(t1)
            norm_c(t1)
            maxima(t0, 0)
            maxima(t0, 1)

            def batch_c(t, ahead):
                prev, nxt = t.later(-1), t.later(1)
                if ahead >= 1:
                    copy_ks_c(nxt)
                if ahead >= 2:
                    layer_norm(2, t.later(2))
                if ahead >= 1:
                    bias_v(nxt)
                copy_pt(t, 0)
                if ahead >= 2:
                    bias_qk(t.later(2))
                copy_pt(t, 1)
                if ahead >= 1:
                    maxima(nxt, 0)
                if not t.first:
                    output_c(prev)
                if ahead >= 2:
                    norm_c(t.later(2))
                copy_pt(t, 2)
                copy_pt(t, 3)
                inverse_den(t)
                if ahead >= 1:
                    maxima(nxt, 1)
                if not t.first:
                    residual_c(prev)

            over_batches(v, batch_c)
            t7 = Tile(3, 1)
            output_c(t7)
            residual_c(t7)

            def quantise(t):
                v.wait_ge(s["ln_xn"], 3 * B + t.b + 1)
                v.tensor_reduce(am[:, :], xn[:, :], AX.X, ALU.max, apply_absolute_value=True).then_inc(s["d_amax"], 1)
                v.wait_ge(s["d_amax"], t.b + 1)
                v.tensor_scalar(ac[:, :], am[:, :], Q_EPS, None, ALU.max).then_inc(s["d_scale"], 1)
                v.wait_ge(s["d_scale"], 4 * t.b + 1)
                v.reciprocal(xsc[:, 0:1], ac[:, :]).then_inc(s["d_scale"], 1)
                v.tensor_scalar(alpha[t.p][:, 0:1], ac[:, :], wsc127[:, 0:1], None, ALU.mult).then_inc(s["d_scale"], 1)
                v.wait_ge(s["d_scale"], 4 * t.b + 3)
                v.tensor_scalar(xsc[:, 1:2], xsc[:, 0:1], 127.0, None, ALU.mult)
                v.tensor_scalar(alpha[t.p][:, 1:2], alpha[t.p][:, 0:1], 0.5, None, ALU.mult)
                v.tensor_scalar(alpha[t.p][:, 2:3], alpha[t.p][:, 0:1], alpha[t.p][:, 0:1], 0.5, ALU.mult, ALU.mult)\
                 .then_inc(s["d_scale"], 1)
                v.wait_ge(s["d_scale"], 4 * t.b + 4)
                v.tensor_scalar(xr[:, :], xn[:, :], xsc[:, 1:2], ROUND, ALU.mult, ALU.add).then_inc(s["d_round"], 1)
                v.wait_ge(s["d_round"], t.b + 1)
                after(v, s["d_xqt_pe"], t.b)
                v.tensor_scalar(xq[:, :], xr[:, :], -ROUND, None, ALU.add).then_inc(s["d_xq"], 1)

            def norm_d(t):
                T = 3 * B + t.b
                v.bn_stats(stats[:, :], row(t)).then_inc(s["ln_stats"], 1)
                wait_alone(v, s["ln_stats"], T + 1, s)
                v.bn_aggr(mv[:, :], stats[:, :]).then_inc(s["ln_mv"], 1)
                v.wait_ge(s["ln_rstd"], T + 1)
                v.tensor_scalar(xn[:, :], row(t), mv[:, 0:1], rstd[:, 0:1], ALU.subtract, ALU.mult)\
                 .then_inc(s["ln_xn"], 1)

            def swiglu(t, h):
                cols = slice(512 * h, 512 * h + 512)
                v.wait_ge(s["d_th"], 2 * t.b + h + 1)
                v.scalar_tensor_tensor(u[:, cols], th[:, cols], 1.0, bank[2 * h + 1][:, :], ALU.add, ALU.mult).then_inc(s["d_u"], 1)
                v.wait_ge(s["d_u"], 2 * t.b + h + 1)
                if h == 0:
                    after(v, s["d_hround"], t.b)
                v.scalar_tensor_tensor(hid[:, cols], bank[2 * h][:, :], alpha[t.p][:, 2:3], u[:, cols], ALU.mult, ALU.mult)\
                 .then_inc(s["d_h"], 1)

            def hidden_scale(t):
                v.wait_ge(s["d_h"], 2 * t.b + 2)
                v.tensor_reduce(hm[:, 0:1], hid, AX.X, ALU.max, apply_absolute_value=True).then_inc(s["d_hmax"], 1)
                v.wait_ge(s["d_hmax"], t.b + 1)
                v.tensor_scalar(hm[:, 1:2], hm[:, 0:1], Q_EPS, None, ALU.max).then_inc(s["d_hscale"], 1)
                v.wait_ge(s["d_hscale"], 3 * t.b + 1)
                v.reciprocal(hm[:, 0:1], hm[:, 1:2]).then_inc(s["d_hscale"], 1)
                v.wait_ge(s["d_hscale"], 3 * t.b + 2)
                v.tensor_scalar(hm[:, 2:3], hm[:, 0:1], 127.0, None, ALU.mult).then_inc(s["d_hscale"], 1)
                v.tensor_scalar(hm[:, 3:4], hm[:, 1:2], wsc127[:, 1:2], tg[:, 3:4], ALU.mult, ALU.mult)\
                 .then_inc(s["d_beta"], 1)

            def output_d(t):
                v.wait_ge(s["d_beta"], t.b + 1)
                v.wait_ge(s["d_down_pe"], t.b + 1)
                v.scalar_tensor_tensor(row(t), bank[6][:, 0:D], hm[:, 3:4], row(t), ALU.mult, ALU.add).then_inc(s["d_out"], 1)

            v.wait_ge(s["c_x"], B)
            norm_d(t0)
            quantise(t0)
            norm_d(t1)
            quantise(t1)
            swiglu(t0, 0)
            swiglu(t0, 1)

            def batch_d(t, ahead):
                hidden_scale(t)
                if ahead >= 2:
                    norm_d(t.later(2))
                if ahead >= 1:
                    swiglu(t.later(1), 0)
                if ahead >= 2:
                    quantise(t.later(2))
                if ahead >= 1:
                    swiglu(t.later(1), 1)
                output_d(t)

            over_batches(v, batch_d)


def kernel(**inputs):
    import numpy as np
    from concourse import bacc
    from concourse.bass_utils import run_bass_kernel_spmd

    a = {n: np.asarray(v) for n, v in inputs.items()}
    kv = np.concatenate([a["L0_xattn_Wk"], a["L0_xattn_Wv"]], axis=0)
    arrays = {
        "x": a["x"],
        "ctx_t": a["ctx_2048"].transpose(0, 2, 1),
        "g_xattn": a["g_xattn"],
        "g_ffn": a["g_ffn"],
        "a_wq": a["L0_xattn_Wq"].T,
        "a_wkv": np.concatenate([kv[0::2], kv[1::2]], axis=0).T,
        "b_gate": a["L0_ffn_gate_w"].T,
        "b_w": a["L0_ffn_W"].T,
        "b_atoms": a["L0_ffn_atoms"],
        "b_eaw": a["L0_ffn_expert_atom_weights"],
        "b_imp": a["L0_ffn_importance"].reshape(E, NCH, P).transpose(2, 1, 0).reshape(P, NCH * E),
        "b_idx": a["L0_ffn_mask_idx"],
        "c_wq": a["L1_xattn_Wq"],
        "c_wkv": np.concatenate([a["L1_xattn_Wk_img"], a["L1_xattn_Wv_img"]], axis=1),
        "c_bqk": np.concatenate([a["L1_xattn_bq"], a["L1_xattn_bk_img"]]),
        "c_bv": a["L1_xattn_bv_img"],
        "c_gq": a["L1_xattn_gq"],
        "c_gk": a["L1_xattn_gk_img"],
        "c_wo": a["L1_xattn_Wo"],
        "c_bo": a["L1_xattn_bo"],
        "d_wgu": a["L1_ffn_w_gate_up"].T,
        "d_wd": a["L1_ffn_w_down"].T,
    }
    arrays = {n: np.ascontiguousarray(v) for n, v in arrays.items()}
    nc = bacc.Bacc("TRN2", target_bir_lowering=False, num_devices=1)
    args = [nc.dram_tensor(n, v.shape, mybir.dt.from_np(v.dtype), kind="ExternalInput").ap() for n, v in arrays.items()]
    args.append(nc.dram_tensor("out", (B, N, D), F32, kind="ExternalOutput").ap())
    build(nc, *args)
    r = run_bass_kernel_spmd(nc, [arrays], core_ids=[0])
    return r.results[0]["out"]
```

```python
from contextlib import ExitStack

import concourse.bass as bass
from concourse import mybir

F32 = mybir.dt.float32
F16 = mybir.dt.float16
BF16 = mybir.dt.bfloat16
I32 = mybir.dt.int32
U32 = mybir.dt.uint32
ALU = mybir.AluOpType
ACT = mybir.ActivationFunctionType
AX = mybir.AxisListType

P = 128
B, N, D = 8, 128, 256
KD = D // P
H0, DH0 = 32, 8
H1, DH1 = 16, 16
E, A, NS = 8, 64, 2048
NCH = NS // P
FF = 1024
LN_EPS, RMS_EPS, Q_EPS = 1e-5, 1e-6, 1e-5
ROUND = 1.5 * 2.0 ** 23
ROOT_UNIT = 9 / 64
ROOT, GATE = 10, 10

SEMAPHORES = """
passed c_pick const_ready ve_ready x_first x_rest ct_loaded0 ct_loaded1 wa_loaded wkv_loaded small_loaded idx_loaded
atoms_loaded wb_loaded wc_loaded cvec_loaded wgu_loaded wd_loaded tanh_done
ln_stats ln_mv ln_veps ln_rstd ln_xn ln_xt_pe ln_xt
a_qk_pe kv_pe a_sq a_raw a_ss a_rs a_qkn a_v a_hi a_lo a_stq_pe a_stk_pe a_qs a_ks
a_s_pe a_exp a_pv_pe a_ot a_otok_pe a_rd a_att a_x
t_eq t_eqm t_cnt t_int t_new t_soft t_softact t_smt_pe t_smt t_dt_pe t_sig t_sigact t_wt
t_piece t_sum_pe t_vals t_zero t_zeroed t_stage t_scattered t_loaded b_table
w_abs w_sum w_sum_pe w_scale w_sign w_mask w_tern
b_log_pe b_gate b_exp b_y_pe b_y
c_vec c_qkb c_vb c_qk_pe c_sq c_sse c_rs c_norm c_hi c_lo c_stq_pe c_stk_pe c_qs c_ks
c_s_pe c_max c_neg c_neg_t_pe c_neg_t c_shifted_pe c_exp c_pv_pe c_ot c_otok_pe c_rd c_on c_ont_pe c_ont c_wo_pe c_wo
c_x
d_amax d_scale d_round d_xq d_xqt_pe d_xqt d_up_pe d_th d_u d_h d_hmax d_hscale d_hround d_hq
d_hqt_pe d_hqt d_down_pe d_beta d_out stored
""".split()


class Tile:

    def __init__(self, pair, parity):
        self.pair, self.p = pair, parity
        self.b = pair * 2 + parity
        self.first = isinstance(pair, int) and self.b == 0

    def later(self, n):
        q = self.p + n
        return Tile(self.pair + q // 2, q % 2)


def over_batches(eng, body):
    body(Tile(0, 0), 2)
    body(Tile(0, 1), 2)
    with eng.Fori(1, B // 2 - 1) as i:
        for p in range(2):
            body(Tile(i, p), 2)
    body(Tile(B // 2 - 1, 0), 1)
    body(Tile(B // 2 - 1, 1), 0)


def after(eng, sem, value):
    if not isinstance(value, int) or value > 0:
        eng.wait_ge(sem, value)


def wait_alone(eng, sem, value, s):
    eng.wait_ge(sem, value)
    eng.sem_inc(s["passed"], 1)


def strided(view, dims):
    return bass.AP(tensor=view.tensor, offset=view.offset, ap=[list(view.ap[0])] + [list(d) for d in dims])


def spread(dram, n):
    return bass.AP(tensor=dram.tensor, offset=dram.offset, ap=[[0, P], [1, n]])


def build(nc, x, ctx_t, g_xattn, g_ffn, a_wq, a_wkv, b_gate, b_w, b_atoms, b_eaw, b_imp, b_idx,
          c_wq, c_wkv, c_bqk, c_bv, c_gq, c_gk, c_wo, c_bo, d_wgu, d_wd, out):
    stack = ExitStack()
    with stack:
        def sb(name, shape, dt=F32):
            return stack.enter_context(nc.sbuf_tensor(name, shape, dt))

        s = {n: stack.enter_context(nc.semaphore(n)) for n in SEMAPHORES}
        pair = [stack.enter_context(nc.psum_tensor(f"banks{2 * i}_{2 * i + 1}", [P, 1024], F32)) for i in range(4)]
        bank = [pair[i // 2][:, (i % 2) * 512:(i % 2 + 1) * 512] for i in range(8)]

        def banks(first):
            return pair[first // 2][:, :]

        X = sb("X", [P, B, D])
        id32 = sb("id32", [P, P])
        id16 = sb("id16", [P, P], F16)
        idbf = sb("idbf", [P, P], BF16)
        ones = sb("ones", [P, P])
        below = sb("below", [P, P], BF16)
        neghalf = sb("neghalf", [P, 2])
        eps = sb("eps", [P, 2])
        iota8 = sb("iota8", [P, 8])
        dump = sb("dump", [P, NCH])
        gains = sb("gains", [P, 4])
        tg = sb("tg", [P, 4])
        stats = sb("stats", [P, 6])
        mv = sb("mv", [P, 2])
        veps = sb("veps", [P, 1])
        rstd = sb("rstd", [P, 1])
        xn = sb("xn", [P, D])
        xt = [sb(f"xt{p}", [P, KD, P]) for p in range(2)]
        ct = [sb(f"ct{p}", [P, KD, P]) for p in range(2)]
        wqa = sb("wqa", [P, KD, D])
        wkva = sb("wkva", [P, KD, 2 * D])
        sq = sb("sq", [P, 2 * D])
        ss = sb("ss", [P, 2 * H0])
        rs = sb("rs", [P, 2 * H0])
        root = [sb(f"root{i}", [P, 2 * H0]) for i in range(2)]
        qkn = sb("qkn", [P, 2 * D])
        stq = sb("stq", [P, 4 * D], F16)
        stk = sb("stk", [P, 4 * D], F16)
        qs = [sb(f"qs{p}", [P, 8, P], F16) for p in range(2)]
        ks = [sb(f"ks{p}", [P, 8, P], F16) for p in range(2)]
        ve = [sb(f"ve{p}", [P, H0 * 32]) for p in range(2)]
        probs = [sb(f"probs{h}", [P, 16 * P]) for h in range(2)]
        ots = sb("ots", [P, 3 * P])
        rd = sb("rd", [P, H0])
        att = sb("att", [P, D])
        table = sb("table", [P, KD * D * E])
        idx_col = sb("idx_col", [P, NCH], I32)
        same = sb("same", [P, NS], BF16)
        same_below = sb("same_below", [P, NS], BF16)
        ci = sb("ci", [P, NCH], I32)
        ri = sb("ri", [P, NCH], I32)
        cf = sb("cf", [P, NCH])
        rf = sb("rf", [P, NCH])
        rowid = sb("rowid", [P, NCH])
        cnt = sb("cnt", [P, NCH])
        away = sb("away", [P, NCH])
        newid = sb("newid", [P, NCH], U32)
        atoms = sb("atoms", [A, NS])
        eaw = sb("eaw", [E, A])
        eaw_max = sb("eaw_max", [E, 1])
        eaw_exp = sb("eaw_exp", [E, A])
        eaw_sum = sb("eaw_sum", [E, 1])
        eaw_soft = sb("eaw_soft", [E, A])
        soft_t = sb("soft_t", [A, E])
        imp = sb("imp", [P, NCH * E])
        sig = sb("sig", [P, NCH * E])
        wt = sb("wt", [P, NCH * E])
        rest = sb("rest", [P, NCH * E])
        piece = [sb(f"piece{i}", [P, NCH * E], BF16) for i in range(3)]
        vals = sb("vals", [P, NCH * E])
        stage_idx = sb("stage_idx", [P, 1], U32)
        stage_val = sb("stage_val", [P, E])
        wb = sb("wb", [P, KD, D])
        gw = sb("gw", [P, KD, E])
        dw = sb("dw", [P, KD, E, D])
        qk_raw = dw[:, 1, 0:2, :].rearrange("p e r -> p (e r)")
        idx_row = dw[:, 0, :, :].rearrange("p e r -> p (e r)").bitcast(I32)
        l8 = sb("l8", [P, E])
        m8 = sb("m8", [P, 8])
        i8 = sb("i8", [P, 8], U32)
        i2 = sb("i2", [P, 2])
        gsm = sb("gsm", [P, 8])
        oh = sb("oh", [P, 2, E])
        gate = [sb(f"gate{p}", [P, E]) for p in range(2)]
        wqc = sb("wqc", [P, KD, D])
        wkvc = sb("wkvc", [P, KD, 2 * D])
        woc = sb("woc", [P, KD, D])
        bqk = sb("bqk", [P, 2 * D])
        bv = sb("bv", [P, D])
        bo = sb("bo", [P, D])
        gqk = sb("gqk", [P, 2, D])
        gscale = sb("gscale", [P, 3])
        ssc = sb("ssc", [P, 2])
        ssce = sb("ssce", [P, 2])
        rsc = sb("rsc", [P, 2])
        vce = [sb(f"vce{p}", [P, H1 * 32]) for p in range(2)]
        mx = sb("mx", [P, H1])
        mneg = sb("mneg", [P, 2 * H1], BF16)
        mneg_t = sb("mneg_t", [2 * H1, P], BF16)
        pick = same_below[0:2 * H1, :]
        otc = sb("otc", [P, 4 * P])
        rdc = sb("rdc", [P, H1])
        on = sb("on", [P, D])
        ont = sb("ont", [P, KD, P])
        wo_out = sb("wo_out", [P, D])
        wgu = sb("wgu", [P, KD * 2 * FF])
        wd = sb("wd", [P, 8 * D])
        wgu_q = sb("wgu_q", [P, KD * 2 * FF], BF16)
        wd_q = sb("wd_q", [P, 8 * D], BF16)
        neg = sb("neg", [P, 768], BF16)
        sgn = sb("sgn", [P, 768], BF16)
        junk = sb("junk", [P, 768])
        wabs = sb("wabs", [P, 2, B])
        wsum = sb("wsum", [P, 2])
        wscale = sb("wscale", [P, 2])
        wlim = sb("wlim", [P, 2, 2])
        wsc127 = sb("wsc127", [P, 2])
        am = sb("am", [P, 1])
        ac = sb("ac", [P, 1])
        xsc = sb("xsc", [P, 2])
        alpha = [sb(f"alpha{p}", [P, 4]) for p in range(2)]
        xr = sb("xr", [P, D])
        xq = sb("xq", [P, D], BF16)
        xqt = [sb(f"xqt{p}", [P, KD, P], BF16) for p in range(2)]
        th, u, hid, hr = (table[:, i * FF:(i + 1) * FF] for i in range(4))
        hm = sb("hm", [P, 4])
        hq = sb("hq", [P, FF], BF16)
        hqt = sb("hqt", [P, 8, P], BF16)

        scratch = nc.dram_tensor("delta_table", (D * D + P, E), F32, kind="Internal").ap()

        STA, XVA, OTA, QKA = bank[4:8]

        block = stack.enter_context(nc.Block())

        @block.sync
        def _(sp):
            sp.dma_start(X[:, 0:2, :], x[0:2].rearrange("b n d -> n b d")).then_inc(s["x_first"], 16)
            sp.dma_start(wqa[:, :, :], a_wq.rearrange("(k p) o -> p k o", p=P)).then_inc(s["wa_loaded"], 16)

            def load_ct(t, stage):
                after(sp, s["kv_pe"], stage * B + t.b - 1)
                sp.dma_start(ct[t.p][:, :, :], ctx_t[t.b].rearrange("(k p) m -> p k m", p=P))\
                  .then_inc(s[f"ct_loaded{t.p}"], 16)

            load_ct(Tile(0, 0), 0)
            sp.dma_start(wkva[:, :, :], a_wkv.rearrange("(k p) o -> p k o", p=P)).then_inc(s["wkv_loaded"], 16)
            load_ct(Tile(0, 1), 0)
            sp.dma_start(X[:, 2:B, :], x[2:B].rearrange("b n d -> n b d")).then_inc(s["x_rest"], 16)
            load_ct(Tile(1, 0), 0)
            sp.wait_ge(s["t_zero"], 1)
            sp.dma_start(scratch[0:D * D, :].rearrange("(p n) e -> p (n e)", p=P), table[:, :]).then_inc(s["t_zeroed"], 16)
            sp.dma_start(scratch[D * D:D * D + P, :], table[:, 0:E]).then_inc(s["t_zeroed"], 16)
            sp.dma_start(wgu[:, :].rearrange("p (k o) -> p k o", k=KD), d_wgu.rearrange("(k p) o -> p k o", p=P)).then_inc(s["wgu_loaded"], 16)
            load_ct(Tile(1, 1), 0)
            sp.dma_start(wd[:, :].rearrange("p (k o) -> p k o", k=8), d_wd.rearrange("(k p) o -> p k o", p=P)).then_inc(s["wd_loaded"], 16)
            sp.dma_start(wb[:, :, :], b_w.rearrange("(k p) o -> p k o", p=P)).then_inc(s["wb_loaded"], 16)
            sp.dma_start(gw[:, :, :], b_gate.rearrange("(k p) o -> p k o", p=P)).then_inc(s["wb_loaded"], 16)
            sp.dma_start(wqc[:, :, :], c_wq.rearrange("(k p) o -> p k o", p=P)).then_inc(s["wc_loaded"], 16)
            sp.dma_start(wkvc[:, :, :], c_wkv.rearrange("(k p) o -> p k o", p=P)).then_inc(s["wc_loaded"], 16)
            sp.dma_start(woc[:, :, :], c_wo.rearrange("(k p) o -> p k o", p=P)).then_inc(s["wc_loaded"], 16)
            sp.dma_start(bqk[:, :], spread(c_bqk, 2 * D)).then_inc(s["cvec_loaded"], 16)
            sp.dma_start(bv[:, :], spread(c_bv, D)).then_inc(s["cvec_loaded"], 16)
            sp.dma_start(bo[:, :], spread(c_bo, D)).then_inc(s["cvec_loaded"], 16)
            sp.dma_start(gqk[:, 0, :], spread(c_gq, D)).then_inc(s["cvec_loaded"], 16)
            sp.dma_start(gqk[:, 1, :], spread(c_gk, D)).then_inc(s["cvec_loaded"], 16)
            with sp.Fori(2, B // 2) as i:
                for p in range(2):
                    load_ct(Tile(i, p), 0)
            sp.wait_ge(s["t_scattered"], 16 * NCH)
            sp.dma_start(table[:, :].rearrange("p (k n) -> p k n", k=KD),
                         scratch[0:D * D, :].rearrange("(k p n) e -> p k (n e)", p=P, k=KD)).then_inc(s["t_loaded"], 16)
            with sp.Fori(0, B // 2) as i:
                for p in range(2):
                    load_ct(Tile(i, p), 1)
            with sp.Fori(0, B) as b:
                sp.wait_ge(s["d_out"], b + 1)
                sp.dma_start(out[b], X[:, b, :]).then_inc(s["stored"], 16)
            sp.wait_ge(s["stored"], 16 * B)

        @block.gpsimd
        def _(gp):
            gp.memset(id32[:, :], 0.0).then_inc(s["const_ready"], 1)
            gp.memset(ones[:, :], 1.0).then_inc(s["const_ready"], 1)
            gp.wait_ge(s["const_ready"], 2)
            gp.affine_select(out=id32[:, :], in_=id32[:, :], compare_op=ALU.not_equal, fill=1.0, base=0,
                             pattern=[[-1, P]], channel_multiplier=1).then_inc(s["const_ready"], 1)
            gp.memset(neghalf[:, :], -0.5)
            gp.memset(eps[:, 0:1], LN_EPS)
            gp.memset(eps[:, 1:2], D * RMS_EPS).then_inc(s["const_ready"], 1)
            gp.wait_ge(s["const_ready"], 4)
            gp.tensor_copy(id16[:, :], id32[:, :]).then_inc(s["const_ready"], 1)
            gp.tensor_copy(idbf[:, :], id32[:, :]).then_inc(s["const_ready"], 1)

            def ln_rstd(stage, t):
                T = stage * B + t.b
                gp.wait_ge(s["ln_mv"], T + 1)
                gp.tensor_tensor(veps[:, :], mv[:, 1:2], eps[:, 0:1], ALU.add).then_inc(s["ln_veps"], 1)
                gp.wait_ge(s["ln_veps"], T + 1)
                gp.tensor_tensor(rstd[:, :], veps[:, :], neghalf[:, 0:1], ALU.pow).then_inc(s["ln_rstd"], 1)

            def low_parts(t, hi, norm, done, width):
                reps = D // width
                q3 = qkn[:, 0:D].rearrange("p (h d) -> p h d", d=width).unsqueeze(2).broadcast_to([P, reps, 2, width])
                k3 = qkn[:, D:2 * D].rearrange("p (h d) -> p h d", d=width).unsqueeze(2).broadcast_to([P, reps, 2, width])
                q4 = stq[:, :].rearrange("p (h r d) -> p h r d", r=4, d=width)
                k4 = stk[:, :].rearrange("p (h r d) -> p h r d", r=4, d=width)
                gp.wait_ge(s[hi], 2 * t.b + 1)
                gp.tensor_tensor(q4[:, :, 2:4, :], q3, q4[:, :, 0:2, :], ALU.subtract).then_inc(s[done], 1)
                gp.wait_ge(s[hi], 2 * t.b + 2)
                gp.tensor_tensor(k4[:, :, 1:4:2, :], k3, k4[:, :, 0:3:2, :], ALU.subtract).then_inc(s[done], 1)

            def scatter(j):
                after(gp, s["t_scattered"], 16 * j)
                gp.tensor_copy(stage_idx[:, :], newid[:, bass.ds(j, 1)])
                gp.tensor_copy(stage_val[:, :], vals[:, bass.ds(j * E, E)]).then_inc(s["t_stage"], 1)
                wait_alone(gp, s["t_stage"], j + 1, s)
                gp.indirect_dma_start(out=scratch, out_offset=bass.IndirectOffsetOnAxis(ap=stage_idx[:, 0:1], axis=0),
                                      in_=stage_val[:, :], in_offset=None, compute_op=ALU.add)\
                  .then_inc(s["t_scattered"], 16)

            ln_rstd(0, Tile(0, 0))
            ln_rstd(0, Tile(0, 1))
            gp.iota(iota8[:, :], pattern=[[1, 8]], base=0, channel_multiplier=0, allow_small_or_imprecise_dtypes=True)
            gp.iota(dump[:, :], pattern=[[0, NCH]], base=D * D, channel_multiplier=1, allow_small_or_imprecise_dtypes=True)
            gp.memset(below[:, :], 0.0).then_inc(s["const_ready"], 1)
            gp.wait_ge(s["const_ready"], 7)
            gp.affine_select(out=below[:, :], in_=below[:, :], compare_op=ALU.is_gt, fill=1.0, base=1,
                             pattern=[[1, P]], channel_multiplier=-1).then_inc(s["const_ready"], 1)
            gp.memset(table[:, :], 0.0).then_inc(s["t_zero"], 1)
            low_parts(Tile(0, 0), "a_hi", "a_qkn", "a_lo", DH0)
            gp.memset(vce[0][:, :], 0.0)
            gp.memset(vce[1][:, :], 0.0).then_inc(s["const_ready"], 1)
            gp.wait_ge(s["const_ready"], 9)
            for p in range(2):
                gp.memset(strided(vce[p][:, 16:], [[32, H1], [1, 1]]), 1.0).then_inc(s["const_ready"], 1)

            def batch_a(t, ahead):
                chunk = 3 * t.b - 2
                if ahead >= 2:
                    ln_rstd(0, t.later(2))
                    if not t.first:
                        scatter(chunk)
                        scatter(chunk + 1)
                if ahead >= 1:
                    low_parts(t.later(1), "a_hi", "a_qkn", "a_lo", DH0)
                if t.first:
                    gp.wait_ge(s["t_new"], 9)
                    gp.wait_ge(s["t_vals"], 1)
                    gp.wait_ge(s["t_zeroed"], 32)
                    scatter(0)
                elif ahead >= 2:
                    scatter(chunk + 2)

            over_batches(gp, batch_a)

            ln_rstd(1, Tile(0, 0))
            ln_rstd(1, Tile(0, 1))
            gp.memset(pick, 0.0).then_inc(s["c_pick"], 1)
            for i in range(2):
                gp.wait_ge(s["c_pick"], i + 1)
                gp.affine_select(out=pick, in_=pick, compare_op=ALU.not_equal, fill=1.0, base=-H1 * i,
                                 pattern=[[-1, H1], [0, P]], channel_multiplier=1).then_inc(s["c_pick"], 1)

            def batch_b(t, ahead):
                if ahead >= 2:
                    ln_rstd(1, t.later(2))

            over_batches(gp, batch_b)

            def rms_c(t):
                gp.wait_ge(s["c_sq"], 2 * t.b + 2)
                gp.tensor_tensor(ssce[:, :], ssc[:, :], eps[:, 1:2].broadcast_to([P, 2]), ALU.add).then_inc(s["c_sse"], 1)
                gp.wait_ge(s["c_sse"], t.b + 1)
                gp.tensor_tensor(rsc[:, :], ssce[:, :], neghalf[:, 0:2], ALU.pow).then_inc(s["c_rs"], 1)

            ln_rstd(2, Tile(0, 0))
            ln_rstd(2, Tile(0, 1))
            rms_c(Tile(0, 0))
            low_parts(Tile(0, 0), "c_hi", "c_norm", "c_lo", DH1)
            rms_c(Tile(0, 1))
            low_parts(Tile(0, 1), "c_hi", "c_norm", "c_lo", DH1)

            def batch_c(t, ahead):
                if ahead >= 2:
                    ln_rstd(2, t.later(2))
                    rms_c(t.later(2))
                    low_parts(t.later(2), "c_hi", "c_norm", "c_lo", DH1)

            over_batches(gp, batch_c)

            ln_rstd(3, Tile(0, 0))
            ln_rstd(3, Tile(0, 1))

            def batch_d(t, ahead):
                if ahead >= 2:
                    ln_rstd(3, t.later(2))
                wait_alone(gp, s["d_hscale"], 3 * t.b + 3, s)
                gp.tensor_scalar(hr, hid, hm[:, 2:3], ROUND, ALU.mult, ALU.add).then_inc(s["d_hround"], 1)

            over_batches(gp, batch_d)

        @block.scalar
        def _(act):
            act.dma_start(eaw[:, :], b_eaw).then_inc(s["atoms_loaded"], 16)
            act.dma_start(atoms[:, :], b_atoms).then_inc(s["atoms_loaded"], 16)
            act.dma_start(imp[:, :], b_imp).then_inc(s["atoms_loaded"], 16)
            act.dma_start(idx_col[:, :], b_idx.rearrange("(c p) -> p c", p=P), allow_slow_non_contiguous=True).then_inc(s["idx_loaded"], 16)
            act.dma_start(idx_row, spread(b_idx, NS)).then_inc(s["idx_loaded"], 16)
            act.dma_start(gains[:, 0:2], spread(g_xattn, 2)).then_inc(s["small_loaded"], 16)
            act.dma_start(gains[:, 2:4], spread(g_ffn, 2)).then_inc(s["small_loaded"], 16)

            def copy_xt(stage, t, src):
                act.wait_ge(s["ln_xt_pe"], stage * B + t.b + 1)
                act.activation(xt[t.p][:, :, :].rearrange("p k n -> p (k n)"), src, ACT.Copy)\
                   .then_inc(s["ln_xt"], 1)

            def square_a(t):
                act.wait_ge(s["a_qk_pe"], t.b + 1)
                after(act, s["a_ss"], t.b)
                act.activation(sq[:, :], QKA[:, :], ACT.Square).then_inc(s["a_sq"], 1)
                after(act, s["a_qkn"], t.b)
                act.activation(qk_raw, QKA[:, :], ACT.Copy).then_inc(s["a_raw"], 1)

            def copy_v_a(t):
                act.wait_ge(s["kv_pe"], t.b + 1)
                after(act, s["a_pv_pe"], 2 * t.b - 2)
                for R, nr in ((0, 3), (1, 3), (2, 2)):
                    src = strided(XVA[:, 96 * R:], [[32, nr], [8, 4], [1, 8]])
                    dst = strided(ve[t.p][:, 384 * R:], [[137, nr], [32, 4], [1, 8]])
                    last = act.activation(dst, src, ACT.Copy)
                last.then_inc(s["a_v"], 1)

            def high_parts(t, ready, width, used, done):
                reps = D // width
                act.wait_ge(s[ready[0]], ready[1])
                after(act, s[used], t.b)
                for half, dst in ((0, stq[:, :].rearrange("p (h r d) -> p h r d", r=4, d=width)[:, :, 0:2, :]),
                                  (1, stk[:, :].rearrange("p (h r d) -> p h r d", r=4, d=width)[:, :, 0:3:2, :])):
                    src = qkn[:, half * D:(half + 1) * D].rearrange("p (h d) -> p h d", d=width)
                    act.activation(dst, src.unsqueeze(2).broadcast_to([P, reps, 2, width]), ACT.Copy)\
                       .then_inc(s[done], 1)

            def copy_qs(t, ready, src, done):
                act.wait_ge(s[ready], t.b + 1)
                act.activation(qs[t.p][:, :, :].rearrange("p w n -> p (w n)"), src, ACT.Copy).then_inc(s[done], 1)

            def exp_a(t, step):
                half, pair = step // 2, step % 2
                act.wait_ge(s["a_s_pe"], 4 * t.b + step + 1)
                act.activation(probs[half][:, pair * 1024:(pair + 1) * 1024], banks(2 * pair), ACT.Exp,
                               scale=float(DH0) ** 0.5 * ROOT_UNIT ** 2).then_inc(s["a_exp"], 1)

            def copy_ot(t):
                act.wait_ge(s["a_pv_pe"], 2 * t.b + 2)
                after(act, s["a_otok_pe"], t.b)
                act.activation(ots[:, :], OTA[:, 0:384], ACT.Copy).then_inc(s["a_ot"], 1)

            t0, t1 = Tile(0, 0), Tile(0, 1)
            copy_xt(0, t0, XVA[:, 0:256])
            act.wait_ge(s["t_soft"], 1)
            act.activation(eaw_exp[:, :], eaw[:, :], ACT.Exp, bias=eaw_max[:, 0:1], accum_out=eaw_sum[:, 0:1])\
               .then_inc(s["t_softact"], 1)
            act.activation(sig[:, :], imp[:, :], ACT.Exp, scale=-1.0).then_inc(s["t_sigact"], 1)
            square_a(t0)
            act.wait_ge(s["ve_ready"], 3)
            copy_v_a(t0)
            high_parts(t0, ("a_qkn", 1), DH0, "a_stk_pe", "a_hi")
            copy_xt(0, t1, XVA[:, 0:256])
            act.wait_ge(s["small_loaded"], 32)
            act.activation(tg[:, :], gains[:, :], ACT.Tanh).then_inc(s["tanh_done"], 1)
            copy_qs(t0, "a_stq_pe", STA[:, :].bitcast(F16), "a_qs")
            square_a(t1)
            copy_v_a(t1)

            def gate_exp(t):
                act.wait_ge(s["b_gate"], GATE * t.b + 3)
                act.activation(gsm[:, 1:2], gsm[:, 0:1], ACT.Exp).then_inc(s["b_exp"], 1)

            def batch_a(t, ahead):
                exp_a(t, 0)
                exp_a(t, 1)
                if ahead >= 2:
                    copy_xt(0, t.later(2), XVA[:, 0:256])
                if ahead == 0:
                    copy_xt(1, t0, XVA[:, 0:256])
                exp_a(t, 3)
                if ahead >= 1:
                    high_parts(t.later(1), ("a_qkn", t.later(1).b + 1), DH0, "a_stk_pe", "a_hi")
                exp_a(t, 2)
                if ahead >= 2:
                    square_a(t.later(2))
                if ahead >= 1:
                    copy_qs(t.later(1), "a_stq_pe", STA[:, :].bitcast(F16), "a_qs")
                if ahead >= 2:
                    copy_v_a(t.later(2))
                if t.first:
                    act.wait_ge(s["wgu_loaded"], 16)
                    act.wait_ge(s["wd_loaded"], 16)
                after(act, s["w_abs"], 2 * t.b)
                act.activation(junk[:, 0:512], wgu[:, bass.ds(t.b * 512, 512)], ACT.Abs, accum_out=wabs[:, 0, bass.ds(t.b, 1)])\
                   .then_inc(s["w_abs"], 1)
                act.activation(junk[:, 512:768], wd[:, bass.ds(t.b * 256, 256)], ACT.Abs, accum_out=wabs[:, 1, bass.ds(t.b, 1)])\
                   .then_inc(s["w_abs"], 1)
                if ahead == 0:
                    gate_exp(t0)
                copy_ot(t)

            over_batches(act, batch_a)

            def below_mask(t):
                act.wait_ge(s["w_tern"], 2 * t.b + 1)
                for i, (w, n) in enumerate(((wgu, 512), (wd, 256))):
                    at = slice(512 * i, 512 * i + n)
                    act.activation(sgn[:, at], w[:, bass.ds(t.b * n, n)], ACT.Sign, bias=wlim[:, i, 0:1]).then_inc(s["w_sign"], 1)
                    act.wait_ge(s["w_sign"], 2 * t.b + i + 1)
                    act.activation(neg[:, at], sgn[:, at], ACT.Relu, scale=-1.0).then_inc(s["w_mask"], 1)

            act.wait_ge(s["w_scale"], 5)
            below_mask(t0)

            def square_c(t):
                act.wait_ge(s["c_qkb"], t.b + 1)
                after(act, s["c_sq"], 2 * t.b)
                for i in range(2):
                    act.activation(junk[:, i * D:(i + 1) * D], sq[:, i * D:(i + 1) * D], ACT.Square,
                                   accum_out=ssc[:, i:i + 1]).then_inc(s["c_sq"], 1)

            def batch_b(t, ahead):
                if ahead >= 1:
                    copy_xt(1, t.later(1), bank[6][:, 0:256])
                    below_mask(t.later(1))
                    gate_exp(t.later(1))
                else:
                    copy_xt(2, t0, bank[7][:, 0:256])
                    square_c(t0)
                    high_parts(t0, ("c_norm", 2), DH1, "c_stk_pe", "c_hi")

            over_batches(act, batch_b)

            def exp_c(t, step):
                act.wait_ge(s["c_shifted_pe"], 2 * t.b + step + 1)
                after(act, s["c_pv_pe"], 2 * t.b - 2)
                act.activation(probs[t.p][:, step * 1024:(step + 1) * 1024], banks(2), ACT.Exp, scale=gscale[:, 2:3])\
                   .then_inc(s["c_exp"], 1)

            def copy_ont(t):
                act.wait_ge(s["c_ont_pe"], t.b + 1)
                act.activation(ont[:, :, :].rearrange("p k n -> p (k n)"), bank[7][:, 0:256], ACT.Copy)\
                   .then_inc(s["c_ont"], 1)

            def copy_otc(t):
                act.wait_ge(s["c_pv_pe"], 2 * t.b + 2)
                after(act, s["c_otok_pe"], t.b)
                act.activation(otc[:, :], bank[6][:, :], ACT.Copy).then_inc(s["c_ot"], 1)

            copy_xt(2, t1, bank[7][:, 0:256])
            square_c(t1)
            copy_qs(t0, "c_stq_pe", bank[4][:, :].bitcast(F16), "c_qs")
            high_parts(t1, ("c_norm", 4), DH1, "c_stk_pe", "c_hi")

            def copy_xqt(t):
                act.wait_ge(s["d_xqt_pe"], t.b + 1)
                act.activation(xqt[t.p][:, :, :].rearrange("p k n -> p (k n)"), bank[4][:, :].bitcast(BF16)[:, 0:256],
                               ACT.Copy).then_inc(s["d_xqt"], 1)

            def batch_c(t, ahead):
                if not t.first:
                    copy_otc(t.later(-1))
                exp_c(t, 0)
                if ahead >= 1:
                    copy_qs(t.later(1), "c_stq_pe", bank[4][:, :].bitcast(F16), "c_qs")
                if ahead >= 2:
                    copy_xt(2, t.later(2), bank[7][:, 0:256])
                exp_c(t, 1)
                if ahead >= 2:
                    square_c(t.later(2))
                if ahead == 0:
                    copy_xqt(t0)
                if not t.first:
                    copy_ont(t.later(-1))
                if ahead >= 2:
                    high_parts(t.later(2), ("c_norm", 2 * t.later(2).b + 2), DH1, "c_stk_pe", "c_hi")

            over_batches(act, batch_c)

            def tanh_d(t, h):
                act.wait_ge(s["d_up_pe"], 2 * t.b + h + 1)
                if h == 0:
                    after(act, s["d_u"], 2 * t.b)
                act.activation(th[:, h * 512:(h + 1) * 512], bank[2 * h][:, :], ACT.Tanh, scale=alpha[t.p][:, 1:2])\
                   .then_inc(s["d_th"], 1)

            def ints_d(t):
                act.wait_ge(s["d_hround"], t.b + 1)
                after(act, s["d_hqt_pe"], t.b)
                act.activation(hq[:, :], hr, ACT.Copy, bias=-ROUND).then_inc(s["d_hq"], 1)

            def copy_hqt(t):
                act.wait_ge(s["d_hqt_pe"], t.b + 1)
                after(act, s["d_down_pe"], t.b)
                act.activation(hqt[:, :, :].rearrange("p k n -> p (k n)"), bank[5][:, :].bitcast(BF16), ACT.Copy)\
                   .then_inc(s["d_hqt"], 1)

            copy_otc(Tile(3, 1))
            tanh_d(t0, 0)
            tanh_d(t0, 1)
            copy_xqt(t1)

            def batch_d(t, ahead):
                if ahead >= 1:
                    tanh_d(t.later(1), 0)
                if t.first:
                    copy_ont(Tile(3, 1))
                ints_d(t)
                if ahead >= 1:
                    tanh_d(t.later(1), 1)
                copy_hqt(t)
                if ahead >= 2:
                    copy_xqt(t.later(2))

            over_batches(act, batch_d)

        @block.tensor
        def _(pe):
            mm, tr = nc.tensor.matmul, nc.tensor.transpose
            t0, t1 = Tile(0, 0), Tile(0, 1)

            def turn_xn(stage, t, dst):
                pe.wait_ge(s["ln_xn"], stage * B + t.b + 1)
                for k in range(KD):
                    last = tr(dst[:, k * P:(k + 1) * P], xn[:, k * P:(k + 1) * P], id32[:, :])
                last.then_inc(s["ln_xt_pe"], 1)

            def project(dst, lhs, rhs):
                for k in range(KD):
                    last = mm(dst, lhs[:, k, :], rhs(k), start=(k == 0), stop=(k == KD - 1))
                return last

            def xn_a(t):
                after(pe, s["a_v"], t.b)
                turn_xn(0, t, XVA)

            def qkv_a(t):
                pe.wait_ge(s["ln_xt"], t.b + 1)
                after(pe, s["a_raw"], t.b)
                project(QKA[:, 0:D], xt[t.p], lambda k: wqa[:, k, :])
                pe.wait_ge(s[f"ct_loaded{t.p}"], t.pair * 16 + 16)
                project(QKA[:, D:2 * D], ct[t.p], lambda k: wkva[:, k, 0:D]).then_inc(s["a_qk_pe"], 1)
                project(XVA[:, 0:D], ct[t.p], lambda k: wkva[:, k, D:2 * D]).then_inc(s["kv_pe"], 1)

            def turn_stack(src, dst, name):
                for w in range(8):
                    last = tr(dst[:, :].bitcast(F16)[:, w * P:(w + 1) * P], src[:, w * P:(w + 1) * P], id16[:, :])
                last.then_inc(s[name], 1)

            def stack_q_a(t):
                pe.wait_ge(s["a_lo"], 2 * t.b + 1)
                after(pe, s["a_ks"], t.b)
                turn_stack(stq, STA, "a_stq_pe")

            def stack_k_a(t):
                pe.wait_ge(s["a_lo"], 2 * t.b + 2)
                pe.wait_ge(s["a_qs"], t.b + 1)
                turn_stack(stk, STA, "a_stk_pe")

            def scores_a(t, step):
                half, pair = step // 2, step % 2
                if step == 0:
                    pe.wait_ge(s["a_qs"], t.b + 1)
                    pe.wait_ge(s["a_ks"], t.b + 1)
                after(pe, s["a_exp"], 4 * t.b + step - 1)
                for g in range(4):
                    for j in range(2):
                        h4 = 2 * pair + j
                        rows = slice(32 * h4, 32 * h4 + 32)
                        last = mm(bank[h4][:, g * P:(g + 1) * P], ks[t.p][rows, 4 * half + g, :],
                                  qs[t.p][rows, 4 * half + g, :], start=True, stop=True)
                last.then_inc(s["a_s_pe"], 1)

            def pv_a(t, half, groups):
                if groups[0] == 0:
                    pe.wait_ge(s["a_exp"], 4 * t.b + 2 * half + 2)
                    if half == 0:
                        if t.first:
                            pe.wait_ge(s["t_wt"], 1)
                        after(pe, s["a_att"], t.b)
                for g in groups:
                    v = 4 * half + g
                    for h4 in range(4):
                        h = 4 * v + h4
                        last = mm(OTA[32 * h4:32 * h4 + 32, (v // 3) * P:(v // 3 + 1) * P], ve[t.p][:, 32 * h:32 * h + 32],
                                  probs[half][:, (4 * h4 + g) * P:(4 * h4 + g + 1) * P],
                                  start=(v % 3 == 0), stop=(v % 3 == 2 or v == 7))
                if groups[-1] == 3:
                    last.then_inc(s["a_pv_pe"], 1)

            def turn_out_a(t):
                pe.wait_ge(s["a_ot"], t.b + 1)
                for R in range(3):
                    last = tr(OTA[:, R * P:(R + 1) * P], ots[:, R * P:(R + 1) * P], id32[:, :])
                last.then_inc(s["a_otok_pe"], 1)

            pe.wait_ge(s["const_ready"], 3)
            xn_a(t0)
            pe.wait_ge(s["wa_loaded"], 16)
            pe.wait_ge(s["wkv_loaded"], 16)
            qkv_a(t0)
            pe.wait_ge(s["t_soft"], 3)
            tr(OTA[0:A, 256:256 + E], eaw_soft[:, :], id32[0:E, 0:E]).then_inc(s["t_smt_pe"], 1)
            pe.wait_ge(s["t_smt"], 1)
            pe.wait_ge(s["atoms_loaded"], 48)
            for c in range(NCH):
                last = mm(OTA[:, c * E:(c + 1) * E], atoms[:, c * P:(c + 1) * P], soft_t[:, :], start=True, stop=True)
            last.then_inc(s["t_dt_pe"], 1)
            xn_a(t1)
            pe.wait_ge(s["const_ready"], 6)
            stack_q_a(t0)
            stack_k_a(t0)
            qkv_a(t1)
            scores_a(t0, 0)
            scores_a(t0, 1)

            def total_positions():
                pe.wait_ge(s["t_piece"], 5)
                pe.wait_ge(s["a_ks"], 2)
                for c in range(NCH):
                    for i in range(3):
                        last = mm(STA[:, c * E:(c + 1) * E], same[:, c * P:(c + 1) * P], piece[i][:, c * E:(c + 1) * E],
                                  start=(i == 0), stop=(i == 2))
                last.then_inc(s["t_sum_pe"], 1)

            def logits(t):
                pe.wait_ge(s["ln_xt"], B + t.b + 1)
                if t.first:
                    pe.wait_ge(s["a_raw"], B)
                    pe.wait_ge(s["wb_loaded"], 32)
                after(pe, s["b_gate"], GATE * t.b)
                project(bank[7][:, 0:E], xt[t.p], lambda k: gw[:, k, :]).then_inc(s["b_log_pe"], 1)

            def batch_a(t, ahead):
                scores_a(t, 2)
                scores_a(t, 3)
                if ahead >= 2:
                    xn_a(t.later(2))
                if ahead == 0:
                    turn_xn(1, t0, XVA)
                pv_a(t, 0, range(4))
                if ahead >= 2:
                    qkv_a(t.later(2))
                if ahead >= 1:
                    stack_q_a(t.later(1))
                pv_a(t, 1, range(4))
                if isinstance(t.b, int) and t.b == 1:
                    pe.wait_ge(s["t_vals"], 1)
                if ahead >= 1:
                    stack_k_a(t.later(1))
                    scores_a(t.later(1), 0)
                    scores_a(t.later(1), 1)
                else:
                    logits(t0)
                if t.first:
                    total_positions()
                turn_out_a(t)

            over_batches(pe, batch_a)

            def xn_b(t):
                if isinstance(t.b, int) and t.b == 1:
                    pe.wait_ge(s["a_att"], B)
                pe.wait_ge(s["ln_xt"], B + t.b)
                turn_xn(1, t, bank[6])

            def experts(t, unit):
                pe.wait_ge(s["b_y"], 8 * t.b + 2 * unit + 2)
                for k in range(KD):
                    last = mm(bank[unit][:, :], xt[t.p][:, k, :],
                              dw[:, k, 2 * unit:2 * unit + 2, :].rearrange("p e r -> p (e r)"), start=(k == 0), stop=(k == KD - 1))
                last.then_inc(s["b_y_pe"], 1)

            pe.wait_ge(s["w_sum"], 2)
            mm(bank[5][:, 0:2], ones[:, :], wsum[:, :], start=True, stop=True).then_inc(s["w_sum_pe"], 1)
            pe.wait_ge(s["b_table"], 2 * KD)

            def k_c(t):
                after(pe, s["c_wo"], t.b - 3)
                after(pe, s["c_qkb"], t.b)
                pe.wait_ge(s[f"ct_loaded{t.p}"], 16 * (B // 2) + t.pair * 16 + 16)
                project(bank[7][:, D:2 * D], ct[t.p], lambda k: wkvc[:, k, 0:D])

            def xn_c(t):
                turn_xn(2, t, bank[7])

            def v_c(t):
                pe.wait_ge(s[f"ct_loaded{t.p}"], 16 * (B // 2) + t.pair * 16 + 16)
                after(pe, s["c_ot"], t.b - 1)
                project(bank[6][:, 0:D], ct[t.p], lambda k: wkvc[:, k, D:2 * D]).then_inc(s["kv_pe"], 1)

            def q_c(t):
                pe.wait_ge(s["ln_xt"], 2 * B + t.b + 1)
                project(bank[7][:, 0:D], xt[t.p], lambda k: wqc[:, k, :]).then_inc(s["c_qk_pe"], 1)

            def batch_b(t, ahead):
                experts(t, 0)
                if ahead == 0:
                    pe.wait_ge(s["b_gate"], GATE * B)
                    pe.wait_ge(s["wc_loaded"], 48)
                    k_c(t0)
                    xn_c(t0)
                experts(t, 1)
                if ahead >= 1:
                    xn_b(t.later(1))
                else:
                    pe.wait_ge(s["ln_xt"], 2 * B)
                    v_c(t0)
                experts(t, 2)
                if ahead >= 1:
                    logits(t.later(1))
                else:
                    q_c(t0)
                experts(t, 3)

            over_batches(pe, batch_b)

            def stack_q_c(t):
                pe.wait_ge(s["c_lo"], 2 * t.b + 1)
                after(pe, s["c_max"], 2 * t.b)
                turn_stack(stq, bank[4], "c_stq_pe")

            def stack_k_c(t):
                pe.wait_ge(s["c_lo"], 2 * t.b + 2)
                after(pe, s["c_max"], 2 * t.b)
                turn_stack(stk, bank[5], "c_stk_pe")

            def scores_c(t, step):
                if step == 0:
                    pe.wait_ge(s["c_qs"], t.b + 1)
                    pe.wait_ge(s["c_ks"], t.b + 1)
                    after(pe, s["c_neg_t"], t.b)
                for w4 in range(4):
                    for j in range(2):
                        rows = slice(64 * j, 64 * j + 64)
                        w = 4 * step + w4
                        last = mm(bank[4 * step + j][:, w4 * P:(w4 + 1) * P], qs[t.p][rows, w, :], ks[t.p][rows, w, :],
                                  start=True, stop=True)
                last.then_inc(s["c_s_pe"], 1)

            def turn_maxima(t):
                pe.wait_ge(s["c_neg"], 2 * t.b + 2)
                tr(bank[0][:, :].bitcast(BF16)[0:2 * H1, 0:P], mneg[:, :], idbf[:, :]).then_inc(s["c_neg_t_pe"], 1)

            def shifted_c(t, step):
                pe.wait_ge(s["c_neg_t"], t.b + 1)
                after(pe, s["c_exp"], 2 * t.b + step)
                for w4 in range(4):
                    for j in range(2):
                        rows = slice(64 * j, 64 * j + 64)
                        w = 4 * step + w4
                        h = 2 * w + j
                        dst = bank[2 + j][:, w4 * P:(w4 + 1) * P]
                        mm(dst, ks[t.p][rows, w, :], qs[t.p][rows, w, :], start=True, stop=False)
                        last = mm(dst, pick[:, h * P:(h + 1) * P], mneg_t[:, :], start=False, stop=True)
                last.then_inc(s["c_shifted_pe"], 1)

            def pv_c(t, step):
                pe.wait_ge(s["c_exp"], 2 * t.b + step + 1)
                if step == 0:
                    pe.wait_ge(s["c_vb"], min(t.b + 2, B) if isinstance(t.b, int) else t.b + 2)
                    after(pe, s["c_ot"], t.b)
                for w4 in range(4):
                    for j in range(2):
                        i = 2 * w4 + j
                        h = 8 * step + i
                        last = mm(bank[6][32 * (i % 4):32 * (i % 4) + 32, (2 * step + i // 4) * P:(2 * step + i // 4 + 1) * P],
                                  vce[t.p][:, 32 * h:32 * h + 32],
                                  probs[t.p][:, step * 1024 + j * 512 + w4 * P:step * 1024 + j * 512 + (w4 + 1) * P],
                                  start=True, stop=True)
                last.then_inc(s["c_pv_pe"], 1)

            def turn_out_c(t):
                pe.wait_ge(s["c_ot"], t.b + 1)
                after(pe, s["c_wo"], t.b)
                pe.wait_ge(s["c_qkb"], min(t.b + 4, B) if isinstance(t.b, int) else t.b + 4)
                for k in range(4):
                    last = tr(bank[7][:, k * P:(k + 1) * P], otc[:, k * P:(k + 1) * P], id32[:, :])
                last.then_inc(s["c_otok_pe"], 1)

            def turn_on(t):
                pe.wait_ge(s["c_on"], t.b + 1)
                for k in range(KD):
                    last = tr(bank[7][:, k * P:(k + 1) * P], on[:, k * P:(k + 1) * P], id32[:, :])
                last.then_inc(s["c_ont_pe"], 1)

            def out_c(t):
                pe.wait_ge(s["c_ont"], t.b + 1)
                project(bank[7][:, 0:D], ont, lambda k: woc[:, k, :]).then_inc(s["c_wo_pe"], 1)

            k_c(t1)
            xn_c(t1)
            q_c(t1)
            stack_q_c(t0)
            pe.wait_ge(s["w_scale"], 3)
            stack_k_c(t0)
            pe.wait_ge(s["b_y"], 8 * B + 8)
            scores_c(t0, 0)
            scores_c(t0, 1)
            turn_maxima(t0)
            pe.wait_ge(s["c_pick"], 3)

            def turn_xq(t):
                pe.wait_ge(s["d_xq"], t.b + 1)
                after(pe, s["d_xqt"], t.b)
                for k in range(KD):
                    last = tr(bank[4][:, :].bitcast(BF16)[:, k * P:(k + 1) * P], xq[:, k * P:(k + 1) * P], idbf[:, :])
                last.then_inc(s["d_xqt_pe"], 1)

            def up(t):
                pe.wait_ge(s["d_xqt"], t.b + 1)
                for h in range(2):
                    after(pe, s["d_h"], 2 * t.b + h - 1)
                    for part in range(2):
                        for k in range(KD):
                            at = k * 2 * FF + part * FF + h * 512
                            last = mm(bank[2 * h + part][:, :], xqt[t.p][:, k, :], wgu_q[:, at:at + 512],
                                      start=(k == 0), stop=(k == KD - 1))
                    last.then_inc(s["d_up_pe"], 1)

            def batch_c(t, ahead):
                prev, nxt = t.later(-1), t.later(1)
                shifted_c(t, 0)
                if ahead >= 1:
                    stack_q_c(nxt)
                if ahead >= 2:
                    k_c(t.later(2))
                shifted_c(t, 1)
                if ahead >= 1:
                    stack_k_c(nxt)
                if ahead >= 2:
                    xn_c(t.later(2))
                if ahead >= 1:
                    v_c(nxt)
                if ahead >= 2:
                    q_c(t.later(2))
                if ahead >= 1:
                    scores_c(nxt, 0)
                    scores_c(nxt, 1)
                if not t.first:
                    turn_out_c(prev)
                pv_c(t, 0)
                pv_c(t, 1)
                if ahead == 0:
                    pe.wait_ge(s["c_max"], 2 * B)
                    turn_xq(t0)
                if not t.first:
                    turn_on(prev)
                if ahead == 0:
                    pe.wait_ge(s["w_tern"], 2 * B + 1)
                    up(t0)
                if not t.first:
                    out_c(prev)
                if ahead >= 1:
                    turn_maxima(nxt)

            over_batches(pe, batch_c)

            def turn_hq(t):
                pe.wait_ge(s["d_hq"], t.b + 1)
                after(pe, s["d_hqt"], t.b)
                for k in range(8):
                    last = tr(bank[5][:, :].bitcast(BF16)[:, k * P:(k + 1) * P], hq[:, k * P:(k + 1) * P], idbf[:, :])
                last.then_inc(s["d_hqt_pe"], 1)

            def down(t):
                pe.wait_ge(s["d_hqt"], t.b + 1)
                after(pe, s["d_out"], t.b)
                for k in range(8):
                    last = mm(bank[6][:, 0:D], hqt[:, k, :], wd_q[:, k * D:(k + 1) * D], start=(k == 0), stop=(k == 7))
                last.then_inc(s["d_down_pe"], 1)

            t7 = Tile(3, 1)
            turn_xq(t1)
            turn_out_c(t7)

            def batch_d(t, ahead):
                if ahead >= 1:
                    up(t.later(1))
                if t.first:
                    turn_on(t7)
                    out_c(t7)
                turn_hq(t)
                if ahead >= 2:
                    turn_xq(t.later(2))
                down(t)

            over_batches(pe, batch_d)

        @block.vector
        def _(v):
            t0, t1 = Tile(0, 0), Tile(0, 1)

            def row(t):
                return X[:, bass.ds(t.b, 1), :].rearrange("p a d -> p (a d)")

            def measure(stage, t):
                T = stage * B + t.b
                v.bn_stats(stats[:, :], row(t)).then_inc(s["ln_stats"], 1)
                wait_alone(v, s["ln_stats"], T + 1, s)
                v.bn_aggr(mv[:, :], stats[:, :]).then_inc(s["ln_mv"], 1)

            def normalise(stage, t):
                T = stage * B + t.b
                v.wait_ge(s["ln_rstd"], T + 1)
                if stage < 3:
                    after(v, s["ln_xt_pe"], T)
                v.tensor_scalar(xn[:, :], row(t), mv[:, 0:1], rstd[:, 0:1], ALU.subtract, ALU.mult)\
                 .then_inc(s["ln_xn"], 1)

            def layer_norm(stage, t):
                measure(stage, t)
                normalise(stage, t)

            def by_head(view, h, d):
                return view.rearrange("p (h d) -> p h d", d=d)

            def sums_a(t):
                v.wait_ge(s["a_sq"], t.b + 1)
                v.tensor_reduce(ss[:, :], by_head(sq[:, :], 2 * H0, DH0), AX.X, ALU.add).then_inc(s["a_ss"], 1)

            def root_a(t):
                R = ROOT * t.b
                a, h, other = root[0][:, :], rs[:, :], root[1][:, :]
                y = ss[:, :]
                v.wait_ge(s["a_ss"], t.b + 1)
                v.tensor_scalar(a, ss[:, :], float(DH0) * RMS_EPS, None, ALU.add).then_inc(s["a_rs"], 1)
                v.wait_ge(s["a_rs"], R + 1)
                v.tensor_scalar(y.bitcast(I32), a.bitcast(I32), -0.5, float(0x5F3759DF), ALU.mult, ALU.add).then_inc(s["a_rs"], 1)
                for i in range(2):
                    v.wait_ge(s["a_rs"], R + 4 * i + 2)
                    v.scalar_tensor_tensor(h, y, ROOT_UNIT if i else 1.0, y, ALU.mult, ALU.mult).then_inc(s["a_rs"], 1)
                    v.wait_ge(s["a_rs"], R + 4 * i + 3)
                    v.tensor_tensor(other, h, a, ALU.mult).then_inc(s["a_rs"], 1)
                    v.wait_ge(s["a_rs"], R + 4 * i + 4)
                    v.scalar_tensor_tensor(h, other, -10.0 / 3.0, other, ALU.add, ALU.mult).then_inc(s["a_rs"], 1)
                    v.wait_ge(s["a_rs"], R + 4 * i + 5)
                    v.scalar_tensor_tensor(h if i else other, h, 5.0, y, ALU.add, ALU.mult).then_inc(s["a_rs"], 1)
                    y, other = other, y

            def norm_a(t):
                v.wait_ge(s["a_rs"], ROOT * t.b + ROOT)
                v.wait_ge(s["a_raw"], t.b + 1)
                after(v, s["a_lo"], 2 * t.b)
                v.tensor_tensor(by_head(qkn[:, :], 2 * H0, DH0), by_head(qk_raw, 2 * H0, DH0),
                                rs[:, :].unsqueeze(2).broadcast_to([P, 2 * H0, DH0]), ALU.mult).then_inc(s["a_qkn"], 1)

            def copy_ks(t, ready, src, done):
                v.wait_ge(s[ready], t.b + 1)
                v.tensor_copy(ks[t.p][:, :, :].rearrange("p w n -> p (w n)"), src).then_inc(s[done], 1)

            def output_a(t):
                v.wait_ge(s["a_otok_pe"], t.b + 1)
                v.reciprocal(strided(rd[:, 0:], [[12, 2], [1, 4], [4, 3]]),
                             strided(OTA[:, 8:], [[128, 2], [32, 4], [9, 3]]))
                v.reciprocal(strided(rd[:, 24:], [[1, 4], [4, 2]]),
                             strided(OTA[:, 264:], [[32, 4], [9, 2]])).then_inc(s["a_rd"], 1)
                v.wait_ge(s["a_rd"], t.b + 1)
                for R, nr in ((0, 3), (1, 3), (2, 2)):
                    last = v.tensor_tensor(strided(att[:, 96 * R:], [[32, nr], [8, 4], [1, 8]]),
                                           strided(OTA[:, 128 * R:], [[9, nr], [32, 4], [1, 8]]),
                                           strided(rd[:, 12 * R:], [[4, nr], [1, 4], [0, 8]]), ALU.mult)
                last.then_inc(s["a_att"], 1)
                v.wait_ge(s["a_att"], t.b + 1)
                v.scalar_tensor_tensor(row(t), att[:, :], tg[:, 0:1], row(t), ALU.mult, ALU.add).then_inc(s["a_x"], 1)

            v.memset(ve[0][:, :], 0.0).then_inc(s["ve_ready"], 1)
            v.memset(ve[1][:, :], 0.0).then_inc(s["ve_ready"], 1)
            v.wait_ge(s["ve_ready"], 2)
            for p in range(2):
                for R, nr in ((0, 3), (1, 3), (2, 2)):
                    last = v.memset(strided(ve[p][:, 384 * R + 8:], [[137, nr], [32, 4]]), 1.0)
            last.then_inc(s["ve_ready"], 1)

            def softmax_of_atoms():
                v.wait_ge(s["atoms_loaded"], 48)
                v.tensor_reduce(eaw_max[:, :], eaw[:, :], AX.X, ALU.max, negate=True).then_inc(s["t_soft"], 1)
                v.wait_ge(s["t_softact"], 1)
                v.reciprocal(eaw_max[:, :], eaw_sum[:, :]).then_inc(s["t_soft"], 1)
                v.wait_ge(s["t_soft"], 2)
                v.tensor_scalar(eaw_soft[:, :], eaw_exp[:, :], eaw_max[:, 0:1], None, ALU.mult).then_inc(s["t_soft"], 1)

            def copy_softmax():
                v.wait_ge(s["t_smt_pe"], 1)
                v.tensor_copy(soft_t[:, :], OTA[0:A, 256:256 + E]).then_inc(s["t_smt"], 1)

            def sigmoid():
                v.wait_ge(s["t_sigact"], 1)
                v.tensor_scalar(rest[:, :], sig[:, :], 1.0, None, ALU.add).then_inc(s["t_sig"], 1)
                v.wait_ge(s["t_sig"], 1)
                v.reciprocal(imp[:, :], rest[:, :]).then_inc(s["t_sig"], 1)

            def compare_positions():
                v.wait_ge(s["idx_loaded"], 32)
                v.tensor_tensor(same[:, :].rearrange("p (c n) -> p c n", c=NCH), idx_row.rearrange("p (c n) -> p c n", c=NCH),
                                idx_col[:, :].unsqueeze(2).broadcast_to([P, NCH, P]), ALU.is_equal).then_inc(s["t_eq"], 1)
                v.tensor_scalar(ci[:, :], idx_col[:, :], D - 1, None, ALU.bitwise_and).then_inc(s["t_int"], 1)
                v.tensor_scalar(ri[:, :], idx_col[:, :], 8, None, ALU.logical_shift_right).then_inc(s["t_int"], 1)
                v.wait_ge(s["t_int"], 2)
                v.tensor_copy(cf[:, :], ci[:, :]).then_inc(s["t_new"], 1)
                v.tensor_copy(rf[:, :], ri[:, :]).then_inc(s["t_new"], 1)
                v.wait_ge(s["t_new"], 2)
                v.scalar_tensor_tensor(rowid[:, :], cf[:, :], float(D), rf[:, :], ALU.mult, ALU.add).then_inc(s["t_new"], 1)

            def weighted_values():
                v.wait_ge(s["t_sig"], 2)
                v.wait_ge(s["t_dt_pe"], 1)
                v.tensor_tensor(wt[:, :], OTA[:, 0:NCH * E], imp[:, :], ALU.mult).then_inc(s["t_wt"], 1)
                v.wait_ge(s["t_wt"], 1)
                v.tensor_copy(piece[0][:, :], wt[:, :]).then_inc(s["t_piece"], 1)
                v.wait_ge(s["t_piece"], 1)
                v.tensor_tensor(rest[:, :], wt[:, :], piece[0][:, :], ALU.subtract).then_inc(s["t_piece"], 1)
                v.wait_ge(s["t_piece"], 2)
                v.tensor_copy(piece[1][:, :], rest[:, :]).then_inc(s["t_piece"], 1)
                v.wait_ge(s["t_piece"], 3)
                v.tensor_tensor(wt[:, :], rest[:, :], piece[1][:, :], ALU.subtract).then_inc(s["t_piece"], 1)
                v.wait_ge(s["t_piece"], 4)
                v.tensor_copy(piece[2][:, :], wt[:, :]).then_inc(s["t_piece"], 1)

            def number_rows():
                v.wait_ge(s["const_ready"], 8)
                v.wait_ge(s["t_eq"], 1)
                v.tensor_tensor(same_below[:, :].rearrange("p (c n) -> p c n", c=NCH), same[:, :].rearrange("p (c n) -> p c n", c=NCH),
                                below[:, :].unsqueeze(1).broadcast_to([P, NCH, P]), ALU.mult).then_inc(s["t_eqm"], 1)
                v.wait_ge(s["t_eqm"], 1)
                v.tensor_reduce(cnt[:, :], same_below[:, :].rearrange("p (c n) -> p c n", c=NCH), AX.X, ALU.add).then_inc(s["t_cnt"], 1)
                v.wait_ge(s["t_new"], 3)
                v.wait_ge(s["t_cnt"], 1)
                v.tensor_tensor(away[:, :], dump[:, :], rowid[:, :], ALU.subtract).then_inc(s["t_new"], 1)
                v.tensor_scalar(cf[:, :], cnt[:, :], 0.5, None, ALU.is_gt).then_inc(s["t_new"], 1)
                v.wait_ge(s["t_new"], 5)
                v.tensor_tensor(rf[:, :], away[:, :], cf[:, :], ALU.mult).then_inc(s["t_new"], 1)
                v.wait_ge(s["t_new"], 6)
                v.tensor_tensor(cf[:, :], rf[:, :], rowid[:, :], ALU.add).then_inc(s["t_new"], 1)
                v.wait_ge(s["t_new"], 7)
                v.tensor_copy(newid[:, :], cf[:, :]).then_inc(s["t_new"], 2)

            def merge_table(k, half):
                if (k, half) == (0, 0):
                    v.wait_ge(s["t_loaded"], 16)
                    v.wait_ge(s["wb_loaded"], 32)
                by_e = table[:, k * D * E:(k + 1) * D * E].rearrange("p (r e) -> p e r", e=E)
                of = slice(half * E // 2, (half + 1) * E // 2)
                v.tensor_tensor(dw[:, k, of, :], by_e[:, of, :], wb[:, k, :].unsqueeze(1).broadcast_to([P, E // 2, D]),
                                ALU.add).then_inc(s["b_table"], 1)

            def choose(t):
                G = GATE * t.b
                v.wait_ge(s["b_log_pe"], t.b + 1)
                v.tensor_scalar(l8[:, :], bank[7][:, 0:E], 50.0, -50.0, ALU.min, ALU.max).then_inc(s["b_gate"], 1)
                wait_alone(v, s["b_gate"], G + 1, s)
                v.max(m8[:, :], l8[:, :]).then_inc(s["b_gate"], 1)
                wait_alone(v, s["b_gate"], G + 2, s)
                v.tensor_tensor(gsm[:, 0:1], m8[:, 1:2], m8[:, 0:1], ALU.subtract).then_inc(s["b_gate"], 1)
                v.max_index(i8[:, :], m8[:, :], l8[:, :]).then_inc(s["b_gate"], 1)

            def gates(t):
                G = GATE * t.b
                v.wait_ge(s["b_exp"], t.b + 1)
                v.tensor_scalar(gsm[:, 2:3], gsm[:, 1:2], 1.0, None, ALU.add).then_inc(s["b_gate"], 1)
                v.wait_ge(s["b_gate"], G + 4)
                v.tensor_copy(i2[:, :], i8[:, 0:2]).then_inc(s["b_gate"], 1)
                v.wait_ge(s["b_gate"], G + 5)
                v.reciprocal(gsm[:, 3:4], gsm[:, 2:3]).then_inc(s["b_gate"], 1)
                v.wait_ge(s["b_gate"], G + 6)
                v.tensor_scalar(oh[:, 1, :], iota8[:, :], i2[:, 1:2], gsm[:, 1:2], ALU.is_equal, ALU.mult).then_inc(s["b_gate"], 1)
                v.wait_ge(s["b_gate"], G + 8)
                v.scalar_tensor_tensor(oh[:, 0, :], iota8[:, :], i2[:, 0:1], oh[:, 1, :], ALU.is_equal, ALU.add).then_inc(s["b_gate"], 1)
                v.wait_ge(s["b_gate"], G + 9)
                v.tensor_scalar(gate[t.p][:, :], oh[:, 0, :], gsm[:, 3:4], tg[:, 2:3], ALU.mult, ALU.mult).then_inc(s["b_gate"], 1)

            v.sem_inc(s["b_y"], 8)
            v.wait_ge(s["x_first"], 16)
            layer_norm(0, t0)
            layer_norm(0, t1)
            softmax_of_atoms()
            sums_a(t0)
            copy_softmax()
            root_a(t0)
            norm_a(t0)
            sigmoid()
            compare_positions()
            copy_ks(t0, "a_stk_pe", STA[:, :].bitcast(F16), "a_ks")
            weighted_values()
            sums_a(t1)
            v.wait_ge(s["x_rest"], 16)
            v.wait_ge(s["tanh_done"], 1)

            def batch_a(t, ahead):
                if ahead >= 2:
                    measure(0, t.later(2))
                if not t.first:
                    output_a(t.later(-1))
                if ahead >= 2:
                    normalise(0, t.later(2))
                if ahead >= 1:
                    root_a(t.later(1))
                    norm_a(t.later(1))
                if t.first:
                    number_rows()
                if ahead >= 1:
                    copy_ks(t.later(1), "a_stk_pe", STA[:, :].bitcast(F16), "a_ks")
                if t.first:
                    v.wait_ge(s["t_sum_pe"], 1)
                    v.tensor_copy(vals[:, :], STA[:, 0:NCH * E]).then_inc(s["t_vals"], 1)
                if ahead == 1:
                    merge_table(0, 0)
                if ahead >= 2:
                    sums_a(t.later(2))
                if ahead == 1:
                    merge_table(0, 1)
                if ahead == 0:
                    v.wait_ge(s["a_x"], B - 1)
                    layer_norm(1, t0)
                    merge_table(1, 0)
                    choose(t0)
                    measure(1, t1)
                    gates(t0)
                    merge_table(1, 1)
                    v.wait_ge(s["w_abs"], 2 * B)
                    v.tensor_reduce(wsum[:, :], wabs[:, :, :], AX.X, ALU.add).then_inc(s["w_sum"], 2)

            over_batches(v, batch_a)
            output_a(Tile(3, 1))

            def ternary(t):
                for i, (w, wq, n) in enumerate(((wgu, wgu_q, 512), (wd, wd_q, 256))):
                    v.wait_ge(s["w_mask"], 2 * t.b + i + 1)
                    v.scalar_tensor_tensor(wq[:, bass.ds(t.b * n, n)], w[:, bass.ds(t.b * n, n)], wlim[:, i, 0:1],
                                           neg[:, 512 * i:512 * i + n], ALU.is_gt, ALU.subtract).then_inc(s["w_tern"], 1)

            def combine(t, unit):
                v.wait_ge(s["b_y_pe"], 4 * t.b + unit + 1)
                if unit == 0:
                    v.wait_ge(s["b_gate"], GATE * t.b + GATE)
                for j in range(2):
                    e = 2 * unit + j
                    v.wait_ge(s["b_y"], 8 * t.b + e + 8)
                    v.scalar_tensor_tensor(row(t), bank[unit][:, j * D:(j + 1) * D], gate[t.p][:, e:e + 1], row(t),
                                           ALU.mult, ALU.add).then_inc(s["b_y"], 1)

            v.wait_ge(s["a_x"], B)
            v.wait_ge(s["w_sum_pe"], 1)
            for i, n in enumerate((2 * FF * D, FF * D)):
                v.tensor_scalar(wscale[:, i:i + 1], bank[5][:, i:i + 1], 1.0 / n, Q_EPS, ALU.mult, ALU.max)\
                 .then_inc(s["w_scale"], 1)
            v.wait_ge(s["w_scale"], 2)
            v.tensor_scalar(wlim[:, :, 0], wscale[:, :], 0.5, None, ALU.mult)
            v.tensor_scalar(wlim[:, :, 1], wscale[:, :], -0.5, None, ALU.mult)
            v.tensor_scalar(wsc127[:, :], wscale[:, :], 1.0 / 127.0, None, ALU.mult).then_inc(s["w_scale"], 3)
            v.wait_ge(s["w_scale"], 5)
            v.sem_inc(s["w_tern"], 1)
            v.wait_ge(s["cvec_loaded"], 80)
            v.tensor_tensor(gqk[:, 0, :], gqk[:, 0, :], gqk[:, 1, :], ALU.mult).then_inc(s["c_vec"], 1)
            v.wait_ge(s["c_vec"], 1)
            v.tensor_reduce(gscale[:, 0:1], gqk[:, 0, :], AX.X, ALU.max, apply_absolute_value=True).then_inc(s["c_vec"], 1)
            v.wait_ge(s["c_vec"], 2)
            v.tensor_scalar(gscale[:, 0:1], gscale[:, 0:1], 1e-30, None, ALU.max).then_inc(s["c_vec"], 1)
            v.wait_ge(s["c_vec"], 3)
            v.reciprocal(gscale[:, 1:2], gscale[:, 0:1]).then_inc(s["c_vec"], 1)
            v.tensor_scalar(gscale[:, 2:3], gscale[:, 0:1], float(DH1) ** -0.5, None, ALU.mult)
            v.wait_ge(s["c_vec"], 4)
            v.tensor_scalar(gqk[:, 1, :], gqk[:, 0, :], gscale[:, 1:2], float(D) ** 0.5, ALU.mult, ALU.mult).then_inc(s["c_vec"], 1)
            v.wait_ge(s["c_vec"], 5)

            def bias_v(t):
                v.wait_ge(s["kv_pe"], B + t.b + 1)
                v.tensor_tensor(strided(vce[t.p][:, 0:], [[32, H1], [1, DH1]]), by_head(bank[6][:, 0:D], H1, DH1),
                                by_head(bv[:, :], H1, DH1), ALU.add).then_inc(s["c_vb"], 1)

            def bias_qk(t):
                v.wait_ge(s["c_qk_pe"], t.b + 1)
                v.tensor_tensor(sq[:, :], bank[7][:, :], bqk[:, :], ALU.add).then_inc(s["c_qkb"], 1)

            def norm_c(t):
                v.wait_ge(s["c_rs"], t.b + 1)
                after(v, s["c_lo"], 2 * t.b)
                v.scalar_tensor_tensor(qkn[:, 0:D], sq[:, 0:D], rsc[:, 0:1], gqk[:, 1, :], ALU.mult, ALU.mult)\
                 .then_inc(s["c_norm"], 1)
                v.tensor_scalar(qkn[:, D:2 * D], sq[:, D:2 * D], rsc[:, 1:2], float(D) ** 0.5, ALU.mult, ALU.mult).then_inc(s["c_norm"], 1)

            def batch_b(t, ahead):
                if ahead >= 1:
                    normalise(1, t.later(1))
                else:
                    layer_norm(2, t0)
                combine(t, 0)
                combine(t, 1)
                ternary(t)
                combine(t, 2)
                if ahead >= 2:
                    measure(1, t.later(2))
                if ahead >= 1:
                    choose(t.later(1))
                else:
                    v.wait_ge(s["const_ready"], 9)
                    bias_v(t0)
                    measure(2, t1)
                    bias_qk(t0)
                    normalise(2, t1)
                combine(t, 3)
                if ahead >= 1:
                    gates(t.later(1))
                else:
                    norm_c(t0)

            over_batches(v, batch_b)

            def maxima(t, step):
                cols = slice(8 * step, 8 * step + 8)
                v.wait_ge(s["c_s_pe"], 2 * t.b + step + 1)
                if step == 0:
                    after(v, s["c_neg"], 2 * t.b)
                v.tensor_reduce(mx[:, cols].rearrange("p (w j) -> p j w", j=2),
                                banks(4 * step).rearrange("p (j w m) -> p j w m", j=2, m=P), AX.X, ALU.max)\
                 .then_inc(s["c_max"], 1)

            def negate_maxima(t):
                v.wait_ge(s["c_max"], 2 * t.b + 2)
                after(v, s["c_neg_t_pe"], t.b)
                v.tensor_scalar(mneg[:, 0:H1], mx[:, :], -1.0, None, ALU.mult).then_inc(s["c_neg"], 1)
                v.wait_ge(s["c_neg"], 2 * t.b + 1)
                v.scalar_tensor_tensor(mneg[:, H1:2 * H1], mx[:, :], -1.0, mneg[:, 0:H1], ALU.mult, ALU.subtract)\
                 .then_inc(s["c_neg"], 1)

            def copy_maxima(t):
                v.wait_ge(s["c_neg_t_pe"], t.b + 1)
                v.tensor_copy(mneg_t[:, :], bank[0][:, :].bitcast(BF16)[0:2 * H1, 0:P]).then_inc(s["c_neg_t"], 1)

            def output_c(t):
                v.wait_ge(s["c_otok_pe"], t.b + 1)
                after(v, s["c_on"], t.b)
                v.reciprocal(rdc[:, :].unsqueeze(2), strided(bank[7][:, DH1:], [[32, H1], [1, 1]])).then_inc(s["c_rd"], 1)
                v.wait_ge(s["c_rd"], t.b + 1)
                v.tensor_tensor(by_head(on[:, :], H1, DH1), strided(bank[7][:, 0:], [[32, H1], [1, DH1]]),
                                rdc[:, :].unsqueeze(2).broadcast_to([P, H1, DH1]), ALU.mult).then_inc(s["c_on"], 1)

            def residual_c(t):
                v.wait_ge(s["c_wo_pe"], t.b + 1)
                v.tensor_tensor(wo_out[:, :], bank[7][:, 0:D], bo[:, :], ALU.add).then_inc(s["c_wo"], 1)
                v.wait_ge(s["c_wo"], t.b + 1)
                v.scalar_tensor_tensor(row(t), wo_out[:, :], tg[:, 1:2], row(t), ALU.mult, ALU.add).then_inc(s["c_x"], 1)

            def largest_x(t):
                v.wait_ge(s["ln_xn"], 3 * B + t.b + 1)
                v.tensor_reduce(am[:, :], xn[:, :], AX.X, ALU.max, apply_absolute_value=True).then_inc(s["d_amax"], 1)

            def scale_x(t):
                v.wait_ge(s["d_amax"], t.b + 1)
                v.tensor_scalar(ac[:, :], am[:, :], Q_EPS, None, ALU.max).then_inc(s["d_scale"], 1)
                v.wait_ge(s["d_scale"], 4 * t.b + 1)
                v.reciprocal(xsc[:, 0:1], ac[:, :]).then_inc(s["d_scale"], 1)
                v.tensor_scalar(alpha[t.p][:, 0:1], ac[:, :], wsc127[:, 0:1], None, ALU.mult).then_inc(s["d_scale"], 1)
                v.wait_ge(s["d_scale"], 4 * t.b + 3)
                v.tensor_scalar(xsc[:, 1:2], xsc[:, 0:1], 127.0, None, ALU.mult)
                v.tensor_scalar(alpha[t.p][:, 1:2], alpha[t.p][:, 0:1], 0.5, None, ALU.mult)
                v.tensor_scalar(alpha[t.p][:, 2:3], alpha[t.p][:, 0:1], alpha[t.p][:, 0:1], 0.5, ALU.mult, ALU.mult)\
                 .then_inc(s["d_scale"], 1)

            def round_x(t):
                v.wait_ge(s["d_scale"], 4 * t.b + 4)
                v.tensor_scalar(xr[:, :], xn[:, :], xsc[:, 1:2], ROUND, ALU.mult, ALU.add).then_inc(s["d_round"], 1)

            def ints_x(t):
                v.wait_ge(s["d_round"], t.b + 1)
                after(v, s["d_xqt_pe"], t.b)
                v.tensor_scalar(xq[:, :], xr[:, :], -ROUND, None, ALU.add).then_inc(s["d_xq"], 1)

            def quantise(t):
                largest_x(t)
                scale_x(t)
                round_x(t)
                ints_x(t)

            def copy_ks_c(t):
                copy_ks(t, "c_stk_pe", bank[5][:, :].bitcast(F16), "c_ks")

            v.wait_ge(s["b_y"], 8 + 8 * B)
            bias_qk(t1)
            copy_ks_c(t0)
            norm_c(t1)
            maxima(t0, 0)
            maxima(t0, 1)
            negate_maxima(t0)
            copy_maxima(t0)

            def batch_c(t, ahead):
                prev, nxt = t.later(-1), t.later(1)
                if ahead >= 2:
                    measure(2, t.later(2))
                if not isinstance(t.b, int) or t.b >= 2:
                    residual_c(t.later(-2))
                if ahead >= 2:
                    normalise(2, t.later(2))
                if ahead >= 1:
                    copy_ks_c(nxt)
                if ahead == 0:
                    v.wait_ge(s["c_x"], B - 2)
                    v.wait_ge(s["ln_xt_pe"], 3 * B)
                    layer_norm(3, t0)
                    quantise(t0)
                if ahead >= 1:
                    bias_v(nxt)
                if ahead == 0:
                    layer_norm(3, t1)
                if ahead >= 2:
                    bias_qk(t.later(2))
                if ahead >= 1:
                    maxima(nxt, 0)
                if not t.first:
                    output_c(prev)
                if ahead >= 1:
                    maxima(nxt, 1)
                if ahead >= 2:
                    norm_c(t.later(2))
                if ahead >= 1:
                    negate_maxima(nxt)
                    copy_maxima(nxt)

            over_batches(v, batch_c)
            t7 = Tile(3, 1)
            quantise(t1)

            def silu(t, h):
                cols = slice(512 * h, 512 * h + 512)
                v.wait_ge(s["d_th"], 2 * t.b + h + 1)
                v.scalar_tensor_tensor(u[:, cols], th[:, cols], 1.0, bank[2 * h + 1][:, :], ALU.add, ALU.mult).then_inc(s["d_u"], 1)

            def times_up(t, h):
                cols = slice(512 * h, 512 * h + 512)
                v.wait_ge(s["d_u"], 2 * t.b + h + 1)
                if h == 0:
                    after(v, s["d_hround"], t.b)
                v.scalar_tensor_tensor(hid[:, cols], bank[2 * h][:, :], alpha[t.p][:, 2:3], u[:, cols], ALU.mult, ALU.mult)\
                 .then_inc(s["d_h"], 1)

            def swiglu(t, h):
                silu(t, h)
                times_up(t, h)

            def largest_hidden(t):
                v.wait_ge(s["d_h"], 2 * t.b + 2)
                v.tensor_reduce(hm[:, 0:1], hid, AX.X, ALU.max, apply_absolute_value=True).then_inc(s["d_hmax"], 1)

            def scale_hidden(t):
                v.wait_ge(s["d_hmax"], t.b + 1)
                v.tensor_scalar(hm[:, 1:2], hm[:, 0:1], Q_EPS, None, ALU.max).then_inc(s["d_hscale"], 1)
                v.wait_ge(s["d_hscale"], 3 * t.b + 1)
                v.reciprocal(hm[:, 0:1], hm[:, 1:2]).then_inc(s["d_hscale"], 1)
                v.wait_ge(s["d_hscale"], 3 * t.b + 2)
                v.tensor_scalar(hm[:, 2:3], hm[:, 0:1], 127.0, None, ALU.mult).then_inc(s["d_hscale"], 1)
                v.tensor_scalar(alpha[t.p][:, 3:4], hm[:, 1:2], wsc127[:, 1:2], tg[:, 3:4], ALU.mult, ALU.mult)\
                 .then_inc(s["d_beta"], 1)

            def output_d(t):
                v.wait_ge(s["d_beta"], t.b + 1)
                v.wait_ge(s["d_down_pe"], t.b + 1)
                v.scalar_tensor_tensor(row(t), bank[6][:, 0:D], alpha[t.p][:, 3:4], row(t), ALU.mult, ALU.add).then_inc(s["d_out"], 1)

            swiglu(t0, 0)
            residual_c(t7.later(-1))
            swiglu(t0, 1)
            output_c(t7)

            def batch_d(t, ahead):
                if ahead >= 2:
                    measure(3, t.later(2))
                largest_hidden(t)
                scale_hidden(t)
                if t.first:
                    residual_c(t7)
                else:
                    output_d(t.later(-1))
                if ahead >= 2:
                    normalise(3, t.later(2))
                if ahead >= 1:
                    silu(t.later(1), 0)
                if ahead >= 2:
                    largest_x(t.later(2))
                if ahead >= 1:
                    times_up(t.later(1), 0)
                if ahead >= 2:
                    scale_x(t.later(2))
                    round_x(t.later(2))
                    ints_x(t.later(2))
                if ahead >= 1:
                    silu(t.later(1), 1)
                    times_up(t.later(1), 1)
                if t.first:
                    v.wait_ge(s["c_x"], B)

            over_batches(v, batch_d)
            output_d(Tile(3, 1))


def kernel(**inputs):
    import numpy as np
    from concourse import bacc
    from concourse.bass_utils import run_bass_kernel_spmd

    a = {n: np.asarray(v) for n, v in inputs.items()}
    kv = np.concatenate([a["L0_xattn_Wk"], a["L0_xattn_Wv"]], axis=0)
    arrays = {
        "x": a["x"],
        "ctx_t": a["ctx_2048"].transpose(0, 2, 1),
        "g_xattn": a["g_xattn"],
        "g_ffn": a["g_ffn"],
        "a_wq": a["L0_xattn_Wq"].T,
        "a_wkv": np.concatenate([kv[0::2], kv[1::2]], axis=0).T,
        "b_gate": a["L0_ffn_gate_w"].T,
        "b_w": a["L0_ffn_W"].T,
        "b_atoms": a["L0_ffn_atoms"],
        "b_eaw": a["L0_ffn_expert_atom_weights"],
        "b_imp": a["L0_ffn_importance"].reshape(E, NCH, P).transpose(2, 1, 0).reshape(P, NCH * E),
        "b_idx": a["L0_ffn_mask_idx"],
        "c_wq": a["L1_xattn_Wq"],
        "c_wkv": np.concatenate([a["L1_xattn_Wk_img"], a["L1_xattn_Wv_img"]], axis=1),
        "c_bqk": np.concatenate([a["L1_xattn_bq"], a["L1_xattn_bk_img"]]),
        "c_bv": a["L1_xattn_bv_img"],
        "c_gq": a["L1_xattn_gq"],
        "c_gk": a["L1_xattn_gk_img"],
        "c_wo": a["L1_xattn_Wo"],
        "c_bo": a["L1_xattn_bo"],
        "d_wgu": a["L1_ffn_w_gate_up"].T,
        "d_wd": a["L1_ffn_w_down"].T,
    }
    arrays = {n: np.ascontiguousarray(v) for n, v in arrays.items()}
    nc = bacc.Bacc("TRN2", target_bir_lowering=False, num_devices=1)
    args = [nc.dram_tensor(n, v.shape, mybir.dt.from_np(v.dtype), kind="ExternalInput").ap() for n, v in arrays.items()]
    args.append(nc.dram_tensor("out", (B, N, D), F32, kind="ExternalOutput").ap())
    build(nc, *args)
    r = run_bass_kernel_spmd(nc, [arrays], core_ids=[0])
    return r.results[0]["out"]
```
